# Optimizing a Trainium2 kernel written in Bass

```python
import numpy as np
import jax
import jax.numpy as jnp

def _softmax(x, axis=-1):
    return jax.nn.softmax(x, axis=axis)

def _gelu(x):
    return jax.nn.gelu(x, approximate=True)

def _silu(x):
    return jax.nn.silu(x)

def _sigmoid(x):
    return jax.nn.sigmoid(x)

def _layernorm(x, axis=-1, eps=1e-05):
    m = jnp.mean(x, axis=axis, keepdims=True)
    v = jnp.var(x, axis=axis, keepdims=True)
    return (x - m) / jnp.sqrt(v + eps)

def _scatter_add(tgt, idx, src, axis=0):
    return tgt.at[idx].add(src)

def _segment_sum(src, seg, n):
    return jax.ops.segment_sum(src, seg, n)
kernel_name = 'mk_flamingo_gated_d1_seqx_r4_aa39e7'

def setup_inputs(seed: int=0):
    np.random.seed(seed)
    _w = jnp.asarray

    def _rec_inputs():
        import jax
        import jax.numpy as jnp
        _rk = jax.random.key(seed)
        x = 6.313e-05 + 0.9998 * jax.random.normal(jax.random.fold_in(_rk, 1), (4, 512, 256), jnp.float32)
        _lenS = 512 - jax.random.randint(jax.random.fold_in(_rk, 7), (4,), 0, max(1, 512 // 4) + 1, jnp.int32)
        _lenS2 = 512 - jax.random.randint(jax.random.fold_in(_rk, 8), (4,), 0, max(1, 512 // 4) + 1, jnp.int32)
        _ctx_1024P = jax.random.normal(jax.random.fold_in(_rk, 11), (4, 16, 256), jnp.float32)
        _ctx_1024c = jax.random.dirichlet(jax.random.fold_in(_rk, 511), 0.3 * jnp.ones((16,), jnp.float32), (4, 512))
        _ctx_1024t = jnp.einsum('bsk,bkd->bsd', _ctx_1024c, _ctx_1024P)
        _ctx_1024t = _ctx_1024t * jax.lax.rsqrt(jnp.mean(jnp.square(_ctx_1024t)) + 1e-12) * 0.953939
        ctx_1024 = -0.000214406 + 1.00034 * (_ctx_1024t + 0.3 * jax.random.normal(jax.random.fold_in(_rk, 611), (4, 512, 256), jnp.float32))
        _g = jax.random.normal(jax.random.fold_in(_rk, 9001), (2, 1), jnp.float32)
        _g = jnp.sign(_g) * jnp.maximum(jnp.abs(_g), 1.0) + (_g == 0) * 1.0
        g_xattn = _g[0]
        g_ffn = _g[1]
        return (x, ctx_1024, g_xattn, g_ffn)
    x, ctx_1024, g_xattn, g_ffn = _rec_inputs()

    def _L0_xattn_setup():
        import jax, jax.numpy as jnp
        import numpy as np
        from jax import lax
        BIG = jnp.float32(1e+30)

        def _pairwise_euclidean(a, b):
            aa = jnp.sum(a * a, axis=-1)[:, None]
            bb = jnp.sum(b * b, axis=-1)[None, :]
            ab = a @ b.T
            return jnp.sqrt(jnp.maximum(aa + bb - 2.0 * ab, 0.0))

        def _dtw_cost(D):
            row0 = jnp.cumsum(D[0])

            def row_step(prev_row, d_row):
                first = d_row[0] + prev_row[0]

                def col_step(left, inp):
                    d_ij, up, diag = inp
                    r = d_ij + jnp.minimum(jnp.minimum(up, left), diag)
                    return (r, r)
                _, rest = lax.scan(col_step, first, (d_row[1:], prev_row[1:], prev_row[:-1]))
                row = jnp.concatenate([first[None], rest])
                return (row, row)
            _, rows = lax.scan(row_step, row0, D[1:])
            return jnp.concatenate([row0[None], rows], axis=0)

        def _backtrack(R, T1, T2):
            L = T1 + T2 - 1

            def step(carry, _):
                i, j, done = carry
                valid = jnp.logical_not(done)
                cd = jnp.where((i > 0) & (j > 0), R[jnp.maximum(i - 1, 0), jnp.maximum(j - 1, 0)], BIG)
                cu = jnp.where(i > 0, R[jnp.maximum(i - 1, 0), j], BIG)
                cl = jnp.where(j > 0, R[i, jnp.maximum(j - 1, 0)], BIG)
                choice = jnp.argmin(jnp.stack([cd, cu, cl]))
                ni = jnp.where(choice <= 1, i - 1, i)
                nj = jnp.where((choice == 0) | (choice == 2), j - 1, j)
                at_origin = (i == 0) & (j == 0)
                ni = jnp.where(at_origin, 0, ni)
                nj = jnp.where(at_origin, 0, nj)
                return ((ni, nj, done | at_origin), (i, j, valid))
            init = (jnp.int32(T1 - 1), jnp.int32(T2 - 1), jnp.bool_(False))
            _, (i_idx, j_idx, valid) = lax.scan(step, init, None, length=L)
            return (i_idx, j_idx, valid)

        def _align_one(small, large):
            T_small, d = small.shape
            T_large = large.shape[0]
            D = _pairwise_euclidean(small, large)
            R = _dtw_cost(D)
            i_idx, j_idx, valid = _backtrack(R, T_small, T_large)
            contrib = small[i_idx] * valid[:, None].astype(small.dtype)
            expanded = jnp.zeros((T_large, d), dtype=small.dtype).at[j_idx].add(contrib)
            return expanded
        key = jax.random.key(seed)
        k1, k2 = jax.random.split(key)
        teacher = jax.random.normal(k1, (16, 100, 256), dtype=jnp.float32)
        student = jax.random.normal(k2, (16, 150, 256), dtype=jnp.float32)
        return {'teacher_features': teacher, 'student_features': student}
    _L0_xattn_all = _L0_xattn_setup()
    _L0_xattn_in = {k: v for k, v in _L0_xattn_all.items() if k in ()}
    del _L0_xattn_all

    def _L0_ffn_setup():
        import jax, jax.numpy as jnp
        import numpy as np
        B, S, H = (4, 512, 256)
        E, K = (8, 2)
        I_R, I_S = (4 * H, 8 * H)
        CAP_FACTOR = 1.25
        SCALE = 1.0
        key = jax.random.key(seed)
        ks = jax.random.split(key, 9)
        std = 0.02
        return {'x': jax.random.normal(ks[0], (B, S, H), jnp.float32), 'router_w': std * jax.random.normal(ks[1], (E, H), jnp.float32), 'rg': std * jax.random.normal(ks[2], (E, H, I_R), jnp.float32), 'ru': std * jax.random.normal(ks[3], (E, H, I_R), jnp.float32), 'rd': std * jax.random.normal(ks[4], (E, I_R, H), jnp.float32), 'sg': std * jax.random.normal(ks[5], (H, I_S), jnp.float32), 'su': std * jax.random.normal(ks[6], (H, I_S), jnp.float32), 'sd': std * jax.random.normal(ks[7], (I_S, H), jnp.float32)}
    _L0_ffn_all = _L0_ffn_setup()
    _L0_ffn_in = {k: v for k, v in _L0_ffn_all.items() if k in ('router_w', 'rg', 'ru', 'rd', 'sg', 'su', 'sd')}
    del _L0_ffn_all
    return {'x': x, 'ctx_1024': ctx_1024, 'g_xattn': g_xattn, 'g_ffn': g_ffn, 'L0_ffn_router_w': _L0_ffn_in['router_w'], 'L0_ffn_rg': _L0_ffn_in['rg'], 'L0_ffn_ru': _L0_ffn_in['ru'], 'L0_ffn_rd': _L0_ffn_in['rd'], 'L0_ffn_sg': _L0_ffn_in['sg'], 'L0_ffn_su': _L0_ffn_in['su'], 'L0_ffn_sd': _L0_ffn_in['sd']}

def reference(x, ctx_1024, g_xattn, g_ffn, L0_ffn_router_w, L0_ffn_rg, L0_ffn_ru, L0_ffn_rd, L0_ffn_sg, L0_ffn_su, L0_ffn_sd):
    import jax
    import jax.numpy as jnp

    def _L0_xattn_ref(teacher_features, student_features):
        import jax, jax.numpy as jnp
        import numpy as np
        from jax import lax
        BIG = jnp.float32(1e+30)

        def _pairwise_euclidean(a, b):
            aa = jnp.sum(a * a, axis=-1)[:, None]
            bb = jnp.sum(b * b, axis=-1)[None, :]
            ab = a @ b.T
            return jnp.sqrt(jnp.maximum(aa + bb - 2.0 * ab, 0.0))

        def _dtw_cost(D):
            row0 = jnp.cumsum(D[0])

            def row_step(prev_row, d_row):
                first = d_row[0] + prev_row[0]

                def col_step(left, inp):
                    d_ij, up, diag = inp
                    r = d_ij + jnp.minimum(jnp.minimum(up, left), diag)
                    return (r, r)
                _, rest = lax.scan(col_step, first, (d_row[1:], prev_row[1:], prev_row[:-1]))
                row = jnp.concatenate([first[None], rest])
                return (row, row)
            _, rows = lax.scan(row_step, row0, D[1:])
            return jnp.concatenate([row0[None], rows], axis=0)

        def _backtrack(R, T1, T2):
            L = T1 + T2 - 1

            def step(carry, _):
                i, j, done = carry
                valid = jnp.logical_not(done)
                cd = jnp.where((i > 0) & (j > 0), R[jnp.maximum(i - 1, 0), jnp.maximum(j - 1, 0)], BIG)
                cu = jnp.where(i > 0, R[jnp.maximum(i - 1, 0), j], BIG)
                cl = jnp.where(j > 0, R[i, jnp.maximum(j - 1, 0)], BIG)
                choice = jnp.argmin(jnp.stack([cd, cu, cl]))
                ni = jnp.where(choice <= 1, i - 1, i)
                nj = jnp.where((choice == 0) | (choice == 2), j - 1, j)
                at_origin = (i == 0) & (j == 0)
                ni = jnp.where(at_origin, 0, ni)
                nj = jnp.where(at_origin, 0, nj)
                return ((ni, nj, done | at_origin), (i, j, valid))
            init = (jnp.int32(T1 - 1), jnp.int32(T2 - 1), jnp.bool_(False))
            _, (i_idx, j_idx, valid) = lax.scan(step, init, None, length=L)
            return (i_idx, j_idx, valid)

        def _align_one(small, large):
            T_small, d = small.shape
            T_large = large.shape[0]
            D = _pairwise_euclidean(small, large)
            R = _dtw_cost(D)
            i_idx, j_idx, valid = _backtrack(R, T_small, T_large)
            contrib = small[i_idx] * valid[:, None].astype(small.dtype)
            expanded = jnp.zeros((T_large, d), dtype=small.dtype).at[j_idx].add(contrib)
            return expanded
        return jax.vmap(_align_one)(teacher_features, student_features)

    def _L0_ffn_ref(x, router_w, rg, ru, rd, sg, su, sd):
        import jax, jax.numpy as jnp
        import numpy as np
        B, S, H = (4, 512, 256)
        E, K = (8, 2)
        I_R, I_S = (4 * H, 8 * H)
        CAP_FACTOR = 1.25
        SCALE = 1.0
        b, s, h = x.shape
        T = b * s
        capacity = max(int(CAP_FACTOR * T / E), 1)
        xf = x.reshape(T, h)
        eps = jnp.finfo(x.dtype).eps
        xn = xf * jax.lax.rsqrt(jnp.mean(xf * xf, axis=-1, keepdims=True) + eps)
        logits = xn @ router_w.T
        probs = jax.nn.softmax(logits, axis=-1)
        topk_p, topk_i = jax.lax.top_k(probs, K)
        rw = topk_p / jnp.sum(topk_p, axis=-1, keepdims=True)
        one_hot = jax.nn.one_hot(topk_i, E, dtype=x.dtype)
        mask = one_hot.sum(1)
        wdense = (one_hot * rw[..., None]).sum(1)
        sel = mask.T.astype(bool)
        order = jnp.argsort(~sel, axis=1, stable=True)
        dispatch = order[:, :capacity]
        count = sel.sum(axis=1)
        valid = (jnp.arange(capacity)[None, :] < count[:, None]).astype(x.dtype)
        xg = xf[dispatch]
        gate = jax.nn.silu(jnp.einsum('ech,ehi->eci', xg, rg))
        up = jnp.einsum('ech,ehi->eci', xg, ru)
        eout = jnp.einsum('eci,eih->ech', gate * up, rd)
        w = jnp.take_along_axis(wdense.T, dispatch, axis=1)
        contrib = eout * (w * valid)[..., None]
        routed = jnp.zeros_like(xf).at[dispatch.reshape(-1)].add(contrib.reshape(-1, h))
        shared = jax.nn.silu(x @ sg) * (x @ su) @ sd
        return shared + SCALE * routed.reshape(b, s, h)
    x = x + jnp.tanh(g_xattn[0]) * _L0_xattn_ref(ctx_1024, _layernorm(x, axis=-1))
    x = x + jnp.tanh(g_ffn[0]) * _L0_ffn_ref(_layernorm(x, axis=-1), L0_ffn_router_w, L0_ffn_rg, L0_ffn_ru, L0_ffn_rd, L0_ffn_sg, L0_ffn_su, L0_ffn_sd)
    return x

_drawn_inputs = setup_inputs


def setup_inputs(seed=0):
    import zlib

    import numpy as np

    out = dict(_drawn_inputs(seed))
    spreads = {}
    factors = {'L0_ffn_router_w': 4.49, 'L0_ffn_rg': 3.997, 'L0_ffn_ru': 3.951, 'L0_ffn_rd': 3.955}
    for name, (base, spread) in spreads.items():
        noise = np.random.default_rng([zlib.crc32(name.encode()), seed]).standard_normal(out[name].shape)
        drawn = base * np.exp(spread * noise) if base else spread * noise
        out[name] = jnp.asarray(drawn.astype(out[name].dtype))
    for name, factor in factors.items():
        out[name] = (out[name] * factor).astype(out[name].dtype)
    return out
```

```python
from contextlib import ExitStack

import concourse.bass as bass
from concourse import mybir

ALU = mybir.AluOpType
ACT = mybir.ActivationFunctionType
F32 = mybir.dt.float32
F16 = mybir.dt.float16
I32 = mybir.dt.int32
AX_X = mybir.AxisListType.X

P = 128
BIG = 1e30
LN_EPS = 1e-5
RMS_EPS = 1.1920928955078125e-07
CAPACITY_FACTOR = 1.25

Y_SCALE = 64.0
W_SCALE = 256.0
A_SCALE = 16.0
LAG = 2


def flamingo_dtw_moe(nc, x, ctx, g_xattn, g_ffn, router_w, rg, ru, rd, sg, su, sd, out, stop=None):
    B, SEQ, H = x.shape
    E, _, IR = rg.shape
    IS = sg.shape[1]
    T = B * SEQ
    W = T // P
    NJ = P // B
    KC = H // P
    NI = SEQ // P
    CW = W + 1
    SKEW = 2
    S = SEQ + SKEW * (NJ - 1)
    CAP = int(CAPACITY_FACTOR * T / E)
    NG = 4
    WG = W // NG
    GT = WG * P
    NO_SLOT = 4 * E * CAP
    IC, IC_E = IS // P, IR // P
    TILES_E = [(m, min(P, CAP - m)) for m in range(0, CAP, P)]
    JOBS = [("shared", 0), ("shared", 1)] + [("expert", e) for e in range(E)] + [("shared", 2), ("shared", 3)]
    CHUNKS = [(n, kind, i, c) for n, (kind, i) in enumerate(JOBS) for c in range(IC if kind == "shared" else IC_E)]
    NCH = len(CHUNKS)
    FIRST_CHUNK = [next(q for q, ch in enumerate(CHUNKS) if ch[0] == n) for n in range(len(JOBS))] + [NCH]
    PIECE = 1024
    PIECES = 3 * KC * IR // PIECE
    split_at = {}
    for e in range(E):
        base = FIRST_CHUNK[e + 1] + 2 if e else FIRST_CHUNK[0] + 10
        for j in range(PIECES):
            split_at.setdefault(base + j, []).append((e, j))
    turn_at = {FIRST_CHUNK[e + 2] - 3: e for e in range(E)}
    OUT_SCALE = 1.0 / (A_SCALE * W_SCALE)
    assert NJ == 32 and H == 2 * P and SEQ == 4 * P and W == 16

    with ExitStack() as stack:
        def sb(name, shape, dt=F32):
            return stack.enter_context(nc.sbuf_tensor(name, shape, dt))

        def sem(name):
            return stack.enter_context(nc.semaphore(name))

        bank = [stack.enter_context(nc.psum_tensor(f"bank{i}", [P, 512], F32)) for i in range(8)]

        X = sb("x_rows", [P, W, H])
        region_a = sb("region_a", [P, SEQ * CW])
        region_b = sb("region_b", [P, 2 * KC * T // 2])
        region_c = sb("region_c", [P, W * H])
        region_d = sb("region_d", [P, W * (S + 2) // 2])
        region_e = sb("region_e", [P, (S + 2) * CW])
        region_f = sb("region_f", [P, (S + 1) * CW])

        dist = region_a[:, :].rearrange("p (i c) -> p i c", c=CW)
        ctxT = region_b[:, 0:KC * T].rearrange("p (k n) -> p k n", k=KC)
        lnT = region_d[:, 0:KC * T].rearrange("p (k w l) -> p k w l", k=KC, w=W)
        ctx_rows = region_c[:, :].rearrange("p (n h) -> p n h", h=H)
        ln1 = region_e[:, 0:W * H].rearrange("p (w h) -> p w h", h=H)
        ctx_sq = region_f[:, 0:KC * T].rearrange("p (k n) -> p k n", k=KC)
        table = region_e[:, :].rearrange("p (s c) -> p s c", c=CW)
        cost = region_f[:, :].rearrange("p (s c) -> p s c", c=CW)
        is_left = region_d[:, :].bitcast(F16)[:, 0:W * S].rearrange("p (w s) -> p w s", w=W)
        no_up = region_e[:, 0:W * S // 2].bitcast(F16).rearrange("p (w s) -> p w s", w=W)
        halves = W * S // 2
        leave = region_f[:, 0:halves].bitcast(F16).rearrange("p (w s) -> p w s", w=W)
        on_path = region_f[:, halves:2 * halves].bitcast(F16).rearrange("p (w s) -> p w s", w=W)
        path = region_e[:, halves:halves + W * SEQ // 2].bitcast(F16).rearrange("p (w i) -> p w i", w=W)
        pathT = region_d[:, 0:W * SEQ // 2].bitcast(F16).rearrange("p (w n l) -> p w n l", w=W, n=NI)
        ctx16 = region_b[:, 0:W * H].bitcast(F16).rearrange("p (z n h) -> p z n h", z=2, h=H)

        raw = region_d[:, 0:KC * IS]
        gu16 = region_a[:, 0:2 * KC * IS].bitcast(F16).rearrange("p (m z k i) -> p m z k i", m=2, z=2, k=KC)
        down16 = region_c[:, :].bitcast(F16).rearrange("p (z i h) -> p z i h", z=2, h=H)
        yn = region_f[:, 0:W * H].rearrange("p (w h) -> p w h", h=H)
        y16 = region_f[:, W * H:2 * W * H].bitcast(F16).rearrange("p (w z h) -> p w z h", w=W, z=2)
        yT = region_b[:, :].bitcast(F16).rearrange("p (g z k n) -> p g z k n", g=NG, z=2, k=KC)
        ew = 3 * KC * IR
        ex_gu = [r[:, 0:ew].bitcast(F16).rearrange("p (z n) -> p z n", z=2) for r in (region_e, region_f)]
        ex_raw = [r[:, ew:ew + KC * IR] for r in (region_e, region_f)]
        gated = [r[:, ew + KC * IR:ew + KC * IR + 512] for r in (region_e, region_f)]
        act32 = [r[:, ew + KC * IR + 512:ew + KC * IR + 1024] for r in (region_e, region_f)]
        act16 = region_d[:, 0:2048].bitcast(F16).rearrange("p (r z n) -> p r z n", r=4, z=2)
        ex_out = region_d[:, 2048:2048 + 2 * 768].rearrange("p (r m h) -> p r m h", r=2, h=H)
        ex_in = region_d[:, 3584:3584 + 768].bitcast(F16).rearrange("p (m z h) -> p m z h", m=3, z=2)
        gathered_rows = region_e[:, 0:2 * W * H].rearrange("p (w k h) -> p w k h", w=W, k=2)
        slots = nc.dram_tensor("slots", (E * CAP, 2 * H), F16).ap()
        ex_rows = nc.dram_tensor("ex_rows", (E * CAP, H), F32).ap()

        exT = sb("exT", [P, 2, 2 * KC, CAP], F16)
        rw = sb("rw", [P, KC, E])
        rw16 = sb("rw16", [P, 2, KC, E], F16)
        earlier = sb("earlier", [P, P])
        key_of = sb("key_of", [P, E, W])
        slot_of = sb("slot_of", [P, E, W])
        goes_on = sb("goes_on", [P, E, W])
        msq = sb("msq", [P, 3, W])
        rms_eps = sb("rms_eps", [P, 1])
        probs = sb("probs", [P, E, W])
        keys = sb("keys", [P, E, W])
        hot = sb("hot", [P, 2, E, W])
        chosen = sb("chosen", [P, E, W])
        upto = sb("upto", [P, E, W])
        fits = sb("fits", [P, E, W])
        lane_total = sb("lane_total", [P, 2, E])
        per_tok = sb("per_tok", [P, 12, W])
        to_slot = sb("to_slot", [P, 2, W], I32)
        from_slot = sb("from_slot", [P, 2, W], I32)
        out_gate = sb("out_gate", [P, 1])
        ident = sb("ident", [P, P])
        ident16 = sb("ident16", [P, P], F16)
        ones = sb("ones", [P, NJ])
        iota = sb("iota", [P, S], F16)
        iota_less = sb("iota_less", [P, S], F16)
        ctx_norm = sb("ctx_norm", [P, SEQ])
        dist_sq = sb("dist_sq", [P, 2, SEQ])
        ln_norm = sb("ln_norm", [P, W])
        sq_dump = sb("sq_dump", [P, 2, H])
        bn = sb("bn", [P, W, 6])
        mv = sb("mv", [P, W, 2])
        rstd = sb("rstd", [P, 2, W])
        back = sb("back", [P, 2, S + 2], F16)
        pick = sb("pick", [P, 4, S], F16)
        entry = sb("entry", [P, 1])
        leave_at = sb("leave_at", [P, W + 1])
        left_of = sb("left_of", [P, 2])
        lane_keep = sb("lane_keep", [P, 1])
        lane_add = sb("lane_add", [P, 1])
        lane_last = sb("lane_last", [P, 1])
        gates = sb("gates", [P, 2])
        tanhs = sb("tanhs", [P, 2])
        ln_eps = sb("ln_eps", [P, 1])

        x_loaded = sem("x_loaded")
        ctx_loaded = sem("ctx_loaded")
        small_loaded = sem("small_loaded")
        consts = sem("consts")
        bn_done = sem("bn_done")
        dve_step = sem("dve_step")
        act_step = sem("act_step")
        pool_step = sem("pool_step")
        ln1_done = sem("ln1_done")
        std_done = sem("std_done")
        lnT_ready = sem("lnT_ready")
        ctxT_ready = sem("ctxT_ready")
        tr_done = sem("tr_done")
        lnT_moved = sem("lnT_moved")
        ctxT_moved = sem("ctxT_moved")
        sq_done = sem("sq_done")
        norm_ready = sem("norm_ready")
        norm_moved = sem("norm_moved")
        ln_norm_done = sem("ln_norm_done")
        prod_ready = sem("prod_ready")
        prod_used = sem("prod_used")
        dist_sq_done = sem("dist_sq_done")
        dist_done = sem("dist_done")
        skewed = sem("skewed")
        border_set = sem("border_set")
        pads_set = sem("pads_set")
        top_set = sem("top_set")
        min_done = sem("min_done")
        scan_done = sem("scan_done")
        shift_done = sem("shift_done")
        masks_done = sem("masks_done")
        leave_parts = sem("leave_parts")
        on_path_done = sem("on_path_done")
        unskewed = sem("unskewed")
        pathT_ready = sem("pathT_ready")
        pathT_moved_dve = sem("pathT_moved_dve")
        pathT_moved_act = sem("pathT_moved_act")
        ctx_hi_done = sem("ctx_hi_done")
        ctx_lo_done = sem("ctx_lo_done")
        aligned_ready = sem("aligned_ready")
        x2_done = sem("x2_done")
        tanh_done = sem("tanh_done")
        stored = sem("stored")
        raw_loaded = sem("raw_loaded")
        raw_hi_done = sem("raw_hi_done")
        raw_scaled = sem("raw_scaled")
        raw_lo_done = sem("raw_lo_done")
        router_loaded = sem("router_loaded")
        zeros_set = sem("zeros_set")
        slots_zeroed = sem("slots_zeroed")
        bn2_done = sem("bn2_done")
        std2_done = sem("std2_done")
        yn_done = sem("yn_done")
        msq_done = sem("msq_done")
        rms_done = sem("rms_done")
        y_hi_done = sem("y_hi_done")
        y_lo_done = sem("y_lo_done")
        yT_ready = sem("yT_ready")
        yT_moved_act = sem("yT_moved_act")
        yT_moved_dve = sem("yT_moved_dve")
        rw_hi_done = sem("rw_hi_done")
        rw_lo_done = sem("rw_lo_done")
        logits_ready = sem("logits_ready")
        shifted = sem("shifted")
        exp_done = sem("exp_done")
        totals_done = sem("totals_done")
        base_ready = sem("base_ready")
        to_slot_done = sem("to_slot_done")
        scattered = sem("scattered")
        ex_raw_loaded = [sem(f"ex_raw_loaded{i}") for i in range(2)]
        ex_hi_done = sem("ex_hi_done")
        ex_lo_done = sem("ex_lo_done")
        ex_in_loaded = sem("ex_in_loaded")
        exT_ready = sem("exT_ready")
        exT_moved_act = sem("exT_moved_act")
        exT_moved_dve = sem("exT_moved_dve")
        gu_ready = sem("gu_ready")
        silu_done = sem("silu_done")
        gated_done = sem("gated_done")
        act_hi_done = sem("act_hi_done")
        act_lo_done = sem("act_lo_done")
        down_done = sem("down_done")
        ex_out_moved = sem("ex_out_moved")
        ex_stored = sem("ex_stored")
        shared_added = sem("shared_added")
        from_slot_done = sem("from_slot_done")
        gathered = [sem(f"gathered{g}") for g in range(NG)]
        routed_added = sem("routed_added")

        block = stack.enter_context(nc.Block())

        class Count:

            def __init__(self, semaphore):
                self.semaphore, self.n = semaphore, 0

            def link(self, eng, instruction):
                self.n += 1
                instruction.then_inc(self.semaphore, 1)
                eng.wait_ge(self.semaphore, self.n)

            def mark(self, instruction):
                self.n += 1
                instruction.then_inc(self.semaphore, 1)
                return self.n

        def store_expert(sp, e):
            full = sum(n == P for _, n in TILES_E)
            r = e * CAP
            sp.wait_ge(ex_out_moved, 2 * (e + 1))
            sp.dma_start(ex_rows[r:r + full * P, :].rearrange("(m p) h -> p m h", p=P),
                         ex_out[:, e % 2, 0:full, :]).then_inc(ex_stored, 16)
            for m, n in TILES_E[full:]:
                sp.dma_start(ex_rows[r + m:r + m + n, :], ex_out[0:n, e % 2, m // P, :]).then_inc(ex_stored, 16)

        @block.sync
        def _(sp):
            sp.dma_start(X[:, :, :], x.rearrange("b (l w) h -> (b l) w h", w=W)).then_inc(x_loaded, 16)
            sp.dma_start(ctx_rows, ctx.rearrange("b (c p) h -> p (b c) h", p=P)).then_inc(ctx_loaded, 16)
            for n, g in enumerate((g_xattn, g_ffn)):
                sp.dma_start(gates[:, n:n + 1], g.partition_broadcast(P)).then_inc(small_loaded, 16)
            for k in range(KC):
                sp.dma_start(rw[:, k, :], router_w[:, k * P:(k + 1) * P].rearrange("e p -> p e"),
                             allow_slow_non_contiguous=True).then_inc(router_loaded, 16)
            sp.wait_ge(dist_done, W)
            sp.wait_ge(pads_set, 3)
            for j in range(0, NJ, 2):
                sp.dma_start(region_e[j:P:NJ, (SKEW * j + 2) * CW:(SKEW * j + 2 + SEQ) * CW],
                             region_a[j:P:NJ, 0:SEQ * CW]).then_inc(skewed, 16)
            sp.wait_ge(prod_ready, W)
            for n, m in enumerate((sg.rearrange("(k p) i -> p k i", p=P), su.rearrange("(k p) i -> p k i", p=P),
                                   sd.rearrange("(k p) h -> p k h", p=P))):
                if n:
                    sp.wait_ge(raw_lo_done, n)
                sp.dma_start(raw.rearrange("p (k i) -> p k i", k=m.shape[1]), m).then_inc(raw_loaded, 16)
            sp.wait_ge(zeros_set, 1)
            for n in range(E * CAP // P):
                sp.dma_start(slots[n * P:(n + 1) * P, :], dist_sq[:, 0, 0:H].bitcast(F16)).then_inc(slots_zeroed, 16)
            sp.wait_ge(on_path_done, W)
            for j in range(0, NJ, 2):
                sp.dma_start(path[j:P:NJ, :, :], on_path[j:P:NJ, :, SKEW * j:SKEW * j + SEQ]).then_inc(unskewed, 16)

            def load_expert(u):
                e, m = divmod(u, 3)
                src = (rg[e], ru[e], rd[e])[m].rearrange("(k p) i -> p k i", p=P)
                sp.dma_start(ex_raw[u % 2].rearrange("p (k i) -> p k i", k=src.shape[1]), src).then_inc(ex_raw_loaded[u % 2], 16)

            sp.wait_ge(pathT_ready, W // 2)
            load_expert(0)
            sp.wait_ge(scattered, 16 * 2 * W)
            load_expert(1)
            tiles_full = sum(n == P for _, n in TILES_E)
            for e in range(E):
                if e:
                    sp.wait_ge(exT_ready, 2 * e)
                r = e * CAP
                sp.dma_start(ex_in[:, 0:tiles_full, :, :], slots[r:r + tiles_full * P, :].rearrange(
                    "(m p) (z h) -> p m z h", p=P, z=2)).then_inc(ex_in_loaded, 16)
                for m, n in TILES_E[tiles_full:]:
                    sp.dma_start(ex_in[0:n, m // P, :, :], slots[r + m:r + m + n, :].rearrange(
                        "p (z h) -> p z h", z=2)).then_inc(ex_in_loaded, 16)
                for u in range(3 * e + 2, min(3 * e + 5, 3 * E)):
                    sp.wait_ge(ex_lo_done, (u - 1) * KC)
                    load_expert(u)
                if e:
                    store_expert(sp, e - 1)
            store_expert(sp, E - 1)
            outs = out.rearrange("b (l w) h -> (b l) w h", w=W)
            for g in range(NG):
                sp.wait_ge(shared_added, 2 * (g + 1))
                sp.wait_ge(routed_added, 2 * WG * (g + 1))
                sp.dma_start(outs[:, g * WG:(g + 1) * WG, :], X[:, g * WG:(g + 1) * WG, :]).then_inc(stored, 16)
            sp.wait_ge(stored, 16 * NG)

        @block.gpsimd
        def _(pool):
            pool.memset(ident[:, :], 0.0).then_inc(consts, 1)
            pool.memset(ident16[:, :], 0.0).then_inc(consts, 1)
            pool.memset(ones[:, :], 1.0).then_inc(consts, 1)
            pool.memset(ln_eps[:, :], LN_EPS).then_inc(consts, 1)
            pool.iota(iota[:, :], [[1, S]], base=0, channel_multiplier=0,
                      allow_small_or_imprecise_dtypes=True).then_inc(consts, 1)
            pool.wait_ge(consts, 5)
            pool.tensor_scalar(iota_less[:, :], iota[:, :], 0.5, None, ALU.subtract).then_inc(consts, 1)
            for m in (ident, ident16):
                pool.affine_select(out=m[:, :], in_=m[:, :], compare_op=ALU.not_equal, fill=1.0,
                                   base=0, pattern=[[-1, P]], channel_multiplier=1).then_inc(consts, 1)
            pool.memset(earlier[:, :], 1.0).then_inc(consts, 1)
            pool.memset(rms_eps[:, :], RMS_EPS).then_inc(consts, 1)
            pool.memset(goes_on[:, :, :], 1.0).then_inc(consts, 1)
            pool.iota(key_of[:, :, :], [[-1, E], [0, W]], base=E, channel_multiplier=0,
                      allow_small_or_imprecise_dtypes=True).then_inc(consts, 1)
            pool.iota(slot_of[:, :, :], [[CAP, E], [0, W]], base=0, channel_multiplier=0,
                      allow_small_or_imprecise_dtypes=True).then_inc(consts, 1)
            pool.wait_ge(consts, 11)
            pool.memset(goes_on[:, :, 0:1], 0.0).then_inc(consts, 1)
            pool.affine_select(out=earlier[:, :], in_=earlier[:, :], compare_op=ALU.is_gt, fill=0.0,
                               base=0, pattern=[[1, P]], channel_multiplier=-1).then_inc(consts, 1)
            pool.memset(dist[:, :, 0:1], 0.0).then_inc(border_set, 1)
            pool.memset(entry[:, :], float(S - 1)).then_inc(border_set, 1)
            for b in range(B):
                pool.wait_ge(border_set, 2 + b)
                pool.memset(dist[NJ * b:NJ * b + 1, :, 0:1], BIG).then_inc(border_set, 1)
            pool.wait_ge(border_set, 2 + B)
            for n in range(KC * B):
                b, k = divmod(n, KC)
                s = slice(b * SEQ, (b + 1) * SEQ)
                pool.wait_ge(ctxT_moved, n + 1)
                pool.tensor_tensor(ctx_sq[:, k, s], ctxT[:, k, s], ctxT[:, k, s], ALU.mult).then_inc(sq_done, 1)
            pool.wait_ge(lnT_ready, KC * W // 4)
            pool.wait_ge(ln_norm_done, W)
            pool.memset(region_e[:, 0:(SKEW * (NJ - 1) + 2) * CW], 0.0).then_inc(pads_set, 1)
            pool.memset(region_e[:, (SEQ + 2) * CW:(S + 2) * CW], 0.0).then_inc(pads_set, 1)
            pool.wait_ge(pads_set, 2)
            pool.memset(table[:, 0, 0:1], BIG).then_inc(pads_set, 1)
            pool.wait_ge(norm_ready, 1)
            pool.memset(cost[:, 0, :], BIG).then_inc(top_set, 1)
            for b in range(B):
                pool.wait_ge(top_set, 1 + b)
                pool.memset(cost[NJ * b:NJ * b + 1, 0, 0:1], 0.0).then_inc(top_set, 1)
            pool.wait_ge(top_set, 1 + B)
            for b in range(B):
                pool.wait_ge(ctx_hi_done, b + 1)
                s = slice(b * NI, (b + 1) * NI)
                pool.tensor_tensor(ctx16[:, 1, s, :], ctx_rows[:, s, :], ctx16[:, 0, s, :],
                                   ALU.subtract).then_inc(ctx_lo_done, 1)
            pool.wait_ge(dist_done, W)
            pool.memset(dist_sq[:, 0, 0:H], 0.0).then_inc(zeros_set, 1)
            for n, lo in enumerate((gu16[:, 0, 1, :, :], gu16[:, 1, 1, :, :], down16[:, 1, :, :])):
                hi = (gu16[:, 0, 0, :, :], gu16[:, 1, 0, :, :], down16[:, 0, :, :])[n]
                pool.wait_ge(raw_scaled, n + 1)
                pool.tensor_tensor(lo, raw.rearrange("p (k i) -> p k i", k=lo.shape[1]), hi,
                                   ALU.subtract).then_inc(raw_lo_done, 1)
            pool.wait_ge(masks_done, 2)
            for w in range(W):
                pool.tensor_tensor(leave[:, w, :], is_left[:, w, :], iota[:, :], ALU.mult).then_inc(leave_parts, 1)
                pool.tensor_tensor(on_path[:, w, :], no_up[:, w, :], iota_less[:, :], ALU.mult).then_inc(leave_parts, 1)
            pool.wait_ge(slots_zeroed, 16 * (E * CAP // P))
            pool.wait_ge(y_lo_done, NG)
            pool.wait_ge(y_hi_done, NG)
            pool.wait_ge(to_slot_done, 1)
            for w in range(W):
                for k in range(2):
                    pool.indirect_dma_start(slots, bass.IndirectOffsetOnAxis(ap=to_slot[:, k, w:w + 1], axis=0),
                                            y16[:, w, :, :].rearrange("p z h -> p (z h)"), None,
                                            bounds_check=E * CAP - 1, oob_is_err=False).then_inc(scattered, 16)
            pool.wait_ge(from_slot_done, 1)
            pool.wait_ge(ex_stored, 16 * E * 2)
            pool.wait_ge(down_done, FIRST_CHUNK[E + 2])
            pool.wait_ge(ex_lo_done, E * PIECES)
            for w in range(W):
                for k in range(2):
                    pool.indirect_dma_start(gathered_rows[:, w, k, :], None, ex_rows,
                                            bass.IndirectOffsetOnAxis(ap=from_slot[:, k, w:w + 1], axis=0),
                                            bounds_check=E * CAP - 1, oob_is_err=False).then_inc(gathered[w // WG], 16)

        @block.scalar
        def _(act):
            def move_ctxT(n):
                b, k = divmod(n, KC)
                act.wait_ge(ctxT_ready, n + 1)
                act.activation(ctxT[:, k, b * SEQ:(b + 1) * SEQ], bank[n % 4][:, :], ACT.Copy).then_inc(ctxT_moved, 1)

            for n in range(KC * B // 2):
                move_ctxT(n)
            act.wait_ge(consts, 4)
            act.wait_ge(bn_done, 1)
            act.activation(rstd[:, 0, :], mv[:, :, 1], ACT.Sqrt, bias=ln_eps[:, 0:1]).then_inc(std_done, 1)
            for n in range(KC * B // 2, KC * B):
                move_ctxT(n)
            for n in range(KC * W // 4):
                q, k = divmod(n, KC)
                act.wait_ge(lnT_ready, n + 1)
                act.activation(lnT[:, k, 4 * q:4 * q + 4, :], bank[4 + n % 4][:, :], ACT.Copy,
                               scale=-2.0).then_inc(lnT_moved, 1)
            act.wait_ge(norm_ready, 1)
            act.activation(ctx_norm[:, :], bank[0][:, :], ACT.Copy).then_inc(norm_moved, 1)
            act.wait_ge(ln1_done, W)
            for w in range(W):
                if w >= 2:
                    act.wait_ge(ln_norm_done, w - 1)
                act.activation(sq_dump[:, w % 2, :], ln1[:, w, :], ACT.Square,
                               accum_out=ln_norm[:, w:w + 1]).then_inc(ln_norm_done, 1)
            act.wait_ge(border_set, 1)
            for w in range(W):
                act.wait_ge(dist_sq_done, w + 1)
                act.activation(dist[:, :, 1 + w], dist_sq[:, w % 2, :], ACT.Sqrt).then_inc(dist_done, 1)
            act.wait_ge(dist_done, W)
            act.wait_ge(border_set, 2 + B)
            act.wait_ge(pads_set, 3)
            for j in range(1, NJ, 2):
                act.dma_start(region_e[j:P:NJ, (SKEW * j + 2) * CW:(SKEW * j + 2 + SEQ) * CW],
                              region_a[j:P:NJ, 0:SEQ * CW]).then_inc(skewed, 16)
            act.wait_ge(prod_ready, W)
            for b in range(B):
                s = slice(b * NI, (b + 1) * NI)
                act.activation(ctx16[:, 0, s, :], ctx_rows[:, s, :], ACT.Copy).then_inc(ctx_hi_done, 1)
            act.wait_ge(skewed, 16 * NJ)
            act.wait_ge(ctx_lo_done, B)
            for n, hi in enumerate((gu16[:, 0, 0, :, :], gu16[:, 1, 0, :, :], down16[:, 0, :, :])):
                act.wait_ge(raw_loaded, 16 * (n + 1))
                act.activation(hi, raw.rearrange("p (k i) -> p k i", k=hi.shape[1]), ACT.Copy,
                               scale=W_SCALE).then_inc(raw_hi_done, 1)
                act.activation(raw, raw, ACT.Copy, scale=W_SCALE).then_inc(raw_scaled, 1)
            act.wait_ge(router_loaded, 16 * KC)
            act.activation(rw16[:, 0, :, :], rw[:, :, :], ACT.Copy, scale=W_SCALE).then_inc(rw_hi_done, 1)
            act.wait_ge(small_loaded, 32)
            act.activation(tanhs[:, :], gates[:, :], ACT.Tanh).then_inc(tanh_done, 1)
            act.wait_ge(on_path_done, W)
            for j in range(1, NJ, 2):
                act.dma_start(path[j:P:NJ, :, :], on_path[j:P:NJ, :, SKEW * j:SKEW * j + SEQ]).then_inc(unskewed, 16)
            for n in range(1, W // 2, 2):
                act.wait_ge(pathT_ready, n + 1)
                act.activation(pathT[:, 2 * n:2 * n + 2, :, :], bank[n % 4][:, :].bitcast(F16).rearrange("p (w n l) -> p w n l", w=2, n=NI), ACT.Copy).then_inc(pathT_moved_act, 1)

            act.wait_ge(bn2_done, 1)
            act.activation(rstd[:, 0, :], mv[:, :, 1], ACT.Sqrt, bias=ln_eps[:, 0:1]).then_inc(std2_done, 1)
            for g in range(NG):
                s = slice(g * WG, (g + 1) * WG)
                act.wait_ge(yn_done, (g + 1) * WG)
                act.activation(y16[:, s, 0, :], yn[:, s, :], ACT.Copy).then_inc(y_hi_done, 1)
            for w in range(W):
                if w >= 2:
                    act.wait_ge(msq_done, w - 1)
                act.activation(sq_dump[:, w % 2, :], yn[:, w, :], ACT.Square, scale=1.0 / Y_SCALE,
                               accum_out=msq[:, 0, w:w + 1]).then_inc(msq_done, 1)
            act.wait_ge(msq_done, W)
            act.activation(msq[:, 1, :], msq[:, 0, :], ACT.Sqrt, scale=1.0 / H, bias=rms_eps[:, 0:1]).then_inc(rms_done, 1)
            for g in range(NG):
                act.wait_ge(yT_ready, 2 * g + 1)
                act.activation(yT[:, g, 0, :, :], bank[6][:, :].bitcast(F16).rearrange("p (k n) -> p k n", k=KC),
                               ACT.Copy).then_inc(yT_moved_act, 1)
            act.wait_ge(shifted, 1)
            act.activation(probs[:, :, :], probs[:, :, :], ACT.Exp).then_inc(exp_done, 1)

            for q in range(NCH + 1):
                if q < NCH:
                    n, kind, i, c = CHUNKS[q]
                    cols = GT if kind == "shared" else CAP
                    act.wait_ge(gu_ready, q + 1)
                    if q >= 2:
                        act.wait_ge(gated_done, q - 1)
                    act.activation(gated[q % 2][:, 0:cols], bank[q % 2][:, 0:cols], ACT.Silu,
                                   scale=1.0 / (Y_SCALE * W_SCALE)).then_inc(silu_done, 1)
                if q >= 1:
                    r = q - 1
                    cols = GT if CHUNKS[r][1] == "shared" else CAP
                    act.wait_ge(gated_done, q)
                    if r >= 4:
                        act.wait_ge(down_done, r - 3)
                    act.activation(act16[:, r % 4, 0, 0:cols], act32[r % 2][:, 0:cols], ACT.Copy).then_inc(act_hi_done, 1)
                for e, j in split_at.get(q, ()):
                    u, k = divmod(j, KC)
                    m = 3 * e + u
                    act.wait_ge(ex_raw_loaded[m % 2], 16 * (m // 2 + 1))
                    if e >= 2:
                        act.wait_ge(down_done, FIRST_CHUNK[e + 1])
                    act.activation(ex_gu[e % 2][:, 0, j * PIECE:(j + 1) * PIECE],
                                   ex_raw[m % 2][:, k * PIECE:(k + 1) * PIECE], ACT.Copy,
                                   scale=W_SCALE).then_inc(ex_hi_done, 1)
                if q in turn_at:
                    e = turn_at[q]
                    act.wait_ge(exT_ready, 2 * e + 1)
                    act.activation(exT[:, e % 2, 0:KC, :], bank[6][:, :].bitcast(F16)[:, 0:KC * CAP].rearrange(
                        "p (k n) -> p k n", k=KC), ACT.Copy).then_inc(exT_moved_act, 1)
                job = next((n for n in range(len(JOBS)) if FIRST_CHUNK[n + 1] + LAG - 1 == q), None)
                if job is not None and JOBS[job][0] == "expert":
                    e = JOBS[job][1]
                    act.wait_ge(down_done, FIRST_CHUNK[job + 1])
                    if e >= 2:
                        act.wait_ge(ex_stored, 32 * (e - 1))
                    act.activation(ex_out[:, e % 2, 0:2, :], bank[4][:, :].rearrange("p (m h) -> p m h", m=2),
                                   ACT.Copy).then_inc(ex_out_moved, 1)
                    act.activation(ex_out[0:64, e % 2, 2, :], bank[5][0:64, 0:H], ACT.Copy).then_inc(ex_out_moved, 1)

        @block.vector
        def _(dve):
            step = Count(dve_step)

            def link(instruction):
                step.link(dve, instruction)

            dve.wait_ge(x_loaded, 16)
            for w in range(W):
                last = step.mark(nc.vector.bn_stats(bn[:, w, :], X[:, w, :]))
            dve.wait_ge(dve_step, last)
            for w in range(W - 1):
                last = step.mark(nc.vector.bn_aggr(mv[:, w, :], bn[:, w, :]))
            dve.wait_ge(dve_step, last)
            nc.vector.bn_aggr(mv[:, W - 1, :], bn[:, W - 1, :]).then_inc(bn_done, 1)
            dve.wait_ge(std_done, 1)
            link(nc.vector.reciprocal(rstd[:, 1, :], rstd[:, 0, :]))
            for w in range(W):
                nc.vector.tensor_scalar(ln1[:, w, :], X[:, w, :], mv[:, w, 0:1], rstd[:, 1, w:w + 1],
                                        ALU.subtract, ALU.mult).then_inc(ln1_done, 1)
            dve.wait_ge(consts, 8)
            link(nc.vector.tensor_reduce(lane_last[:, :], ident[:, NJ - 1:P:NJ], AX_X, ALU.add))
            nc.vector.tensor_scalar(lane_keep[:, :], lane_last[:, :], -1.0, 1.0, ALU.mult, ALU.add).then_inc(dve_step, 1)
            step.n += 1
            link(nc.vector.tensor_scalar(lane_add[:, :], lane_last[:, :], float(S - 1 + SKEW), -float(SKEW),
                                         ALU.mult, ALU.add))
            dve.wait_ge(norm_moved, 1)
            dve.wait_ge(ln_norm_done, W)
            for w in range(W):
                dve.wait_ge(prod_ready, w + 1)
                if w >= 2:
                    dve.wait_ge(dist_done, w - 1)
                nc.vector.scalar_tensor_tensor(out=dist_sq[:, w % 2, :], in0=bank[1 + w % 3][:, :],
                                               scalar=ln_norm[:, w:w + 1], in1=ctx_norm[:, :],
                                               op0=ALU.add, op1=ALU.add).then_inc(prod_used, 1)
                dve.wait_ge(prod_used, w + 1)
                nc.vector.tensor_scalar(dist_sq[:, w % 2, :], dist_sq[:, w % 2, :], 0.0, None,
                                        ALU.max).then_inc(dist_sq_done, 1)
            dve.wait_ge(skewed, 16 * NJ)
            dve.wait_ge(top_set, 1 + B)
            to_right = [0] + list(range(NJ - 1))
            for s in range(S):
                if s:
                    dve.wait_ge(scan_done, s)
                nc.vector.tensor_tensor(table[:, s, 1:CW], cost[:, s, 1:CW], cost[:, s, 0:W],
                                        ALU.min).then_inc(min_done, 1)
                dve.wait_ge(min_done, s + 1)
                if s:
                    dve.wait_ge(shift_done, s)
                nc.vector.tensor_tensor_scan(out=cost[:, s + 1, :], data0=table[:, s, :], data1=table[:, s + 2, :],
                                             initial=BIG, op0=ALU.min, op1=ALU.add).then_inc(scan_done, 1)
                nc.vector.stream_shuffle(table[:, s + 1, 0:1], cost[:, s, W:CW], to_right).then_inc(shift_done, 1)
            dve.wait_ge(scan_done, S)
            dve.wait_ge(shift_done, S)
            dve.wait_ge(raw_lo_done, 3)
            at_left = cost[:, 1:S + 1, 0:W].rearrange("p s w -> p w s")
            at_diag = cost[:, 0:S, 0:W].rearrange("p s w -> p w s")
            at_up = cost[:, 0:S, 1:CW].rearrange("p s w -> p w s")
            least = table[:, 0:S, 1:CW].rearrange("p s w -> p w s")
            nc.vector.tensor_tensor(is_left, at_left, least, ALU.is_lt).then_inc(masks_done, 1)
            dve.wait_ge(masks_done, 1)
            nc.vector.tensor_tensor(no_up, at_up, at_diag, ALU.is_ge).then_inc(masks_done, 1)
            step.mark(nc.vector.memset(back[:, :, 0:1], 0.0))
            link(nc.vector.tensor_copy(back[:, 0, 1:S + 1], iota[:, :]))
            dve.wait_ge(masks_done, 2)
            for w in range(W):
                a = w % 2
                step.mark(nc.vector.tensor_tensor(pick[:, 0, :], no_up[:, w, :], back[:, a, 0:S], ALU.mult))
                link(nc.vector.tensor_tensor(pick[:, 1, :], is_left[:, w, :], back[:, a, 1:S + 1], ALU.mult))
                link(nc.vector.tensor_tensor_scan(out=back[:, 1 - a, 1:S + 1], data0=pick[:, 0, :], data1=pick[:, 1, :],
                                                  initial=0.0, op0=ALU.max, op1=ALU.max))
            to_left = list(range(1, NJ)) + [NJ - 1]
            dve.wait_ge(border_set, 2 + B)
            for j in range(NJ - 1):
                link(nc.vector.scalar_tensor_tensor(out=pick[:, 0, :], in0=iota[:, :], scalar=entry[:, 0:1],
                                                    in1=back[:, 0, 1:S + 1], op0=ALU.is_equal, op1=ALU.mult,
                                                    accum_out=left_of[:, 0:1]))
                link(nc.vector.stream_shuffle(left_of[:, 1:2], left_of[:, 0:1], to_left))
                link(nc.vector.tensor_scalar(entry[:, :], left_of[:, 1:2], lane_keep[:, 0:1], lane_add[:, 0:1],
                                             ALU.mult, ALU.add))
            link(nc.vector.tensor_copy(leave_at[:, W:W + 1], entry[:, :]))
            dve.wait_ge(leave_parts, 2 * W)
            link(nc.vector.tensor_tensor(leave, leave, on_path, ALU.max))
            for w in reversed(range(W)):
                step.mark(nc.vector.tensor_scalar(pick[:, 2 + w % 2, :], iota[:, :], leave_at[:, w + 1:w + 2], None, ALU.is_le))
                link(nc.vector.scalar_tensor_tensor(out=pick[:, 0, :], in0=iota[:, :], scalar=leave_at[:, w + 1:w + 2],
                                                    in1=leave[:, w, :], op0=ALU.is_le, op1=ALU.mult))
                link(nc.vector.tensor_reduce(leave_at[:, w:w + 1], pick[:, 0, :], AX_X, ALU.max))
                nc.vector.scalar_tensor_tensor(out=on_path[:, w, :], in0=iota[:, :], scalar=leave_at[:, w:w + 1],
                                               in1=pick[:, 2 + w % 2, :], op0=ALU.is_ge, op1=ALU.mult).then_inc(on_path_done, 1)
            dve.wait_ge(on_path_done, W)
            for n in range(0, W // 2, 2):
                dve.wait_ge(pathT_ready, n + 1)
                nc.vector.tensor_copy(pathT[:, 2 * n:2 * n + 2, :, :], bank[n % 4][:, :].bitcast(F16).rearrange("p (w n l) -> p w n l", w=2, n=NI)).then_inc(pathT_moved_dve, 1)
            dve.wait_ge(tanh_done, 1)
            for n in range(W // 2):
                dve.wait_ge(aligned_ready, n + 1)
                nc.vector.scalar_tensor_tensor(out=X[:, 2 * n:2 * n + 2, :], in0=bank[4 + n % 4][:, :],
                                               scalar=tanhs[:, 0:1], in1=X[:, 2 * n:2 * n + 2, :],
                                               op0=ALU.mult, op1=ALU.add).then_inc(x2_done, 1)


            for w in range(W):
                dve.wait_ge(x2_done, w // 2 + 1)
                last = step.mark(nc.vector.bn_stats(bn[:, w, :], X[:, w, :]))
            dve.wait_ge(dve_step, last)
            for w in range(W - 1):
                last = step.mark(nc.vector.bn_aggr(mv[:, w, :], bn[:, w, :]))
            dve.wait_ge(dve_step, last)
            nc.vector.bn_aggr(mv[:, W - 1, :], bn[:, W - 1, :]).then_inc(bn2_done, 1)
            dve.wait_ge(std2_done, 1)
            link(nc.vector.reciprocal(rstd[:, 1, :], rstd[:, 0, :]))
            link(nc.vector.tensor_scalar(rstd[:, 1, :], rstd[:, 1, :], Y_SCALE, None, ALU.mult))
            dve.wait_ge(unskewed, 16 * NJ)
            for w in range(W):
                nc.vector.tensor_scalar(yn[:, w, :], X[:, w, :], mv[:, w, 0:1], rstd[:, 1, w:w + 1],
                                        ALU.subtract, ALU.mult).then_inc(yn_done, 1)
            for g in range(NG):
                s = slice(g * WG, (g + 1) * WG)
                dve.wait_ge(y_hi_done, g + 1)
                dve.wait_ge(yn_done, (g + 1) * WG)
                nc.vector.tensor_tensor(y16[:, s, 1, :], yn[:, s, :], y16[:, s, 0, :], ALU.subtract).then_inc(y_lo_done, 1)
            dve.wait_ge(rw_hi_done, 1)
            nc.vector.scalar_tensor_tensor(out=rw16[:, 1, :, :], in0=rw[:, :, :], scalar=W_SCALE,
                                           in1=rw16[:, 0, :, :], op0=ALU.mult, op1=ALU.subtract).then_inc(rw_lo_done, 1)
            for g in range(NG):
                dve.wait_ge(yT_ready, 2 * g + 2)
                nc.vector.tensor_copy(yT[:, g, 1, :, :], bank[7][:, :].bitcast(F16).rearrange("p (k n) -> p k n", k=KC))\
                    .then_inc(yT_moved_dve, 1)

            by_token = "p e w -> p w e"
            all_e = (P, E, W)

            def over_e(row):
                return row.unsqueeze(1).broadcast_to(all_e)

            dve.wait_ge(rms_done, 1)
            link(nc.vector.reciprocal(msq[:, 2, :], msq[:, 1, :]))
            link(nc.vector.tensor_scalar(msq[:, 2, :], msq[:, 2, :], 1.0 / (Y_SCALE * W_SCALE), None, ALU.mult))
            dve.wait_ge(logits_ready, 1)
            link(nc.vector.tensor_tensor(probs[:, :, :], bank[0][:, 0:W * E].rearrange("p (w e) -> p e w", e=E),
                                         over_e(msq[:, 2, :]), ALU.mult))
            link(nc.vector.tensor_reduce(per_tok[:, 0, :], probs[:, :, :].rearrange(by_token), AX_X, ALU.max))
            nc.vector.tensor_tensor(probs[:, :, :], probs[:, :, :], over_e(per_tok[:, 0, :]), ALU.subtract).then_inc(shifted, 1)
            dve.wait_ge(exp_done, 1)
            link(nc.vector.tensor_reduce(per_tok[:, 1, :], probs[:, :, :].rearrange(by_token), AX_X, ALU.add))
            link(nc.vector.reciprocal(per_tok[:, 2, :], per_tok[:, 1, :]))
            link(nc.vector.tensor_tensor(probs[:, :, :], probs[:, :, :], over_e(per_tok[:, 2, :]), ALU.mult))
            for k in range(2):
                link(nc.vector.tensor_reduce(per_tok[:, 3 + k, :], probs[:, :, :].rearrange(by_token), AX_X, ALU.max))
                link(nc.vector.tensor_tensor(keys[:, :, :], probs[:, :, :], over_e(per_tok[:, 3 + k, :]), ALU.is_equal))
                link(nc.vector.tensor_tensor(keys[:, :, :], keys[:, :, :], key_of[:, :, :], ALU.mult))
                link(nc.vector.tensor_reduce(per_tok[:, 5, :], keys[:, :, :].rearrange(by_token), AX_X, ALU.max))
                link(nc.vector.tensor_tensor(hot[:, k, :, :], keys[:, :, :], over_e(per_tok[:, 5, :]), ALU.is_equal))
                if k == 0:
                    link(nc.vector.scalar_tensor_tensor(out=probs[:, :, :], in0=hot[:, 0, :, :], scalar=-2.0,
                                                        in1=probs[:, :, :], op0=ALU.mult, op1=ALU.add))
            link(nc.vector.tensor_tensor(chosen[:, :, :], hot[:, 0, :, :], hot[:, 1, :, :], ALU.add))
            link(nc.vector.tensor_tensor_scan(out=upto[:, :, :].rearrange("p e w -> p (e w)"),
                                              data0=goes_on[:, :, :].rearrange("p e w -> p (e w)"),
                                              data1=chosen[:, :, :].rearrange("p e w -> p (e w)"),
                                              initial=0.0, op0=ALU.mult, op1=ALU.add))
            nc.vector.tensor_copy(lane_total[:, 0, :], upto[:, :, W - 1]).then_inc(totals_done, 1)
            dve.wait_ge(totals_done, 1)
            link(nc.vector.tensor_tensor(upto[:, :, :], upto[:, :, :], chosen[:, :, :], ALU.subtract))
            dve.wait_ge(base_ready, 1)
            link(nc.vector.tensor_copy(lane_total[:, 1, :], bank[1][:, 0:E]))
            link(nc.vector.tensor_tensor(upto[:, :, :], upto[:, :, :], lane_total[:, 1, :].unsqueeze(2).broadcast_to(all_e),
                                         ALU.add))
            step.mark(nc.vector.tensor_scalar(fits[:, :, :], upto[:, :, :], float(CAP), None, ALU.is_lt))
            link(nc.vector.tensor_tensor(upto[:, :, :], upto[:, :, :], slot_of[:, :, :], ALU.add))
            for k in range(2):
                for v, row in ((fits, 6 + k), (upto, 8 + k)):
                    link(nc.vector.tensor_tensor(keys[:, :, :], hot[:, k, :, :], v[:, :, :], ALU.mult))
                    link(nc.vector.tensor_reduce(per_tok[:, row, :], keys[:, :, :].rearrange(by_token), AX_X, ALU.add))
            link(nc.vector.tensor_tensor(per_tok[:, 10:12, :], per_tok[:, 8:10, :], per_tok[:, 6:8, :], ALU.mult))
            nc.vector.tensor_copy(from_slot[:, :, :], per_tok[:, 10:12, :]).then_inc(from_slot_done, 1)
            dve.wait_ge(from_slot_done, 1)
            link(nc.vector.tensor_scalar(per_tok[:, 8:10, :], per_tok[:, 8:10, :], float(NO_SLOT), None, ALU.subtract))
            link(nc.vector.tensor_tensor(per_tok[:, 8:10, :], per_tok[:, 8:10, :], per_tok[:, 6:8, :], ALU.mult))
            link(nc.vector.tensor_scalar(per_tok[:, 8:10, :], per_tok[:, 8:10, :], float(NO_SLOT), None, ALU.add))
            nc.vector.tensor_copy(to_slot[:, :, :], per_tok[:, 8:10, :]).then_inc(to_slot_done, 1)
            link(nc.vector.tensor_tensor(per_tok[:, 0, :], per_tok[:, 3, :], per_tok[:, 4, :], ALU.add))
            link(nc.vector.reciprocal(per_tok[:, 1, :], per_tok[:, 0, :]))
            link(nc.vector.tensor_scalar(out_gate[:, :], tanhs[:, 1:2], OUT_SCALE, None, ALU.mult))
            for k in range(2):
                link(nc.vector.tensor_tensor(per_tok[:, 3 + k, :], per_tok[:, 3 + k, :], per_tok[:, 1, :], ALU.mult))
            link(nc.vector.scalar_tensor_tensor(out=per_tok[:, 3:5, :], in0=per_tok[:, 3:5, :], scalar=out_gate[:, 0:1],
                                                in1=per_tok[:, 6:8, :], op0=ALU.mult, op1=ALU.mult))

            def add_routed(w):
                for k in range(2):
                    dve.wait_ge(gathered[w // WG], 16 * 2 * WG)
                    if k:
                        dve.wait_ge(routed_added, 2 * w + 1)
                    nc.vector.scalar_tensor_tensor(out=X[:, w, :], in0=gathered_rows[:, w, k, :],
                                                   scalar=per_tok[:, 3 + k, w:w + 1], in1=X[:, w, :],
                                                   op0=ALU.mult, op1=ALU.add).then_inc(routed_added, 1)

            def add_shared(g):
                for h in range(2):
                    w = g * WG + 2 * h
                    nc.vector.scalar_tensor_tensor(out=X[:, w:w + 2, :], in0=bank[4 + h][:, :].rearrange(
                        "p (w h) -> p w h", w=2), scalar=out_gate[:, 0:1], in1=X[:, w:w + 2, :],
                        op0=ALU.mult, op1=ALU.add).then_inc(shared_added, 1)

            for q in range(NCH + 1):
                if q < NCH:
                    n, kind, i, c = CHUNKS[q]
                    cols = GT if kind == "shared" else CAP
                    dve.wait_ge(silu_done, q + 1)
                    if q >= 2:
                        dve.wait_ge(act_lo_done, q - 1)
                    nc.vector.scalar_tensor_tensor(out=act32[q % 2][:, 0:cols], in0=bank[2 + q % 2][:, 0:cols],
                                                   scalar=A_SCALE / (Y_SCALE * W_SCALE), in1=gated[q % 2][:, 0:cols],
                                                   op0=ALU.mult, op1=ALU.mult).then_inc(gated_done, 1)
                if q >= 1:
                    r = q - 1
                    cols = GT if CHUNKS[r][1] == "shared" else CAP
                    dve.wait_ge(act_hi_done, q)
                    dve.wait_ge(gated_done, q)
                    nc.vector.tensor_tensor(act16[:, r % 4, 1, 0:cols], act32[r % 2][:, 0:cols],
                                            act16[:, r % 4, 0, 0:cols], ALU.subtract).then_inc(act_lo_done, 1)
                for e, j in split_at.get(q, ()):
                    u, k = divmod(j, KC)
                    m = 3 * e + u
                    dve.wait_ge(ex_hi_done, e * PIECES + j + 1)
                    nc.vector.scalar_tensor_tensor(out=ex_gu[e % 2][:, 1, j * PIECE:(j + 1) * PIECE],
                                                   in0=ex_raw[m % 2][:, k * PIECE:(k + 1) * PIECE], scalar=W_SCALE,
                                                   in1=ex_gu[e % 2][:, 0, j * PIECE:(j + 1) * PIECE],
                                                   op0=ALU.mult, op1=ALU.subtract).then_inc(ex_lo_done, 1)
                if q in turn_at:
                    e = turn_at[q]
                    dve.wait_ge(exT_ready, 2 * e + 2)
                    nc.vector.tensor_copy(exT[:, e % 2, KC:2 * KC, :], bank[7][:, :].bitcast(F16)[:, 0:KC * CAP].rearrange(
                        "p (k n) -> p k n", k=KC)).then_inc(exT_moved_dve, 1)
                job = next((n for n in range(len(JOBS)) if FIRST_CHUNK[n + 1] + LAG - 1 == q), None)
                if job is not None and JOBS[job][0] == "shared":
                    dve.wait_ge(down_done, FIRST_CHUNK[job + 1])
                    add_shared(JOBS[job][1])
                if q >= FIRST_CHUNK[-2] and q < NCH:
                    add_routed(q - FIRST_CHUNK[-2])
            dve.wait_ge(down_done, NCH)
            dve.wait_ge(routed_added, 2 * W)
            add_shared(JOBS[-1][1])

        @block.tensor
        def _(pe):
            pe.wait_ge(consts, 8)
            pe.wait_ge(ctx_loaded, 16)
            for n in range(KC * B):
                b, k = divmod(n, KC)
                if n >= 4:
                    pe.wait_ge(ctxT_moved, n - 3)
                for c in range(NI):
                    last = pe.transpose(bank[n % 4][:, c * P:(c + 1) * P],
                                        ctx_rows[:, b * NI + c, k * P:(k + 1) * P], ident[:, :])
                last.then_inc(ctxT_ready, 1)
            for n in range(KC * W // 4):
                q, k = divmod(n, KC)
                pe.wait_ge(ln1_done, 4 * q + 4)
                if n >= 4:
                    pe.wait_ge(lnT_moved, n - 3)
                for c in range(4):
                    last = pe.transpose(bank[4 + n % 4][:, c * P:(c + 1) * P],
                                        ln1[:, 4 * q + c, k * P:(k + 1) * P], ident[:, :])
                last.then_inc(lnT_ready, 1)
            pe.wait_ge(sq_done, KC * B)
            pe.wait_ge(ctxT_moved, KC * B)
            for k in range(KC):
                for b in range(B):
                    last = pe.matmul(bank[0][NJ * b:NJ * (b + 1), :], ones[:, :], ctx_sq[:, k, b * SEQ:(b + 1) * SEQ],
                                     start=(k == 0), stop=(k == KC - 1))
            last.then_inc(norm_ready, 1)
            pe.wait_ge(lnT_moved, KC * W // 4)
            for w in range(W):
                if w >= 3:
                    pe.wait_ge(prod_used, w - 2)
                for k in range(KC):
                    for b in range(B):
                        last = pe.matmul(bank[1 + w % 3][NJ * b:NJ * (b + 1), :], lnT[:, k, w, NJ * b:NJ * (b + 1)],
                                         ctxT[:, k, b * SEQ:(b + 1) * SEQ], start=(k == 0), stop=(k == KC - 1))
                last.then_inc(prod_ready, 1)
            pe.wait_ge(unskewed, 16 * NJ)
            for n in range(W // 2):
                if n >= 4:
                    pe.wait_ge((pathT_moved_dve, pathT_moved_act)[n % 2], (n - 4) // 2 + 1)
                if n < 4:
                    pe.wait_ge(prod_used, W)
                for c in range(2 * NI):
                    last = pe.transpose(bank[n % 4][:, :].bitcast(F16)[:, c * P:(c + 1) * P],
                                        path[:, 2 * n + c // NI, (c % NI) * P:(c % NI + 1) * P], ident16[:, :])
                last.then_inc(pathT_ready, 1)
            pe.wait_ge(ctx_lo_done, B)
            pe.wait_ge(ctx_hi_done, B)
            pe.wait_ge(lnT_moved, KC * W // 4)
            for n in range(W // 2):
                pe.wait_ge((pathT_moved_dve, pathT_moved_act)[n % 2], n // 2 + 1)
                if n >= 4:
                    pe.wait_ge(x2_done, n - 3)
                for c in range(2):
                    for z in range(2):
                        for i in range(NI):
                            for b in range(B):
                                last = pe.matmul(bank[4 + n % 4][NJ * b:NJ * (b + 1), c * H:(c + 1) * H],
                                                 pathT[:, 2 * n + c, i, NJ * b:NJ * (b + 1)],
                                                 ctx16[:, z, b * NI + i, :],
                                                 start=(z == 0 and i == 0), stop=(z == 1 and i == NI - 1))
                last.then_inc(aligned_ready, 1)

            for g in range(NG):
                pe.wait_ge(y_hi_done, g + 1)
                pe.wait_ge(y_lo_done, g + 1)
                pe.wait_ge(x2_done, W // 2)
                for z in range(2):
                    if g:
                        pe.wait_ge((yT_moved_act, yT_moved_dve)[z], g)
                    for k in range(KC):
                        for c in range(WG):
                            last = pe.transpose(bank[6 + z][:, :].bitcast(F16)[:, (k * WG + c) * P:(k * WG + c + 1) * P],
                                                y16[:, g * WG + c, z, k * P:(k + 1) * P], ident16[:, :])
                    last.then_inc(yT_ready, 1)
            pe.wait_ge(yT_moved_act, NG)
            pe.wait_ge(yT_moved_dve, NG)
            pe.wait_ge(rw_lo_done, 1)
            pairs = ((0, 0), (0, 1), (1, 0))
            for w in range(W):
                g, c = divmod(w, WG)
                for n, (k, (zy, zw)) in enumerate((k, p) for k in range(KC) for p in pairs):
                    last = pe.matmul(bank[0][:, w * E:(w + 1) * E], yT[:, g, zy, k, c * P:(c + 1) * P], rw16[:, zw, k, :],
                                     start=(n == 0), stop=(n == 3 * KC - 1))
            last.then_inc(logits_ready, 1)
            pe.wait_ge(totals_done, 1)
            pe.matmul(bank[1][:, 0:E], earlier[:, :], lane_total[:, 0, :], start=True, stop=True).then_inc(base_ready, 1)

            def gate_and_up(q):
                n, kind, i, c = CHUNKS[q]
                cols = GT if kind == "shared" else CAP
                for m in range(2):
                    for k in range(KC):
                        for zw, zy in pairs:
                            if kind == "shared":
                                weights = gu16[:, m, zw, k, c * P:(c + 1) * P]
                                moving = yT[:, i, zy, k, :]
                            else:
                                o = (m * KC + k) * IR + c * P
                                weights = ex_gu[i % 2][:, zw, o:o + P]
                                moving = exT[:, i % 2, zy * KC + k, :]
                            first = k == 0 and (zw, zy) == pairs[0]
                            final = k == KC - 1 and (zw, zy) == pairs[-1]
                            last = pe.matmul(bank[2 * m + q % 2][:, 0:cols], weights, moving, start=first, stop=final)
                last.then_inc(gu_ready, 1)

            def down(q):
                n, kind, i, c = CHUNKS[q]
                tiles = [(m * P, P) for m in range(WG)] if kind == "shared" else TILES_E
                for t, (m, rows) in enumerate(tiles):
                    for za, zw in pairs:
                        weights = down16[:, zw, c, :] if kind == "shared" else \
                            ex_gu[i % 2][:, zw, 2 * KC * IR + c * H:2 * KC * IR + (c + 1) * H]
                        last = pe.matmul(bank[4 + t // 2][0:rows, (t % 2) * H:(t % 2 + 1) * H],
                                         act16[:, q % 4, za, m:m + rows], weights,
                                         start=(c == 0 and t % 2 == 0 and (za, zw) == pairs[0]),
                                         stop=(q + 1 == FIRST_CHUNK[n + 1] and (za, zw) == pairs[-1]),
                                         skip_group_check=True)
                last.then_inc(down_done, 1)

            for q in range(NCH + LAG):
                if q < NCH:
                    n, kind, i, c = CHUNKS[q]
                    if kind == "shared" and q == 0:
                        pe.wait_ge(raw_lo_done, 3)
                        pe.wait_ge(base_ready, 1)
                    if kind == "expert" and c == 0:
                        pe.wait_ge(ex_lo_done, i * PIECES + 2 * PIECES // 3)
                        pe.wait_ge(exT_moved_act, i + 1)
                        pe.wait_ge(exT_moved_dve, i + 1)
                    if q >= 2:
                        pe.wait_ge(silu_done, q - 1)
                        pe.wait_ge(gated_done, q - 1)
                    elif q == 0:
                        pe.wait_ge(to_slot_done, 1)
                    gate_and_up(q)
                if q >= LAG:
                    r = q - LAG
                    n, kind, i, c = CHUNKS[r]
                    if kind == "expert" and c == 0:
                        pe.wait_ge(ex_lo_done, (i + 1) * PIECES)
                    if c == 0 and n:
                        if JOBS[n - 1][0] == "shared":
                            pe.wait_ge(shared_added, 2 * sum(k == "shared" for k, _ in JOBS[:n]))
                        else:
                            pe.wait_ge(ex_out_moved, 2 * (JOBS[n - 1][1] + 1))
                    pe.wait_ge(act_lo_done, r + 1)
                    down(r)
                if q in turn_at:
                    e = turn_at[q]
                    pe.wait_ge(ex_in_loaded, 32 * (e + 1))
                    for z in range(2):
                        if e:
                            pe.wait_ge((exT_moved_act, exT_moved_dve)[z], e)
                        for k in range(KC):
                            for t, (m, rows) in enumerate(TILES_E):
                                o = k * CAP + m
                                last = pe.transpose(bank[6 + z][:, :].bitcast(F16)[:, o:o + rows],
                                                    ex_in[0:rows, t, z, k * P:(k + 1) * P], ident16[0:rows, 0:rows])
                        last.then_inc(exT_ready, 1)


_INS = ["x", "ctx_1024", "g_xattn", "g_ffn", "L0_ffn_router_w", "L0_ffn_rg", "L0_ffn_ru", "L0_ffn_rd",
        "L0_ffn_sg", "L0_ffn_su", "L0_ffn_sd"]
_OUTS = [((4, 512, 256), "float32")]


def kernel(**inputs):
    import numpy as _np
    import concourse.bacc as _bacc
    from concourse import mybir as _mybir
    from concourse.bass_utils import run_bass_kernel_spmd as _run

    nc = _bacc.Bacc("TRN2", target_bir_lowering=False, num_devices=1)
    arrays, args = {}, []
    for name in _INS:
        a = _np.ascontiguousarray(inputs[name])
        arrays[f"in_{name}_dram"] = a
        args.append(nc.dram_tensor(f"in_{name}_dram", a.shape, _mybir.dt.from_np(a.dtype), kind="ExternalInput").ap())
    for i, (shape, dtype) in enumerate(_OUTS):
        dt = _mybir.dt.from_np(_np.dtype(dtype))
        args.append(nc.dram_tensor(f"out_{i}_dram", shape, dt, kind="ExternalOutput").ap())
    flamingo_dtw_moe(nc, *args)
    r = _run(nc, [arrays], core_ids=[0])
    return r.results[0]["out_0_dram"]
```

```python
from contextlib import ExitStack

import concourse.bass as bass
from concourse import mybir

ALU = mybir.AluOpType
ACT = mybir.ActivationFunctionType
F32 = mybir.dt.float32
F16 = mybir.dt.float16
I32 = mybir.dt.int32
AX_X = mybir.AxisListType.X

P = 128
BIG = 1e30
LN_EPS = 1e-5
RMS_EPS = 1.1920928955078125e-07
CAPACITY_FACTOR = 1.25

Y_SCALE = 64.0
W_SCALE = 256.0
A_SCALE = 16.0
LAG = 2
WARM_UP = 32


def flamingo_dtw_moe(nc, x, folded, g_xattn, g_ffn, router_w, rg, ru, rd, sg, su, sd, out, stop=None):
    B, SEQ, H = x.shape
    E, _, IR = rg.shape
    IS = sg.shape[1]
    T = B * SEQ
    W = T // P
    NJ = P // B
    KC = H // P
    NI = SEQ // P
    HALF = SEQ // 2
    NP = NJ // 2
    BW = SEQ // NP
    CW = BW + 1
    SKEW = 2
    S = HALF + SKEW * (NP - 1)
    ROWS = [32, 32, 64, 64, 64]
    RC = max(ROWS)
    NC = len(ROWS)
    ROW_0 = [sum(ROWS[:m]) for m in range(NC)]
    PER_BANK = [P * 2 // n for n in ROWS]
    PARTS = [(m, q) for m in range(NC) for q in range(BW // PER_BANK[m])]
    PARTS_TO = [sum(m <= c for m, _ in PARTS) for c in range(NC)]
    WQ = 4
    NW = BW // WQ
    CAP = int(CAPACITY_FACTOR * T / E)
    NG = 4
    WG = W // NG
    GT = WG * P
    NO_SLOT = 4 * E * CAP
    IC, IC_E = IS // P, IR // P
    TILES_E = [(m, min(P, CAP - m)) for m in range(0, CAP, P)]
    ORDER = [1, 2, 0, 3]
    JOBS = [("shared", g) for g in ORDER[:2]] + [("expert", e) for e in range(E)] + [("shared", g) for g in ORDER[2:]]
    CHUNKS = [(n, kind, i, c) for n, (kind, i) in enumerate(JOBS) for c in range(IC if kind == "shared" else IC_E)]
    NCH = len(CHUNKS)
    FIRST_CHUNK = [next(q for q, ch in enumerate(CHUNKS) if ch[0] == n) for n in range(len(JOBS))] + [NCH]
    PIECE = 1024
    PIECES = 3 * KC * IR // PIECE
    split_at = {}
    for e in range(E):
        base = FIRST_CHUNK[e + 1] + 2 if e else FIRST_CHUNK[0] + 14
        for j in range(PIECES):
            split_at.setdefault(base + j, []).append((e, j))
    turn_at = {FIRST_CHUNK[e + 2] - (3 if e else 2): e for e in range(E)}
    LATE_TURN = 2
    ROUTER_FROM = 4
    BASE_AT = ROUTER_FROM + 5
    router_stages = {ROUTER_FROM: (0,), ROUTER_FROM + 1: (1,), ROUTER_FROM + 2: (2,), ROUTER_FROM + 3: (3, 4),
                     BASE_AT: (5,), BASE_AT + 1: (6, 7), BASE_AT + 2: (8,)}
    OUT_SCALE = 1.0 / (A_SCALE * W_SCALE)
    assert NJ == 32 and H == 2 * P and SEQ == 4 * P and W == 16

    with ExitStack() as stack:
        def sb(name, shape, dt=F32):
            return stack.enter_context(nc.sbuf_tensor(name, shape, dt))

        def sem(name):
            return stack.enter_context(nc.semaphore(name))

        bank = [stack.enter_context(nc.psum_tensor(f"bank{i}", [P, 512], F32)) for i in range(8)]

        X = sb("x_rows", [P, W, H])
        region_a = sb("region_a", [P, 3 * KC * T])
        region_c = sb("region_c", [P, W * H])
        region_d = sb("region_d", [P, BW * (S + 2) // 2])
        region_e = sb("region_e", [P, (S + 2) * CW])
        region_f = sb("region_f", [P, (S + 1) * CW])

        ctxT = region_a[:, 0:KC * T].rearrange("p (k n) -> p k n", k=KC)
        lnT = region_a[:, KC * T:3 * KC * T].rearrange("p (k w b l) -> p k w b l", k=KC, w=BW, b=B)
        ctx_rows = region_c[:, :].rearrange("p (n h) -> p n h", h=H)
        ln1 = region_e[:, 0:W * H].rearrange("p (w h) -> p w h", h=H)
        spread = region_e[:, W * H:W * H + 4 * P].rearrange("p (d f l) -> p d f l", d=2, f=2)
        ctx_sq = region_f[:, 0:KC * T].rearrange("p (k n) -> p k n", k=KC)
        dist = region_d[:, 0:2 * RC * CW].rearrange("p (m i c) -> p m i c", m=2, c=CW)
        table = region_e[:, :].rearrange("p (s c) -> p s c", c=CW)
        cost = region_f[:, :].rearrange("p (s c) -> p s c", c=CW)
        halves = BW * S // 2
        is_left = region_d[:, 0:halves].bitcast(F16).rearrange("p (w s) -> p w s", w=BW)
        no_up = region_e[:, 0:halves].bitcast(F16).rearrange("p (w s) -> p w s", w=BW)
        leave = region_f[:, 0:halves].bitcast(F16).rearrange("p (w s) -> p w s", w=BW)
        leave_b = region_f[:, halves:2 * halves].bitcast(F16).rearrange("p (w s) -> p w s", w=BW)
        path = region_e[:, halves:halves + BW * HALF // 2].bitcast(F16).rearrange("p (w i) -> p w i", w=BW)
        pathT = region_d[:, 0:W * SEQ // 2].bitcast(F16).rearrange("p (n w b j) -> p n w b j", n=NI, w=W, b=B)
        ctx16 = region_f[:, halves:halves + W * H].bitcast(F16).rearrange("p (z n h) -> p z n h", z=2, h=H)

        gu16 = region_a[:, 0:2 * KC * IS].bitcast(F16).rearrange("p (m z k i) -> p m z k i", m=2, z=2, k=KC)
        down16 = region_a[:, 2 * KC * IS:3 * KC * IS].bitcast(F16).rearrange("p (z i h) -> p z i h", z=2, h=H)
        yn = region_e[:, 0:W * H].rearrange("p (w h) -> p w h", h=H)
        y16 = region_f[:, 0:W * H].bitcast(F16).rearrange("p (w z h) -> p w z h", w=W, z=2)
        yT = region_c[:, :].bitcast(F16).rearrange("p (g z k n) -> p g z k n", g=NG, z=2, k=KC)
        ew = 3 * KC * IR
        ex_gu = [r[:, 0:ew].bitcast(F16).rearrange("p (z n) -> p z n", z=2) for r in (region_e, region_f)]
        ex_raw = [r[:, ew:ew + KC * IR] for r in (region_e, region_f)]
        gated = [r[:, ew + KC * IR:ew + KC * IR + 512] for r in (region_e, region_f)]
        act32 = [r[:, ew + KC * IR + 512:ew + KC * IR + 1024] for r in (region_e, region_f)]
        act16 = region_d[:, 0:2048].bitcast(F16).rearrange("p (r z n) -> p r z n", r=4, z=2)
        ex_out = region_d[:, 2048:2048 + 2 * 768].rearrange("p (r m h) -> p r m h", r=2, h=H)
        ex_in = region_d[:, 3584:3584 + 768].bitcast(F16).rearrange("p (m z h) -> p m z h", m=3, z=2)
        gathered_rows = region_e[:, 0:2 * W * H].rearrange("p (w k h) -> p w k h", w=W, k=2)
        slots = nc.dram_tensor("slots", (E * CAP, 2 * H), F16).ap()
        ex_rows = nc.dram_tensor("ex_rows", (E * CAP, H), F32).ap()

        exT = sb("exT", [P, 2, 2 * KC, CAP], F16)
        rw = sb("rw", [P, KC, E])
        rw16 = sb("rw16", [P, 2, KC, E], F16)
        earlier = sb("earlier", [P, P])
        key_of = sb("key_of", [P, E, W])
        slot_of = sb("slot_of", [P, E, W])
        goes_on = sb("goes_on", [P, E, W])
        msq = sb("msq", [P, 3, W])
        rms_eps = sb("rms_eps", [P, 1])
        probs = sb("probs", [P, E, W])
        keys = sb("keys", [P, E, W])
        hot = sb("hot", [P, 2, E, W])
        chosen = sb("chosen", [P, E, W])
        upto = sb("upto", [P, E, W])
        fits = sb("fits", [P, E, W])
        lane_total = sb("lane_total", [P, 2, E])
        per_tok = sb("per_tok", [P, 12, W])
        to_slot = sb("to_slot", [P, 2, W], I32)
        from_slot = sb("from_slot", [P, 2, W], I32)
        out_gate = sb("out_gate", [P, 1])
        ident = sb("ident", [P, P])
        ident16 = sb("ident16", [P, P], F16)
        same_batch = sb("same_batch", [P, P])
        ones = sb("ones", [P, NJ])
        iota = sb("iota", [P, S], F16)
        iota_less = sb("iota_less", [P, S], F16)
        ctx_norm = sb("ctx_norm", [P, HALF])
        raw = sb("raw", [P, 2, PIECE])
        picked = raw[:, 0, :].rearrange("p (r d n) -> p r d n", r=2, d=2)
        end_pick = raw[:, 1, 0:NP * BW].rearrange("p (s w) -> p s w", w=BW)
        ends = raw[:, 1, NP * BW:NP * BW + 8 * CW].rearrange("p (n w) -> p n w", w=CW)
        ln_norm = sb("ln_norm", [P, 2, W])
        lane_norm = sb("lane_norm", [P, BW])
        sq_dump = sb("sq_dump", [P, 2, H])
        bn = sb("bn", [P, W, 6])
        mv = sb("mv", [P, W, 2])
        rstd = sb("rstd", [P, 2, W])
        back = sb("back", [P, 2, S + 2], F16)
        pick = sb("pick", [P, 3, S], F16)
        reach = sb("reach", [P, 2, HALF], F16)
        entry = sb("entry", [P, 1])
        leave_at = sb("leave_at", [P, BW + 1])
        leave_row = sb("leave_row", [P, 2, BW + 1])
        left_of = sb("left_of", [P, 2])
        lane_of = sb("lane_of", [P, NJ])
        at_pos = sb("at_pos", [P, NP])
        lane_pos = sb("lane_pos", [P, 9])
        pos, shift, border, no_next, base_col, last_row, chain0, chain1, nat_col = (
            lane_pos[:, n:n + 1] for n in range(9))
        chain_col = sb("chain_col", [P, BW])
        meet = sb("meet", [P, 16])
        offers = sb("offers", [P, 4, NP])
        outside = sb("outside", [P, 3, BW])
        gates = sb("gates", [P, 2])
        tanhs = sb("tanhs", [P, 2])
        ln_eps = sb("ln_eps", [P, 1])

        x_loaded = sem("x_loaded")
        ctx_loaded = sem("ctx_loaded")
        small_loaded = sem("small_loaded")
        consts = sem("consts")
        bn_done = sem("bn_done")
        dve_step = sem("dve_step")
        act_step = sem("act_step")
        pool_step = sem("pool_step")
        ln1_done = sem("ln1_done")
        std_done = sem("std_done")
        lnT_ready = sem("lnT_ready")
        ctxT_ready = sem("ctxT_ready")
        tr_done = sem("tr_done")
        ctxT_moved = sem("ctxT_moved")
        sq_done = sem("sq_done")
        norm_ready = sem("norm_ready")
        dist_done = sem("dist_done")
        top_set = sem("top_set")
        min_done = sem("min_done")
        scan_done = sem("scan_done")
        shift_done = sem("shift_done")
        pathT_ready = sem("pathT_ready")
        pathT_moved = sem("pathT_moved")
        ctx_hi_done = sem("ctx_hi_done")
        ctx_lo_done = sem("ctx_lo_done")
        aligned_ready = sem("aligned_ready")
        x2_done = sem("x2_done")
        tanh_done = sem("tanh_done")
        stored = sem("stored")
        lnT_moved_act = sem("lnT_moved_act")
        lnT_moved_dve = sem("lnT_moved_dve")
        lanes_done = sem("lanes_done")
        spread_done = sem("spread_done")
        ln_norm_done = sem("ln_norm_done")
        ln_norm_turned = sem("ln_norm_turned")
        lane_norm_ready = sem("lane_norm_ready")
        lane_norm_done = sem("lane_norm_done")
        ctx_norm_done = sem("ctx_norm_done")
        border_set = sem("border_set")
        pads_set = sem("pads_set")
        prod_ready = sem("prod_ready")
        picked_done = sem("picked_done")
        summed = sem("summed")
        clamped = sem("clamped")
        skewed = [sem(f"skewed{m}") for m in range(NC)]
        raw_loaded = [sem(f"raw_loaded{i}") for i in range(2)]
        masks_done = sem("masks_done")
        offers_done = sem("offers_done")
        offers_ready = sem("offers_ready")
        overridden = sem("overridden")
        leave_parts = sem("leave_parts")
        leave_done = sem("leave_done")
        row_done = sem("row_done")
        reach_done = sem("reach_done")
        on_path_done = sem("on_path_done")
        raw_hi_done = sem("raw_hi_done")
        raw_scaled = sem("raw_scaled")
        raw_lo_done = sem("raw_lo_done")
        router_loaded = sem("router_loaded")
        zeros_set = sem("zeros_set")
        slots_zeroed = sem("slots_zeroed")
        bn2_done = sem("bn2_done")
        std2_done = sem("std2_done")
        yn_done = sem("yn_done")
        msq_done = sem("msq_done")
        rms_done = sem("rms_done")
        y_hi_done = sem("y_hi_done")
        y_lo_done = sem("y_lo_done")
        yT_ready = sem("yT_ready")
        yT_moved_act = sem("yT_moved_act")
        yT_moved_dve = sem("yT_moved_dve")
        rw_hi_done = sem("rw_hi_done")
        rw_lo_done = sem("rw_lo_done")
        logits_ready = sem("logits_ready")
        shifted = sem("shifted")
        exp_done = sem("exp_done")
        totals_done = sem("totals_done")
        base_ready = sem("base_ready")
        to_slot_done = sem("to_slot_done")
        scattered = sem("scattered")
        ex_raw_loaded = [sem(f"ex_raw_loaded{i}") for i in range(2)]
        ex_hi_done = sem("ex_hi_done")
        ex_lo_done = sem("ex_lo_done")
        ex_in_loaded = sem("ex_in_loaded")
        exT_ready = sem("exT_ready")
        exT_moved_act = sem("exT_moved_act")
        exT_moved_dve = sem("exT_moved_dve")
        gu_ready = sem("gu_ready")
        silu_done = sem("silu_done")
        gated_done = sem("gated_done")
        act_hi_done = sem("act_hi_done")
        act_lo_done = sem("act_lo_done")
        down_done = sem("down_done")
        ex_out_moved = sem("ex_out_moved")
        ex_stored = sem("ex_stored")
        shared_added = sem("shared_added")
        from_slot_done = sem("from_slot_done")
        gathered = [sem(f"gathered{g}") for g in range(NG)]
        routed_added = sem("routed_added")

        block = stack.enter_context(nc.Block())

        class Count:

            def __init__(self, semaphore):
                self.semaphore, self.n = semaphore, 0

            def link(self, eng, instruction):
                self.n += 1
                instruction.then_inc(self.semaphore, 1)
                eng.wait_ge(self.semaphore, self.n)

            def mark(self, instruction):
                self.n += 1
                instruction.then_inc(self.semaphore, 1)
                return self.n

        def store_expert(sp, e):
            full = sum(n == P for _, n in TILES_E)
            r = e * CAP
            sp.wait_ge(ex_out_moved, 2 * (e + 1))
            sp.dma_start(ex_rows[r:r + full * P, :].rearrange("(m p) h -> p m h", p=P),
                         ex_out[:, e % 2, 0:full, :]).then_inc(ex_stored, 16)
            for m, n in TILES_E[full:]:
                sp.dma_start(ex_rows[r + m:r + m + n, :], ex_out[0:n, e % 2, m // P, :]).then_inc(ex_stored, 16)

        def raw_piece(n):
            m, r = divmod(n, 4)
            if m == 2:
                return sd[4 * r * P:4 * (r + 1) * P, :].rearrange("(i p) h -> p i h", p=P)
            k, half = divmod(r, 2)
            return (sg, su)[m][k * P:(k + 1) * P, half * PIECE:(half + 1) * PIECE]

        def split_piece(n, z):
            m, r = divmod(n, 4)
            if m == 2:
                return down16[:, z, 4 * r:4 * (r + 1), :].rearrange("p i h -> p (i h)")
            k, half = divmod(r, 2)
            return gu16[:, m, z, k, half * PIECE:(half + 1) * PIECE]

        def group_of_bank(n):
            g, c = divmod(n, 2)
            return NW - 1 - g, c

        PAIRS = [g * WG // 2 + c for g in ORDER for c in range(WG // 2)]
        GROUPS_FOR = [NW - 1] * (W // 4) + [NW] * (W // 4)

        def half(t, h):
            return t.rearrange("p (g w) -> p g w", g=NG)[:, slice(1, 3) if h == 0 else slice(0, NG, NG - 1), :]

        @block.sync
        def _(sp):
            sp.dma_start(X[:, :, :], x.rearrange("b (l w) h -> (b l) w h", w=W)).then_inc(x_loaded, 16)
            sp.dma_start(ctx_rows, folded.rearrange("b d (c p) h -> p (b d c) h", p=P)).then_inc(ctx_loaded, 16)
            for n, g in enumerate((g_xattn, g_ffn)):
                sp.dma_start(gates[:, n:n + 1], g.partition_broadcast(P)).then_inc(small_loaded, 16)
            for k in range(KC):
                sp.dma_start(rw[:, k, :], router_w[:, k * P:(k + 1) * P].rearrange("e p -> p e"),
                             allow_slow_non_contiguous=True).then_inc(router_loaded, 16)
            for m in range(NC):
                sp.wait_ge(dist_done, PARTS_TO[m])
                if m == 0:
                    sp.wait_ge(pads_set, 3)
                    sp.wait_ge(border_set, 1)
                for j in range(NP):
                    r = 2 + ROW_0[m] + SKEW * j
                    sp.dma_start(table[j:P:NP, r:r + ROWS[m], :], dist[j:P:NP, m % 2, 0:ROWS[m], :]).then_inc(skewed[m], 16)
            sp.wait_ge(dist_done, len(PARTS))
            for n in range(12):
                if n >= 2:
                    sp.wait_ge(raw_lo_done, n - 1)
                sp.dma_start(raw[:, n % 2, :] if n < 8 else raw[:, n % 2, :].rearrange("p (i h) -> p i h", h=H),
                             raw_piece(n)).then_inc(raw_loaded[n % 2], 16)
            sp.wait_ge(zeros_set, 1)
            for n in range(E * CAP // P):
                sp.dma_start(slots[n * P:(n + 1) * P, :], end_pick[:, :, :].rearrange(
                    "p s w -> p (s w)")[:, 0:H].bitcast(F16)).then_inc(slots_zeroed, 16)

            def load_expert(u):
                e, m = divmod(u, 3)
                src = (rg[e], ru[e], rd[e])[m].rearrange("(k p) i -> p k i", p=P)
                sp.dma_start(ex_raw[u % 2].rearrange("p (k i) -> p k i", k=src.shape[1]), src).then_inc(ex_raw_loaded[u % 2], 16)

            sp.wait_ge(pathT_ready, 2 * NW)
            load_expert(0)
            sp.wait_ge(x2_done, W // 2)
            load_expert(1)
            tiles_full = sum(n == P for _, n in TILES_E)
            sp.wait_ge(ex_lo_done, KC)
            load_expert(2)
            sp.wait_ge(scattered, 16 * 2 * W)
            for e in range(E):
                if e:
                    sp.wait_ge(exT_ready, 2 * e)
                r = e * CAP
                sp.dma_start(ex_in[:, 0:tiles_full, :, :], slots[r:r + tiles_full * P, :].rearrange(
                    "(m p) (z h) -> p m z h", p=P, z=2)).then_inc(ex_in_loaded, 16)
                for m, n in TILES_E[tiles_full:]:
                    sp.dma_start(ex_in[0:n, m // P, :, :], slots[r + m:r + m + n, :].rearrange(
                        "p (z h) -> p z h", z=2)).then_inc(ex_in_loaded, 16)
                for u in range(max(3 * e + 2, 3), min(3 * e + 5, 3 * E)):
                    sp.wait_ge(ex_lo_done, (u - 1) * KC)
                    load_expert(u)
                if e:
                    store_expert(sp, e - 1)
            store_expert(sp, E - 1)
            outs = out.rearrange("b (l w) h -> (b l) w h", w=W)
            for k, g in enumerate(ORDER):
                sp.wait_ge(shared_added, 2 * (k + 1))
                sp.wait_ge(routed_added, 2 * WG * (k + 1))
                sp.dma_start(outs[:, g * WG:(g + 1) * WG, :], X[:, g * WG:(g + 1) * WG, :]).then_inc(stored, 16)
            sp.wait_ge(stored, 16 * NG)

        @block.gpsimd
        def _(pool):
            pool.memset(ident[:, :], 0.0).then_inc(consts, 1)
            pool.memset(ident16[:, :], 0.0).then_inc(consts, 1)
            pool.memset(ones[:, :], 1.0).then_inc(consts, 1)
            pool.memset(ln_eps[:, :], LN_EPS).then_inc(consts, 1)
            pool.memset(same_batch[:, :], 0.0).then_inc(consts, 1)
            pool.iota(iota[:, :], [[1, S]], base=0, channel_multiplier=0,
                      allow_small_or_imprecise_dtypes=True).then_inc(consts, 1)
            pool.wait_ge(consts, 6)
            pool.tensor_scalar(iota_less[:, :], iota[:, :], 0.5, None, ALU.subtract).then_inc(consts, 1)
            for m in (ident, ident16):
                pool.affine_select(out=m[:, :], in_=m[:, :], compare_op=ALU.not_equal, fill=1.0,
                                   base=0, pattern=[[-1, P]], channel_multiplier=1).then_inc(consts, 1)
            for b in range(B):
                pool.wait_ge(consts, 9 + b)
                pool.memset(same_batch[NJ * b:NJ * (b + 1), NJ * b:NJ * (b + 1)], 1.0).then_inc(consts, 1)
            pool.wait_ge(consts, 13)
            for n in range(KC * B):
                b, k = divmod(n, KC)
                s = slice(b * SEQ, (b + 1) * SEQ)
                pool.wait_ge(ctxT_moved, n + 1)
                pool.tensor_tensor(ctx_sq[:, k, s], ctxT[:, k, s], ctxT[:, k, s], ALU.mult).then_inc(sq_done, 1)
            pool.wait_ge(lnT_ready, KC * W // 4)
            pool.wait_ge(ln_norm_done, W)
            pool.wait_ge(lane_norm_ready, 1)
            pool.memset(region_e[:, 0:(SKEW * (NP - 1) + 2) * CW], 0.0).then_inc(pads_set, 1)
            pool.memset(region_e[:, (HALF + 2) * CW:(S + 2) * CW], 0.0).then_inc(pads_set, 1)
            pool.wait_ge(pads_set, 2)
            pool.memset(table[:, 0, 0:1], BIG).then_inc(pads_set, 1)
            pool.wait_ge(norm_ready, 1)
            pool.memset(cost[:, 0, 1:CW], BIG).then_inc(top_set, 1)
            pool.wait_ge(lane_norm_done, 1)
            pool.wait_ge(ctx_norm_done, 2)
            n_sum = 0
            for n, (m, q) in enumerate(PARTS):
                V, R = PER_BANK[m], ROWS[m]
                both = picked[:, n % 2, :, :]
                total = both[:, 0, :].rearrange("p (w i) -> p w i", w=V)
                pool.wait_ge(picked_done, 2 * (n + 1))
                for part in (both[:, 1, :].rearrange("p (w i) -> p w i", w=V),
                             lane_norm[:, V * q:V * (q + 1)].unsqueeze(2).broadcast_to((P, V, R)),
                             ctx_norm[:, ROW_0[m]:ROW_0[m] + R].unsqueeze(1).broadcast_to((P, V, R))):
                    if n_sum % 3:
                        pool.wait_ge(summed, n_sum)
                    pool.tensor_tensor(total, total, part, ALU.add).then_inc(summed, 1)
                    n_sum += 1
            for n in range(12):
                pool.wait_ge(raw_scaled, n + 1)
                pool.tensor_tensor(split_piece(n, 1), raw[:, n % 2, :], split_piece(n, 0), ALU.subtract).then_inc(raw_lo_done, 1)
            pool.memset(earlier[:, :], 1.0).then_inc(consts, 1)
            pool.memset(rms_eps[:, :], RMS_EPS).then_inc(consts, 1)
            pool.memset(goes_on[:, :, :], 1.0).then_inc(consts, 1)
            pool.iota(key_of[:, :, :], [[-1, E], [0, W]], base=E, channel_multiplier=0,
                      allow_small_or_imprecise_dtypes=True).then_inc(consts, 1)
            pool.iota(slot_of[:, :, :], [[CAP, E], [0, W]], base=0, channel_multiplier=0,
                      allow_small_or_imprecise_dtypes=True).then_inc(consts, 1)
            pool.wait_ge(consts, 18)
            pool.memset(goes_on[:, :, 0:1], 0.0).then_inc(consts, 1)
            pool.affine_select(out=earlier[:, :], in_=earlier[:, :], compare_op=ALU.is_gt, fill=0.0,
                               base=0, pattern=[[1, P]], channel_multiplier=-1).then_inc(consts, 1)
            pool.wait_ge(masks_done, 2)
            pool.wait_ge(overridden, 2)
            for w in range(BW):
                pool.tensor_tensor(leave[:, w, :], is_left[:, w, :], iota[:, :], ALU.mult).then_inc(leave_parts, 1)
                pool.tensor_tensor(leave_b[:, w, :], no_up[:, w, :], iota_less[:, :], ALU.mult).then_inc(leave_parts, 1)
            pool.wait_ge(offers_done, 1)
            pool.memset(end_pick[:, :, :], 0.0).then_inc(zeros_set, 1)
            for b in range(B):
                pool.wait_ge(ctx_hi_done, b + 1)
                s = slice(b * NI, (b + 1) * NI)
                pool.tensor_tensor(ctx16[:, 1, s, :], ctx_rows[:, s, :], ctx16[:, 0, s, :],
                                   ALU.subtract).then_inc(ctx_lo_done, 1)
            pool.wait_ge(slots_zeroed, 16 * (E * CAP // P))
            pool.wait_ge(y_lo_done, NG)
            pool.wait_ge(y_hi_done, NG)
            pool.wait_ge(to_slot_done, 1)
            for w in range(W):
                for k in range(2):
                    pool.indirect_dma_start(slots, bass.IndirectOffsetOnAxis(ap=to_slot[:, k, w:w + 1], axis=0),
                                            y16[:, w, :, :].rearrange("p z h -> p (z h)"), None,
                                            bounds_check=E * CAP - 1, oob_is_err=False).then_inc(scattered, 16)
            pool.wait_ge(from_slot_done, 1)
            pool.wait_ge(ex_stored, 16 * E * 2)
            pool.wait_ge(down_done, FIRST_CHUNK[E + 2])
            pool.wait_ge(ex_lo_done, E * PIECES)
            for w in (g * WG + c for g in ORDER for c in range(WG)):
                for k in range(2):
                    pool.indirect_dma_start(gathered_rows[:, w, k, :], None, ex_rows,
                                            bass.IndirectOffsetOnAxis(ap=from_slot[:, k, w:w + 1], axis=0),
                                            bounds_check=E * CAP - 1, oob_is_err=False).then_inc(gathered[w // WG], 16)

        @block.scalar
        def _(act):
            def move_yT(n):
                act.wait_ge(yT_ready, 2 * n + 1)
                act.activation(yT[:, ORDER[n], 0, :, :], bank[6][:, :].bitcast(F16).rearrange("p (k n) -> p k n", k=KC),
                               ACT.Copy).then_inc(yT_moved_act, 1)

            def move_pathT(g):
                for n in (2 * g, 2 * g + 1):
                    q, c = group_of_bank(n)
                    f, v = divmod(WQ * q, W)
                    src = bank[n % 4][:, :].bitcast(F16)[:, 0:WQ * P].rearrange("p (w b l) -> p w b l", w=WQ, b=B)
                    act.wait_ge(pathT_ready, n + 1)
                    act.activation(pathT[:, c, v:v + WQ, :, f:NJ:2], src[:, :, :, 0:NP], ACT.Copy).then_inc(pathT_moved, 1)
                    act.activation(pathT[:, 2 + c, W - WQ - v:W - v, :, 1 - f:NJ:2], src[:, ::-1, :, NJ - 1:NP - 1:-1],
                                   ACT.Copy).then_inc(pathT_moved, 1)

            def move_ctxT(n):
                b, k = divmod(n, KC)
                act.wait_ge(ctxT_ready, n + 1)
                act.activation(ctxT[:, k, b * SEQ:(b + 1) * SEQ], bank[n % 4][:, :], ACT.Copy).then_inc(ctxT_moved, 1)

            act.wait_ge(consts, 4)
            act.wait_ge(bn_done, 1)
            act.activation(rstd[:, 0, :], mv[:, :, 1], ACT.Sqrt, bias=ln_eps[:, 0:1]).then_inc(std_done, 1)
            for n in range(KC * B):
                move_ctxT(n)
            for n in range(KC * W // 4):
                q, k = divmod(n, KC)
                act.wait_ge(lnT_ready, n + 1)
                for f in range(2):
                    w = W * f + 4 * q
                    act.activation(lnT[:, k, w:w + 4, :, 0:NP],
                                   bank[4 + n % 4][:, :].rearrange("p (w b j f) -> p f w b j", w=4, b=B, f=2)[:, f],
                                   ACT.Copy, scale=-2.0).then_inc(lnT_moved_act, 1)
            act.wait_ge(ln1_done, W)
            for w in range(W):
                if w >= 2:
                    act.wait_ge(ln_norm_done, w - 1)
                act.activation(sq_dump[:, w % 2, :], ln1[:, w, :], ACT.Square,
                               accum_out=ln_norm[:, 0, w:w + 1]).then_inc(ln_norm_done, 1)
            act.wait_ge(lanes_done, 1)
            for n in range(len(PARTS) + 1):
                if n < len(PARTS):
                    V = PER_BANK[PARTS[n][0]]
                    act.wait_ge(prod_ready, n + 1)
                    if n >= 2:
                        act.wait_ge(clamped, n - 1)
                        act.wait_ge(dist_done, n - 1)
                    for d, mine in enumerate((chain0, chain1)):
                        act.activation(picked[:, n % 2, d, :].rearrange("p (w i) -> p w i", w=V),
                                       bank[1 + n % 3][:, :].rearrange("p (w d i) -> p d w i", w=V, d=2)[:, d],
                                       ACT.Copy, scale=mine).then_inc(picked_done, 1)
                if n:
                    r = n - 1
                    m, q = PARTS[r]
                    V = PER_BANK[m]
                    act.wait_ge(summed, 3 * n)
                    act.activation(picked[:, r % 2, 0, :], picked[:, r % 2, 0, :], ACT.Relu).then_inc(clamped, 1)
                    act.wait_ge(clamped, n)
                    if q == 0 and m >= 2:
                        act.wait_ge(skewed[m - 2], 16 * NP)
                    act.activation(dist[:, m % 2, 0:ROWS[m], 1 + V * q:1 + V * (q + 1)].rearrange("p i w -> p w i"),
                                   picked[:, r % 2, 0, :].rearrange("p (w i) -> p w i", w=V), ACT.Sqrt).then_inc(dist_done, 1)
            for n in range(12):
                act.wait_ge(raw_loaded[n % 2], 16 * (n // 2 + 1))
                act.activation(split_piece(n, 0), raw[:, n % 2, :], ACT.Copy, scale=W_SCALE).then_inc(raw_hi_done, 1)
                act.activation(raw[:, n % 2, :], raw[:, n % 2, :], ACT.Copy, scale=W_SCALE).then_inc(raw_scaled, 1)
            act.wait_ge(router_loaded, 16 * KC)
            act.activation(rw16[:, 0, :, :], rw[:, :, :], ACT.Copy, scale=W_SCALE).then_inc(rw_hi_done, 1)
            act.wait_ge(small_loaded, 32)
            act.activation(tanhs[:, :], gates[:, :], ACT.Tanh).then_inc(tanh_done, 1)
            act.wait_ge(leave_done, 1)
            for b in range(B):
                s = slice(b * NI, (b + 1) * NI)
                act.activation(ctx16[:, 0, s, :], ctx_rows[:, s, :], ACT.Copy).then_inc(ctx_hi_done, 1)
            for n, w in enumerate(reversed(range(BW))):
                act.wait_ge(row_done, 2 * (n + 1))
                if n >= 2:
                    act.wait_ge(on_path_done, n - 1)
                if n:
                    act.wait_ge(reach_done, 2 * n)
                act.activation(pick[:, 2, 0:HALF], iota[:, 0:HALF], ACT.Relu, scale=2.0,
                               bias=leave_row[:, 1, w + 1:w + 2]).then_inc(reach_done, 1)
                act.wait_ge(reach_done, 2 * n + 1)
                act.activation(reach[:, n % 2, :], pick[:, 2, 0:HALF], ACT.Relu, scale=outside[:, 2, w:w + 1],
                               bias=outside[:, 1, w:w + 1]).then_inc(reach_done, 1)
                if n > WQ and n % WQ == 2:
                    move_pathT(n // WQ - 1)
            move_pathT(NW - 1)

            for h in range(2):
                if h:
                    for n in range(2):
                        move_yT(n)
                act.wait_ge(bn2_done, h + 1)
                act.activation(half(rstd[:, 0, :], h), half(mv[:, :, 1], h), ACT.Sqrt, bias=ln_eps[:, 0:1]).then_inc(std2_done, 1)
                for n in (2 * h, 2 * h + 1):
                    s = slice(ORDER[n] * WG, (ORDER[n] + 1) * WG)
                    act.wait_ge(yn_done, (n + 1) * WG)
                    act.activation(y16[:, s, 0, :], yn[:, s, :], ACT.Copy).then_inc(y_hi_done, 1)
            act.wait_ge(msq_done, 1)
            act.activation(msq[:, 1, :], msq[:, 0, :], ACT.Sqrt, scale=1.0 / Y_SCALE ** 2, bias=rms_eps[:, 0:1]).then_inc(rms_done, 1)

            for q in range(NCH + 1):
                if q < NCH:
                    n, kind, i, c = CHUNKS[q]
                    cols = GT if kind == "shared" else CAP
                    act.wait_ge(gu_ready, q + 1)
                    if q >= 2:
                        act.wait_ge(gated_done, q - 1)
                    act.activation(gated[q % 2][:, 0:cols], bank[q % 2][:, 0:cols], ACT.Silu,
                                   scale=1.0 / (Y_SCALE * W_SCALE)).then_inc(silu_done, 1)
                if q >= 1:
                    r = q - 1
                    cols = GT if CHUNKS[r][1] == "shared" else CAP
                    act.wait_ge(gated_done, q)
                    if r >= 4:
                        act.wait_ge(down_done, r - 3)
                    act.activation(act16[:, r % 4, 0, 0:cols], act32[r % 2][:, 0:cols], ACT.Copy).then_inc(act_hi_done, 1)
                if q == LATE_TURN:
                    for n in range(2, NG):
                        move_yT(n)
                if q == ROUTER_FROM:
                    act.wait_ge(shifted, 1)
                    act.activation(probs[:, :, :], probs[:, :, :], ACT.Exp).then_inc(exp_done, 1)
                for e, j in split_at.get(q, ()):
                    u, k = divmod(j, KC)
                    m = 3 * e + u
                    act.wait_ge(ex_raw_loaded[m % 2], 16 * (m // 2 + 1))
                    if e >= 2:
                        act.wait_ge(down_done, FIRST_CHUNK[e + 1])
                    if e == 1:
                        act.wait_ge(scattered, 16 * 2 * W)
                    act.activation(ex_gu[e % 2][:, 0, j * PIECE:(j + 1) * PIECE],
                                   ex_raw[m % 2][:, k * PIECE:(k + 1) * PIECE], ACT.Copy,
                                   scale=W_SCALE).then_inc(ex_hi_done, 1)
                if q in turn_at:
                    e = turn_at[q]
                    act.wait_ge(exT_ready, 2 * e + 1)
                    act.activation(exT[:, e % 2, 0:KC, :], bank[6][:, :].bitcast(F16)[:, 0:KC * CAP].rearrange(
                        "p (k n) -> p k n", k=KC), ACT.Copy).then_inc(exT_moved_act, 1)
                job = next((n for n in range(len(JOBS)) if FIRST_CHUNK[n + 1] + LAG - 1 == q), None)
                if job is not None and JOBS[job][0] == "expert":
                    e = JOBS[job][1]
                    act.wait_ge(down_done, FIRST_CHUNK[job + 1])
                    if e >= 2:
                        act.wait_ge(ex_stored, 32 * (e - 1))
                    act.activation(ex_out[:, e % 2, 0:2, :], bank[4][:, :].rearrange("p (m h) -> p m h", m=2),
                                   ACT.Copy).then_inc(ex_out_moved, 1)
                    act.activation(ex_out[0:64, e % 2, 2, :], bank[5][0:64, 0:H], ACT.Copy).then_inc(ex_out_moved, 1)

        @block.vector
        def _(dve):
            step = Count(dve_step)

            def link(instruction):
                step.link(dve, instruction)

            dve.wait_ge(consts, 13)
            link(nc.vector.tensor_reduce(lane_of[:, :], ident[:, :].rearrange("p (b l) -> p l b", b=B), AX_X, ALU.add))
            link(nc.vector.tensor_tensor(at_pos[:, :], lane_of[:, 0:NP], lane_of[:, NP:NJ], ALU.add))
            link(nc.vector.tensor_tensor(offers[:, 0, :], at_pos[:, :], iota[:, 0:NP], ALU.mult))
            link(nc.vector.tensor_reduce(pos, offers[:, 0, :], AX_X, ALU.add))
            for dst, src, a, b2 in ((shift, pos, float(SKEW), 0.0), (border, at_pos[:, 0:1], BIG, 0.0),
                                    (no_next, lane_of[:, NP - 1:NP], BIG, 0.0), (base_col, pos, float(BW), 0.0),
                                    (last_row, pos, float(SKEW), float(HALF - 1)),
                                    (nat_col, pos, float(BW), 0.0)):
                step.mark(nc.vector.tensor_scalar(dst, src, a, b2, ALU.mult, ALU.add))
            step.mark(nc.vector.tensor_reduce(chain0, lane_of[:, 0:NP], AX_X, ALU.add))
            step.mark(nc.vector.tensor_reduce(chain1, lane_of[:, NP:NJ], AX_X, ALU.add))
            dve.wait_ge(dve_step, step.n)
            nc.vector.tensor_scalar(chain_col[:, :], iota[:, 0:BW], base_col, None, ALU.add).then_inc(lanes_done, 1)
            nc.vector.tensor_scalar(dist[:, :, :, 0].rearrange("p m i -> p (m i)"), iota[:, 0:2 * RC], 0.0, border,
                                    ALU.is_ge, ALU.mult).then_inc(border_set, 1)
            dve.wait_ge(x_loaded, 16)
            for w in range(W):
                last = step.mark(nc.vector.bn_stats(bn[:, w, :], X[:, w, :]))
            dve.wait_ge(dve_step, last)
            for w in range(W - 1):
                last = step.mark(nc.vector.bn_aggr(mv[:, w, :], bn[:, w, :]))
            dve.wait_ge(dve_step, last)
            nc.vector.bn_aggr(mv[:, W - 1, :], bn[:, W - 1, :]).then_inc(bn_done, 1)
            dve.wait_ge(std_done, 1)
            link(nc.vector.reciprocal(rstd[:, 1, :], rstd[:, 0, :]))
            for w in range(W):
                nc.vector.tensor_scalar(ln1[:, w, :], X[:, w, :], mv[:, w, 0:1], rstd[:, 1, w:w + 1],
                                        ALU.subtract, ALU.mult).then_inc(ln1_done, 1)
            link(nc.vector.memset(spread, 0.0))
            for f in range(2):
                cols = ident[:, :].rearrange("p (b j) -> p b j", b=B)
                step.mark(nc.vector.tensor_copy(spread[:, 0, f, :].rearrange("p (b l) -> p b l", b=B)[:, :, 0:NP],
                                                cols[:, :, f:NJ:2]))
                nc.vector.tensor_copy(spread[:, 1, f, :].rearrange("p (b l) -> p b l", b=B)[:, :, NP:NJ],
                                      cols[:, :, NJ - 1 - f::-2]).then_inc(spread_done, 1)
            for n in range(KC * W // 4):
                q, k = divmod(n, KC)
                dve.wait_ge(lnT_moved_act, 2 * (n + 1))
                dve.wait_ge(lnT_ready, n + 1)
                for f in range(2):
                    w = W * f + W - 4 - 4 * q
                    src = bank[4 + n % 4][:, :].rearrange("p (w b j) -> p w b j", w=4, b=B)
                    nc.vector.tensor_scalar(lnT[:, k, w:w + 4, :, NP:NJ], src[:, ::-1, :, NJ - 1 - f::-2],
                                            -2.0, None, ALU.mult).then_inc(lnT_moved_dve, 1)
            dve.wait_ge(ln_norm_done, W)
            nc.vector.tensor_copy(ln_norm[:, 1, :], ln_norm[:, 0, ::-1]).then_inc(ln_norm_turned, 1)
            dve.wait_ge(norm_ready, 1)
            nc.vector.tensor_scalar(ctx_norm[:, :], bank[0][:, 0:HALF], chain0, None, ALU.mult).then_inc(ctx_norm_done, 1)
            dve.wait_ge(ctx_norm_done, 1)
            nc.vector.scalar_tensor_tensor(out=ctx_norm[:, :], in0=bank[0][:, HALF:SEQ], scalar=chain1,
                                           in1=ctx_norm[:, :], op0=ALU.mult, op1=ALU.add).then_inc(ctx_norm_done, 1)
            dve.wait_ge(lane_norm_ready, 1)
            nc.vector.tensor_copy(lane_norm[:, :], bank[4][:, 0:BW]).then_inc(lane_norm_done, 1)
            link(nc.vector.tensor_scalar(cost[:, 0, 0:1], border, -1.0, BIG, ALU.mult, ALU.add))
            dve.wait_ge(top_set, 1)
            to_next = [l - (l % NP > 0) for l in range(NJ)]
            for s in range(S):
                if s in ROW_0:
                    dve.wait_ge(skewed[ROW_0.index(s)], 16 * NP)
                if s:
                    dve.wait_ge(scan_done, s)
                nc.vector.tensor_tensor(table[:, s, 1:CW], cost[:, s, 1:CW], cost[:, s, 0:BW],
                                        ALU.min).then_inc(min_done, 1)
                dve.wait_ge(min_done, s + 1)
                if s:
                    dve.wait_ge(shift_done, s)
                nc.vector.tensor_tensor_scan(out=cost[:, s + 1, :], data0=table[:, s, :], data1=table[:, s + 2, :],
                                             initial=BIG, op0=ALU.min, op1=ALU.add).then_inc(scan_done, 1)
                nc.vector.stream_shuffle(table[:, s + 1, 0:1], cost[:, s, BW:CW], to_next).then_inc(shift_done, 1)
            dve.wait_ge(scan_done, S)
            dve.wait_ge(shift_done, S)
            dve.wait_ge(skewed[NC - 1], 16 * NP)
            at_left = cost[:, 1:S + 1, 0:BW].rearrange("p s w -> p w s")
            at_diag = cost[:, 0:S, 0:BW].rearrange("p s w -> p w s")
            at_up = cost[:, 0:S, 1:CW].rearrange("p s w -> p w s")
            least = table[:, 0:S, 1:CW].rearrange("p s w -> p w s")
            nc.vector.tensor_tensor(is_left, at_left, least, ALU.is_lt).then_inc(masks_done, 1)
            dve.wait_ge(raw_lo_done, 12)
            link(nc.vector.tensor_tensor(end_pick[:, :, :], cost[:, HALF:HALF + SKEW * (NP - 1) + 1:SKEW, 1:CW],
                                         at_pos[:, :].unsqueeze(2).broadcast_to((P, NP, BW)), ALU.mult))
            dve.wait_ge(masks_done, 1)
            nc.vector.tensor_tensor(no_up, at_up, at_diag, ALU.is_ge).then_inc(masks_done, 1)
            link(nc.vector.tensor_reduce(ends[:, 0, 0:BW], end_pick[:, :, :].rearrange("p s w -> p w s"), AX_X, ALU.add))
            beside = [NJ - 1 - l if l < NP else l for l in range(NJ)]
            beside_next = [NJ - 2 - l if l < NP - 1 else l for l in range(NJ)]
            link(nc.vector.stream_shuffle(ends[:, 1, 0:BW], ends[:, 0, 0:BW], beside))
            link(nc.vector.stream_shuffle(ends[:, 2, BW:CW], ends[:, 0, BW - 1:BW], beside_next))
            link(nc.vector.tensor_copy(ends[:, 2, 0:BW], ends[:, 1, BW - 1::-1]))
            link(nc.vector.tensor_scalar(ends[:, 2, BW:CW], ends[:, 2, BW:CW], no_next, None, ALU.add))
            link(nc.vector.tensor_tensor(ends[:, 3, 0:BW], ends[:, 2, 0:BW], ends[:, 2, 1:CW], ALU.min))
            link(nc.vector.tensor_tensor(ends[:, 3, 0:BW], ends[:, 3, 0:BW], ends[:, 0, 0:BW], ALU.add))
            link(nc.vector.tensor_tensor(ends[:, 4, 0:BW], ends[:, 2, 1:CW], ends[:, 2, 0:BW], ALU.is_le))
            link(nc.vector.tensor_reduce(meet[:, 0:1], ends[:, 3, 0:BW], AX_X, ALU.min))
            link(nc.vector.tensor_scalar(ends[:, 5, 0:BW], ends[:, 3, 0:BW], meet[:, 0:1], None, ALU.is_equal))
            link(nc.vector.tensor_tensor(ends[:, 5, 0:BW], ends[:, 5, 0:BW], iota[:, BW:0:-1], ALU.mult))
            link(nc.vector.tensor_reduce(meet[:, 1:2], ends[:, 5, 0:BW], AX_X, ALU.max))
            link(nc.vector.tensor_scalar(ends[:, 6, 0:BW], ends[:, 5, 0:BW], meet[:, 1:2], None, ALU.is_equal))
            link(nc.vector.tensor_tensor(ends[:, 6, 0:BW], ends[:, 6, 0:BW], ends[:, 4, 0:BW], ALU.mult))
            link(nc.vector.tensor_reduce(meet[:, 3:4], ends[:, 6, 0:BW], AX_X, ALU.add))
            link(nc.vector.tensor_scalar(meet[:, 2:3], meet[:, 1:2], -1.0, float(BW), ALU.mult, ALU.add))
            link(nc.vector.tensor_tensor(meet[:, 1:2], meet[:, 2:3], nat_col, ALU.add))
            link(nc.vector.tensor_tensor(meet[:, 2:3], meet[:, 1:2], meet[:, 3:4], ALU.add))
            for n in range(2):
                step.mark(nc.vector.tensor_scalar(offers[:, n, :], lane_of[:, 0:NP], meet[:, n:n + 1], None, ALU.mult))
            nc.vector.tensor_scalar(offers[:, 2, :], lane_of[:, 0:NP], meet[:, 2:3], None, ALU.mult).then_inc(offers_done, 1)
            dve.wait_ge(offers_ready, 1)
            got = bank[0][:, 0:3 * NP].rearrange("p (n j) -> p n j", n=3)
            link(nc.vector.tensor_reduce(meet[:, 4:5], got[:, 0, :], AX_X, ALU.min))
            link(nc.vector.tensor_scalar(offers[:, 3, :], got[:, 0, :], meet[:, 4:5], None, ALU.is_equal))
            link(nc.vector.tensor_tensor(offers[:, 3, :], offers[:, 3, :], iota[:, NP:0:-1], ALU.mult))
            link(nc.vector.tensor_reduce(meet[:, 5:6], offers[:, 3, :], AX_X, ALU.max))
            link(nc.vector.tensor_scalar(offers[:, 3, :], offers[:, 3, :], meet[:, 5:6], None, ALU.is_equal))
            for n in range(1, 3):
                link(nc.vector.tensor_tensor(offers[:, n, :], got[:, n, :], offers[:, 3, :], ALU.mult))
                link(nc.vector.tensor_reduce(meet[:, 5 + n:6 + n], offers[:, n, :], AX_X, ALU.add))
            link(nc.vector.tensor_scalar(meet[:, 8:9], meet[:, 7:8], -1.0, float(SEQ - 1), ALU.mult, ALU.add))
            link(nc.vector.tensor_tensor(meet[:, 8:9], meet[:, 8:9], chain1, ALU.mult))
            link(nc.vector.scalar_tensor_tensor(out=meet[:, 9:10], in0=meet[:, 6:7], scalar=chain0, in1=meet[:, 8:9],
                                                op0=ALU.mult, op1=ALU.add))
            step.mark(nc.vector.tensor_scalar(outside[:, 0, :], chain_col[:, :], meet[:, 9:10], None, ALU.is_gt))
            step.mark(nc.vector.tensor_scalar(outside[:, 1, :], chain_col[:, :], meet[:, 9:10], None, ALU.is_le))
            link(nc.vector.tensor_scalar(outside[:, 2, :], chain_col[:, :], meet[:, 9:10], -1.0, ALU.is_le, ALU.mult))
            link(nc.vector.tensor_scalar(meet[:, 10:11], chain_col[:, BW - 1:BW], meet[:, 9:10], last_row, ALU.is_ge, ALU.mult))
            step.mark(nc.vector.tensor_copy(entry[:, :], meet[:, 10:11]))
            forced = end_pick[:, :, :].rearrange("p s w -> p w s")
            nc.vector.tensor_tensor(forced, outside[:, 0, :].unsqueeze(2).broadcast_to((P, BW, NP)),
                                    at_pos[:, :].unsqueeze(1).broadcast_to((P, BW, NP)), ALU.mult).then_inc(overridden, 1)
            dve.wait_ge(overridden, 1)
            dve.wait_ge(masks_done, 2)
            last_cells = is_left[:, :, HALF - 1:S:SKEW]
            nc.vector.tensor_tensor(last_cells, last_cells, forced, ALU.max).then_inc(overridden, 1)
            step.mark(nc.vector.memset(back[:, :, 0:1], 0.0))
            link(nc.vector.tensor_copy(back[:, 0, 1:S + 1], iota[:, :]))
            dve.wait_ge(overridden, 2)
            for w in range(BW):
                a = w % 2
                step.mark(nc.vector.tensor_tensor(pick[:, 0, :], no_up[:, w, :], back[:, a, 0:S], ALU.mult))
                link(nc.vector.tensor_tensor(pick[:, 1, :], is_left[:, w, :], back[:, a, 1:S + 1], ALU.mult))
                link(nc.vector.tensor_tensor_scan(out=back[:, 1 - a, 1:S + 1], data0=pick[:, 0, :], data1=pick[:, 1, :],
                                                  initial=0.0, op0=ALU.max, op1=ALU.max))
            to_before = [l + (l % NP < NP - 1) for l in range(NJ)]
            for j in range(NP - 1):
                link(nc.vector.scalar_tensor_tensor(out=pick[:, 0, :], in0=iota[:, :], scalar=entry[:, 0:1],
                                                    in1=back[:, 0, 1:S + 1], op0=ALU.is_equal, op1=ALU.mult,
                                                    accum_out=left_of[:, 0:1]))
                link(nc.vector.stream_shuffle(left_of[:, 1:2], left_of[:, 0:1], to_before))
                link(nc.vector.tensor_scalar(entry[:, :], left_of[:, 1:2], float(SKEW), meet[:, 10:11],
                                             ALU.subtract, ALU.max))
            link(nc.vector.tensor_copy(leave_at[:, BW:BW + 1], entry[:, :]))
            dve.wait_ge(leave_parts, 2 * BW)
            nc.vector.tensor_tensor(leave, leave, leave_b, ALU.max).then_inc(leave_done, 1)
            dve.wait_ge(leave_done, 1)

            def to_row(w):
                nc.vector.tensor_scalar(leave_row[:, 0, w:w + 1], leave_at[:, w:w + 1], shift, None,
                                        ALU.subtract).then_inc(row_done, 1)
                nc.vector.tensor_scalar(leave_row[:, 1, w:w + 1], leave_at[:, w:w + 1], shift, -2.0,
                                        ALU.subtract, ALU.mult).then_inc(row_done, 1)

            def mark_path(w):
                n = BW - 1 - w
                dve.wait_ge(reach_done, 2 * (n + 1))
                nc.vector.scalar_tensor_tensor(out=path[:, w, :], in0=iota[:, 0:HALF], scalar=leave_row[:, 0, w:w + 1],
                                               in1=reach[:, n % 2, :], op0=ALU.is_ge, op1=ALU.mult).then_inc(on_path_done, 1)

            to_row(BW)
            for w in reversed(range(BW)):
                link(nc.vector.tensor_scalar(pick[:, 1, :], iota[:, :], leave_at[:, w + 1:w + 2], None, ALU.is_le))
                link(nc.vector.tensor_tensor_reduce(out=pick[:, 0, :], in0=pick[:, 1, :], in1=leave[:, w, :], scale=1.0,
                                                    scalar=0.0, op0=ALU.mult, op1=ALU.max,
                                                    accum_out=leave_at[:, w:w + 1]))
                to_row(w)
                if w + 1 < BW:
                    mark_path(w + 1)
            dve.wait_ge(row_done, 2 * (BW + 1))
            mark_path(0)
            dve.wait_ge(rw_hi_done, 1)
            nc.vector.scalar_tensor_tensor(out=rw16[:, 1, :, :], in0=rw[:, :, :], scalar=W_SCALE,
                                           in1=rw16[:, 0, :, :], op0=ALU.mult, op1=ALU.subtract).then_inc(rw_lo_done, 1)

            def normalise(h):
                dve.wait_ge(std2_done, h + 1)
                r = half(rstd[:, 1, :], h)
                link(nc.vector.reciprocal(r, half(rstd[:, 0, :], h)))
                link(nc.vector.tensor_scalar(r, r, Y_SCALE, None, ALU.mult))
                if h == 0:
                    dve.wait_ge(pathT_ready, 2 * NW - 2)
                for n in (2 * h, 2 * h + 1):
                    for w in range(ORDER[n] * WG, (ORDER[n] + 1) * WG):
                        nc.vector.tensor_scalar(yn[:, w, :], X[:, w, :], mv[:, w, 0:1], rstd[:, 1, w:w + 1],
                                                ALU.subtract, ALU.mult).then_inc(yn_done, 1)
                if h:
                    link(nc.vector.tensor_tensor(msq[:, 0, :], mv[:, :, 1], rstd[:, 1, :], ALU.mult))
                    nc.vector.tensor_tensor(msq[:, 0, :], msq[:, 0, :], rstd[:, 1, :], ALU.mult).then_inc(msq_done, 1)

            def low_half(n):
                s = slice(ORDER[n] * WG, (ORDER[n] + 1) * WG)
                dve.wait_ge(y_hi_done, n + 1)
                dve.wait_ge(yn_done, (n + 1) * WG)
                nc.vector.tensor_tensor(y16[:, s, 1, :], yn[:, s, :], y16[:, s, 0, :], ALU.subtract).then_inc(y_lo_done, 1)

            def move_yT(n):
                dve.wait_ge(yT_ready, 2 * n + 2)
                nc.vector.tensor_copy(yT[:, ORDER[n], 1, :, :], bank[7][:, :].bitcast(F16).rearrange("p (k n) -> p k n", k=KC))\
                    .then_inc(yT_moved_dve, 1)

            dve.wait_ge(tanh_done, 1)
            for m, n in enumerate(PAIRS):
                dve.wait_ge(aligned_ready, m + 1)
                nc.vector.scalar_tensor_tensor(out=X[:, 2 * n:2 * n + 2, :], in0=bank[4 + m % 4][:, :],
                                               scalar=tanhs[:, 0:1], in1=X[:, 2 * n:2 * n + 2, :],
                                               op0=ALU.mult, op1=ALU.add).then_inc(x2_done, 1)
                dve.wait_ge(x2_done, m + 1)
                for w in (2 * n, 2 * n + 1):
                    last = step.mark(nc.vector.bn_stats(bn[:, w, :], X[:, w, :]))
                dve.wait_ge(dve_step, last)
                last = step.mark(nc.vector.bn_aggr(mv[:, 2 * n, :], bn[:, 2 * n, :]))
                last = nc.vector.bn_aggr(mv[:, 2 * n + 1, :], bn[:, 2 * n + 1, :])
                if m % 4 < 3:
                    step.mark(last)
                else:
                    last.then_inc(bn2_done, 1)
                if m == 3:
                    normalise(0)
                elif m in (4, 5):
                    low_half(m - 4)
            for n in range(2):
                move_yT(n)
            normalise(1)
            for n in range(2, NG):
                low_half(n)

            by_token = "p e w -> p w e"
            all_e = (P, E, W)

            def over_e(row):
                return row.unsqueeze(1).broadcast_to(all_e)

            def route(stage):
                if stage == 0:
                    dve.wait_ge(rms_done, 1)
                    link(nc.vector.reciprocal(msq[:, 2, :], msq[:, 1, :]))
                    link(nc.vector.tensor_scalar(msq[:, 2, :], msq[:, 2, :], 1.0 / (Y_SCALE * W_SCALE), None, ALU.mult))
                    dve.wait_ge(logits_ready, 1)
                    link(nc.vector.tensor_tensor(probs[:, :, :], bank[7][:, 0:W * E].rearrange("p (w e) -> p e w", e=E),
                                                 over_e(msq[:, 2, :]), ALU.mult))
                    link(nc.vector.tensor_reduce(per_tok[:, 0, :], probs[:, :, :].rearrange(by_token), AX_X, ALU.max))
                    nc.vector.tensor_tensor(probs[:, :, :], probs[:, :, :], over_e(per_tok[:, 0, :]), ALU.subtract).then_inc(shifted, 1)
                elif stage == 1:
                    dve.wait_ge(exp_done, 1)
                    link(nc.vector.tensor_reduce(per_tok[:, 1, :], probs[:, :, :].rearrange(by_token), AX_X, ALU.add))
                    link(nc.vector.reciprocal(per_tok[:, 2, :], per_tok[:, 1, :]))
                    link(nc.vector.tensor_tensor(probs[:, :, :], probs[:, :, :], over_e(per_tok[:, 2, :]), ALU.mult))
                elif stage in (2, 3):
                    k = stage - 2
                    link(nc.vector.tensor_reduce(per_tok[:, 3 + k, :], probs[:, :, :].rearrange(by_token), AX_X, ALU.max))
                    link(nc.vector.tensor_tensor(keys[:, :, :], probs[:, :, :], over_e(per_tok[:, 3 + k, :]), ALU.is_equal))
                    link(nc.vector.tensor_tensor(keys[:, :, :], keys[:, :, :], key_of[:, :, :], ALU.mult))
                    link(nc.vector.tensor_reduce(per_tok[:, 5, :], keys[:, :, :].rearrange(by_token), AX_X, ALU.max))
                    link(nc.vector.tensor_tensor(hot[:, k, :, :], keys[:, :, :], over_e(per_tok[:, 5, :]), ALU.is_equal))
                    if stage == 2:
                        link(nc.vector.scalar_tensor_tensor(out=probs[:, :, :], in0=hot[:, 0, :, :], scalar=-2.0,
                                                            in1=probs[:, :, :], op0=ALU.mult, op1=ALU.add))
                elif stage == 4:
                    link(nc.vector.tensor_tensor(chosen[:, :, :], hot[:, 0, :, :], hot[:, 1, :, :], ALU.add))
                    link(nc.vector.tensor_tensor_scan(out=upto[:, :, :].rearrange("p e w -> p (e w)"),
                                                      data0=goes_on[:, :, :].rearrange("p e w -> p (e w)"),
                                                      data1=chosen[:, :, :].rearrange("p e w -> p (e w)"),
                                                      initial=0.0, op0=ALU.mult, op1=ALU.add))
                    nc.vector.tensor_copy(lane_total[:, 0, :], upto[:, :, W - 1]).then_inc(totals_done, 1)
                    dve.wait_ge(totals_done, 1)
                    link(nc.vector.tensor_tensor(upto[:, :, :], upto[:, :, :], chosen[:, :, :], ALU.subtract))
                elif stage == 5:
                    dve.wait_ge(base_ready, 1)
                    link(nc.vector.tensor_copy(lane_total[:, 1, :], bank[7][:, W * E:(W + 1) * E]))
                    link(nc.vector.tensor_tensor(upto[:, :, :], upto[:, :, :], lane_total[:, 1, :].unsqueeze(2).broadcast_to(all_e),
                                                 ALU.add))
                    step.mark(nc.vector.tensor_scalar(fits[:, :, :], upto[:, :, :], float(CAP), None, ALU.is_lt))
                    link(nc.vector.tensor_tensor(upto[:, :, :], upto[:, :, :], slot_of[:, :, :], ALU.add))
                elif stage == 6:
                    for k in range(2):
                        for v, row in ((fits, 6 + k), (upto, 8 + k)):
                            link(nc.vector.tensor_tensor(keys[:, :, :], hot[:, k, :, :], v[:, :, :], ALU.mult))
                            link(nc.vector.tensor_reduce(per_tok[:, row, :], keys[:, :, :].rearrange(by_token), AX_X, ALU.add))
                    link(nc.vector.tensor_tensor(per_tok[:, 10:12, :], per_tok[:, 8:10, :], per_tok[:, 6:8, :], ALU.mult))
                    nc.vector.tensor_copy(from_slot[:, :, :], per_tok[:, 10:12, :]).then_inc(from_slot_done, 1)
                    dve.wait_ge(from_slot_done, 1)
                elif stage == 7:
                    link(nc.vector.tensor_scalar(per_tok[:, 8:10, :], per_tok[:, 8:10, :], float(NO_SLOT), None, ALU.subtract))
                    link(nc.vector.tensor_tensor(per_tok[:, 8:10, :], per_tok[:, 8:10, :], per_tok[:, 6:8, :], ALU.mult))
                    link(nc.vector.tensor_scalar(per_tok[:, 8:10, :], per_tok[:, 8:10, :], float(NO_SLOT), None, ALU.add))
                    nc.vector.tensor_copy(to_slot[:, :, :], per_tok[:, 8:10, :]).then_inc(to_slot_done, 1)
                elif stage == 8:
                    link(nc.vector.tensor_tensor(per_tok[:, 0, :], per_tok[:, 3, :], per_tok[:, 4, :], ALU.add))
                    link(nc.vector.reciprocal(per_tok[:, 1, :], per_tok[:, 0, :]))
                    link(nc.vector.tensor_scalar(out_gate[:, :], tanhs[:, 1:2], OUT_SCALE, None, ALU.mult))
                    for k in range(2):
                        link(nc.vector.tensor_tensor(per_tok[:, 3 + k, :], per_tok[:, 3 + k, :], per_tok[:, 1, :], ALU.mult))
                    link(nc.vector.scalar_tensor_tensor(out=per_tok[:, 3:5, :], in0=per_tok[:, 3:5, :], scalar=out_gate[:, 0:1],
                                                        in1=per_tok[:, 6:8, :], op0=ALU.mult, op1=ALU.mult))

            def add_routed(n):
                w = ORDER[n // WG] * WG + n % WG
                for k in range(2):
                    dve.wait_ge(gathered[ORDER[n // WG]], 16 * 2 * WG)
                    if k:
                        dve.wait_ge(routed_added, 2 * n + 1)
                    nc.vector.scalar_tensor_tensor(out=X[:, w, :], in0=gathered_rows[:, w, k, :],
                                                   scalar=per_tok[:, 3 + k, w:w + 1], in1=X[:, w, :],
                                                   op0=ALU.mult, op1=ALU.add).then_inc(routed_added, 1)

            def add_shared(g):
                for h in range(2):
                    w = g * WG + 2 * h
                    nc.vector.scalar_tensor_tensor(out=X[:, w:w + 2, :], in0=bank[4 + h][:, :].rearrange(
                        "p (w h) -> p w h", w=2), scalar=out_gate[:, 0:1], in1=X[:, w:w + 2, :],
                        op0=ALU.mult, op1=ALU.add).then_inc(shared_added, 1)

            for q in range(NCH + 1):
                if q < NCH:
                    n, kind, i, c = CHUNKS[q]
                    cols = GT if kind == "shared" else CAP
                    dve.wait_ge(silu_done, q + 1)
                    if q >= 2:
                        dve.wait_ge(act_lo_done, q - 1)
                    nc.vector.scalar_tensor_tensor(out=act32[q % 2][:, 0:cols], in0=bank[2 + q % 2][:, 0:cols],
                                                   scalar=A_SCALE / (Y_SCALE * W_SCALE), in1=gated[q % 2][:, 0:cols],
                                                   op0=ALU.mult, op1=ALU.mult).then_inc(gated_done, 1)
                if q >= 1:
                    r = q - 1
                    cols = GT if CHUNKS[r][1] == "shared" else CAP
                    dve.wait_ge(act_hi_done, q)
                    dve.wait_ge(gated_done, q)
                    nc.vector.tensor_tensor(act16[:, r % 4, 1, 0:cols], act32[r % 2][:, 0:cols],
                                            act16[:, r % 4, 0, 0:cols], ALU.subtract).then_inc(act_lo_done, 1)
                if q == LATE_TURN:
                    for n in range(2, NG):
                        move_yT(n)
                for stage in router_stages.get(q, ()):
                    route(stage)
                for e, j in split_at.get(q, ()):
                    u, k = divmod(j, KC)
                    m = 3 * e + u
                    dve.wait_ge(ex_hi_done, e * PIECES + j + 1)
                    nc.vector.scalar_tensor_tensor(out=ex_gu[e % 2][:, 1, j * PIECE:(j + 1) * PIECE],
                                                   in0=ex_raw[m % 2][:, k * PIECE:(k + 1) * PIECE], scalar=W_SCALE,
                                                   in1=ex_gu[e % 2][:, 0, j * PIECE:(j + 1) * PIECE],
                                                   op0=ALU.mult, op1=ALU.subtract).then_inc(ex_lo_done, 1)
                if q in turn_at:
                    e = turn_at[q]
                    dve.wait_ge(exT_ready, 2 * e + 2)
                    nc.vector.tensor_copy(exT[:, e % 2, KC:2 * KC, :], bank[7][:, :].bitcast(F16)[:, 0:KC * CAP].rearrange(
                        "p (k n) -> p k n", k=KC)).then_inc(exT_moved_dve, 1)
                job = next((n for n in range(len(JOBS)) if FIRST_CHUNK[n + 1] + LAG - 1 == q), None)
                if job is not None and JOBS[job][0] == "shared":
                    dve.wait_ge(down_done, FIRST_CHUNK[job + 1])
                    add_shared(JOBS[job][1])
                if q >= FIRST_CHUNK[-2] and q < NCH:
                    add_routed(q - FIRST_CHUNK[-2])
            dve.wait_ge(down_done, NCH)
            dve.wait_ge(routed_added, 2 * W)
            add_shared(JOBS[-1][1])

        @block.tensor
        def _(pe):
            def warm_up():
                for _ in range(WARM_UP):
                    pe.matmul(bank[7][:, 0:P], ident[:, :], ident[:, :], start=True, stop=True)

            pe.wait_ge(consts, 13)
            pe.wait_ge(ctx_loaded, 16)
            for n in range(KC * B):
                b, k = divmod(n, KC)
                if n >= 4:
                    pe.wait_ge(ctxT_moved, n - 3)
                for c in range(NI):
                    last = pe.transpose(bank[n % 4][:, c * P:(c + 1) * P],
                                        ctx_rows[:, b * NI + c, k * P:(k + 1) * P], ident[:, :])
                last.then_inc(ctxT_ready, 1)
            for n in range(KC * W // 4):
                q, k = divmod(n, KC)
                pe.wait_ge(ln1_done, 4 * q + 4)
                if n >= 4:
                    pe.wait_ge(lnT_moved_act, 2 * (n - 3))
                    pe.wait_ge(lnT_moved_dve, 2 * (n - 3))
                for c in range(4):
                    last = pe.transpose(bank[4 + n % 4][:, c * P:(c + 1) * P],
                                        ln1[:, 4 * q + c, k * P:(k + 1) * P], ident[:, :])
                last.then_inc(lnT_ready, 1)
            pe.wait_ge(sq_done, KC * B)
            pe.wait_ge(ctxT_moved, KC * B)
            for k in range(KC):
                for b in range(B):
                    last = pe.matmul(bank[0][NJ * b:NJ * (b + 1), :], ones[:, :], ctx_sq[:, k, b * SEQ:(b + 1) * SEQ],
                                     start=(k == 0), stop=(k == KC - 1))
            last.then_inc(norm_ready, 1)
            pe.wait_ge(lnT_moved_act, 2 * KC * W // 4)
            pe.wait_ge(lnT_moved_dve, 2 * KC * W // 4)

            warm_up()

            def lane_norms():
                pe.wait_ge(spread_done, 2)
                pe.wait_ge(ln_norm_turned, 1)
                for f in range(2):
                    o = bank[4][:, W * f:W * (f + 1)]
                    pe.matmul(o, spread[:, 0, f, :], ln_norm[:, 0, :], start=True, stop=False)
                    last = pe.matmul(o, spread[:, 1, f, :], ln_norm[:, 1, :], start=False, stop=True)
                last.then_inc(lane_norm_ready, 1)

            for n, (m, q) in enumerate(PARTS):
                V, R = PER_BANK[m], ROWS[m]
                if n == 1:
                    lane_norms()
                if n >= 3:
                    pe.wait_ge(picked_done, 2 * (n - 2))
                for v in range(V):
                    for k in range(KC):
                        rows = ctxT[:, k, :].rearrange("p (b d i) -> p b d i", b=B, d=2)
                        for b in range(B):
                            last = pe.matmul(bank[1 + n % 3][NJ * b:NJ * (b + 1), 2 * R * v:2 * R * (v + 1)],
                                             lnT[:, k, V * q + v, b, :], rows[:, b, :, ROW_0[m]:ROW_0[m] + R],
                                             start=(k == 0), stop=(k == KC - 1))
                last.then_inc(prod_ready, 1)
            pe.wait_ge(offers_done, 1)
            pe.matmul(bank[0][:, 0:3 * NP], same_batch[:, :], offers[:, 0:3, :].rearrange("p n j -> p (n j)"),
                      start=True, stop=True).then_inc(offers_ready, 1)
            def turn_path(g):
                for n in (2 * g, 2 * g + 1):
                    q, c = group_of_bank(n)
                    pe.wait_ge(on_path_done, BW - WQ * q)
                    if n >= 4:
                        pe.wait_ge(pathT_moved, 2 * (n - 3))
                    for v in range(WQ):
                        last = pe.transpose(bank[n % 4][:, :].bitcast(F16)[:, v * P:(v + 1) * P],
                                            path[:, WQ * q + v, c * P:(c + 1) * P], ident16[:, :])
                    last.then_inc(pathT_ready, 1)

            def align(m):
                n = PAIRS[m]
                pe.wait_ge(pathT_moved, 4 * GROUPS_FOR[m])
                if m >= 4:
                    pe.wait_ge(x2_done, m - 3)
                for c in range(2):
                    for z in range(2):
                        for i in range(NI):
                            for b in range(B):
                                last = pe.matmul(bank[4 + m % 4][NJ * b:NJ * (b + 1), c * H:(c + 1) * H],
                                                 pathT[:, i, 2 * n + c, b, :], ctx16[:, z, b * NI + i, :],
                                                 start=(z == 0 and i == 0), stop=(z == 1 and i == NI - 1))
                last.then_inc(aligned_ready, 1)

            for g in range(NW - 2):
                turn_path(g)
            pe.wait_ge(ctx_lo_done, B)
            pe.wait_ge(ctx_hi_done, B)
            warm_up()
            turn_path(NW - 2)
            for m in range(W // 4):
                align(m)
            turn_path(NW - 1)
            for m in range(W // 4, W // 2):
                align(m)

            def turn_y(n):
                pe.wait_ge(y_hi_done, n + 1)
                pe.wait_ge(y_lo_done, n + 1)
                pe.wait_ge(x2_done, W // 2)
                for z in range(2):
                    if n:
                        pe.wait_ge((yT_moved_act, yT_moved_dve)[z], n)
                    for k in range(KC):
                        for c in range(WG):
                            last = pe.transpose(bank[6 + z][:, :].bitcast(F16)[:, (k * WG + c) * P:(k * WG + c + 1) * P],
                                                y16[:, ORDER[n] * WG + c, z, k * P:(k + 1) * P], ident16[:, :])
                    last.then_inc(yT_ready, 1)

            pairs = ((0, 0), (0, 1), (1, 0))
            for n in range(2):
                turn_y(n)

            def logits():
                pe.wait_ge(yT_moved_act, NG)
                pe.wait_ge(yT_moved_dve, NG)
                pe.wait_ge(rw_lo_done, 1)
                for w in range(W):
                    g, c = divmod(w, WG)
                    for n, (k, (zy, zw)) in enumerate((k, p) for k in range(KC) for p in pairs):
                        last = pe.matmul(bank[7][:, w * E:(w + 1) * E], yT[:, g, zy, k, c * P:(c + 1) * P], rw16[:, zw, k, :],
                                         start=(n == 0), stop=(n == 3 * KC - 1))
                last.then_inc(logits_ready, 1)

            def gate_and_up(q):
                n, kind, i, c = CHUNKS[q]
                cols = GT if kind == "shared" else CAP
                for m in range(2):
                    for k in range(KC):
                        for zw, zy in pairs:
                            if kind == "shared":
                                weights = gu16[:, m, zw, k, c * P:(c + 1) * P]
                                moving = yT[:, i, zy, k, :]
                            else:
                                o = (m * KC + k) * IR + c * P
                                weights = ex_gu[i % 2][:, zw, o:o + P]
                                moving = exT[:, i % 2, zy * KC + k, :]
                            first = k == 0 and (zw, zy) == pairs[0]
                            final = k == KC - 1 and (zw, zy) == pairs[-1]
                            last = pe.matmul(bank[2 * m + q % 2][:, 0:cols], weights, moving, start=first, stop=final)
                last.then_inc(gu_ready, 1)

            def down(q):
                n, kind, i, c = CHUNKS[q]
                tiles = [(m * P, P) for m in range(WG)] if kind == "shared" else TILES_E
                for t, (m, rows) in enumerate(tiles):
                    for za, zw in pairs:
                        weights = down16[:, zw, c, :] if kind == "shared" else \
                            ex_gu[i % 2][:, zw, 2 * KC * IR + c * H:2 * KC * IR + (c + 1) * H]
                        last = pe.matmul(bank[4 + t // 2][0:rows, (t % 2) * H:(t % 2 + 1) * H],
                                         act16[:, q % 4, za, m:m + rows], weights,
                                         start=(c == 0 and t % 2 == 0 and (za, zw) == pairs[0]),
                                         stop=(q + 1 == FIRST_CHUNK[n + 1] and (za, zw) == pairs[-1]),
                                         skip_group_check=True)
                last.then_inc(down_done, 1)

            for q in range(NCH + LAG):
                if q < NCH:
                    n, kind, i, c = CHUNKS[q]
                    if kind == "shared" and q == 0:
                        pe.wait_ge(raw_lo_done, 12)
                        pe.wait_ge(yT_moved_act, 2)
                        pe.wait_ge(yT_moved_dve, 2)
                    if kind == "expert" and c == 0:
                        pe.wait_ge(ex_lo_done, i * PIECES + 2 * PIECES // 3)
                        pe.wait_ge(exT_moved_act, i + 1)
                        pe.wait_ge(exT_moved_dve, i + 1)
                    if q >= 2:
                        pe.wait_ge(silu_done, q - 1)
                        pe.wait_ge(gated_done, q - 1)
                    gate_and_up(q)
                if q >= LAG:
                    r = q - LAG
                    n, kind, i, c = CHUNKS[r]
                    if kind == "expert" and c == 0:
                        pe.wait_ge(ex_lo_done, (i + 1) * PIECES)
                    if c == 0 and n:
                        if JOBS[n - 1][0] == "shared":
                            pe.wait_ge(shared_added, 2 * sum(k == "shared" for k, _ in JOBS[:n]))
                        else:
                            pe.wait_ge(ex_out_moved, 2 * (JOBS[n - 1][1] + 1))
                    pe.wait_ge(act_lo_done, r + 1)
                    down(r)
                if q == LATE_TURN:
                    for n in range(2, NG):
                        turn_y(n)
                elif q == LATE_TURN + 1:
                    logits()
                elif q == BASE_AT:
                    pe.wait_ge(totals_done, 1)
                    pe.matmul(bank[7][:, W * E:(W + 1) * E], earlier[:, :], lane_total[:, 0, :],
                              start=True, stop=True).then_inc(base_ready, 1)
                if q in turn_at:
                    e = turn_at[q]
                    pe.wait_ge(ex_in_loaded, 32 * (e + 1))
                    for z in range(2):
                        if e:
                            pe.wait_ge((exT_moved_act, exT_moved_dve)[z], e)
                        for k in range(KC):
                            for t, (m, rows) in enumerate(TILES_E):
                                o = k * CAP + m
                                last = pe.transpose(bank[6 + z][:, :].bitcast(F16)[:, o:o + rows],
                                                    ex_in[0:rows, t, z, k * P:(k + 1) * P], ident16[0:rows, 0:rows])
                        last.then_inc(exT_ready, 1)


_INS = ["x", "folded", "g_xattn", "g_ffn", "L0_ffn_router_w", "L0_ffn_rg", "L0_ffn_ru", "L0_ffn_rd",
        "L0_ffn_sg", "L0_ffn_su", "L0_ffn_sd"]
_OUTS = [((4, 512, 256), "float32")]


def kernel(**inputs):
    import numpy as _np
    import concourse.bacc as _bacc
    from concourse import mybir as _mybir
    from concourse.bass_utils import run_bass_kernel_spmd as _run

    nc = _bacc.Bacc("TRN2", target_bir_lowering=False, num_devices=1)
    ctx = inputs["ctx_1024"]
    half = ctx.shape[1] // 2
    inputs = dict(inputs, folded=_np.stack([ctx[:, :half], ctx[:, :half - 1:-1]], axis=1))
    arrays, args = {}, []
    for name in _INS:
        a = _np.ascontiguousarray(inputs[name])
        arrays[f"in_{name}_dram"] = a
        args.append(nc.dram_tensor(f"in_{name}_dram", a.shape, _mybir.dt.from_np(a.dtype), kind="ExternalInput").ap())
    for i, (shape, dtype) in enumerate(_OUTS):
        dt = _mybir.dt.from_np(_np.dtype(dtype))
        args.append(nc.dram_tensor(f"out_{i}_dram", shape, dt, kind="ExternalOutput").ap())
    flamingo_dtw_moe(nc, *args)
    r = _run(nc, [arrays], core_ids=[0])
    return r.results[0]["out_0_dram"]
```

```python
from contextlib import ExitStack

import concourse.bass as bass
from concourse import mybir

ALU = mybir.AluOpType
ACT = mybir.ActivationFunctionType
F32 = mybir.dt.float32
F16 = mybir.dt.float16
I32 = mybir.dt.int32
AX_X = mybir.AxisListType.X

P = 128
BIG = 1e30
BIG_ROW = 1000.0
LN_EPS = 1e-5
RMS_EPS = 1.1920928955078125e-07
CAPACITY_FACTOR = 1.25

Y_SCALE = 64.0
W_SCALE = 256.0
A_SCALE = 16.0
LAG = 2
WARM_UP_D = 20
WARM_UP = 32


def flamingo_dtw_moe(nc, x, folded, g_xattn, g_ffn, router_w, rg, ru, rd, sg, su, sd, out, stop=None):
    B, SEQ, H = x.shape
    E, _, IR = rg.shape
    IS = sg.shape[1]
    T = B * SEQ
    W = T // P
    NJ = P // B
    KC = H // P
    NI = SEQ // P
    HALF = SEQ // 2
    NP = NJ // 2
    BW = SEQ // NP
    CW = BW + 1
    SKEW = 2
    S = HALF + SKEW * (NP - 1)
    ROWS = [32, 32, 64, 64, 64]
    RC = max(ROWS)
    NC = len(ROWS)
    ROW_0 = [sum(ROWS[:m]) for m in range(NC)]
    PER_BANK = [P * 2 // n for n in ROWS]
    PARTS = [(m, q) for m in range(NC) for q in range(BW // PER_BANK[m])]
    PARTS_TO = [sum(m <= c for m, _ in PARTS) for c in range(NC)]
    WQ = 4
    NW = BW // WQ
    TOGETHER = [1, 4, 8, 16, 16]
    CAP = int(CAPACITY_FACTOR * T / E)
    NG = 4
    WG = W // NG
    GT = WG * P
    NO_SLOT = 4 * E * CAP
    IC, IC_E = IS // P, IR // P
    TILES_E = [(m, min(P, CAP - m)) for m in range(0, CAP, P)]
    EX_STORES = 16 * 3
    ORDER = [1, 2, 0, 3]
    JOBS = [("shared", g) for g in ORDER[:2]] + [("expert", e) for e in range(E)] + [("shared", g) for g in ORDER[2:]]
    CHUNKS = [(n, kind, i, c) for n, (kind, i) in enumerate(JOBS) for c in range(IC if kind == "shared" else IC_E)]
    NCH = len(CHUNKS)
    FIRST_CHUNK = [next(q for q, ch in enumerate(CHUNKS) if ch[0] == n) for n in range(len(JOBS))] + [NCH]
    MASK_FROM, MASK_ROWS = S // 2 + 1, 2
    N_MASKS = S // MASK_ROWS
    SPLIT_EARLY, SPLIT_BEFORE, SPLIT_AT_END = range(0, 6), range(6, 8), range(8, 10)
    split_beside = {1: 10, 5: 11}
    PIECE = 1024
    PIECES = 3 * KC * IR // PIECE
    split_at = {}
    for e in range(E):
        base = FIRST_CHUNK[e + 1] + 2 if e else FIRST_CHUNK[0] + 14
        for j in range(PIECES):
            split_at.setdefault(base + j, []).append((e, j))
    turn_at = {FIRST_CHUNK[e + 2] - (3 if e else 2): e for e in range(E)}
    LATE_TURN = 3
    ROUTER_FROM = 5
    BASE_AT = ROUTER_FROM + 5
    router_stages = {ROUTER_FROM: (0,), ROUTER_FROM + 1: (1,), ROUTER_FROM + 2: (2,), ROUTER_FROM + 3: (3, 4),
                     BASE_AT: (5,), BASE_AT + 1: (6, 7), BASE_AT + 2: (8,)}
    OUT_SCALE = 1.0 / (A_SCALE * W_SCALE)
    assert [n for _, n in TILES_E] == [P, P, P // 2]
    assert NJ == 32 and H == 2 * P and SEQ == 4 * P and W == 16

    with ExitStack() as stack:
        def sb(name, shape, dt=F32):
            return stack.enter_context(nc.sbuf_tensor(name, shape, dt))

        def sem(name):
            return stack.enter_context(nc.semaphore(name))

        bank = [stack.enter_context(nc.psum_tensor(f"bank{i}", [P, 512], F32)) for i in range(8)]

        X = sb("x_rows", [P, W, H])
        region_a = sb("region_a", [P, 3 * KC * T])
        region_c = sb("region_c", [P, W * H])
        region_d = sb("region_d", [P, BW * (S + 2) // 2])
        region_e = sb("region_e", [P, (S + 2) * CW])
        region_f = sb("region_f", [P, (S + 1) * CW])

        ctxT = region_a[:, 0:KC * T].rearrange("p (k n) -> p k n", k=KC)
        lnT = region_a[:, KC * T:3 * KC * T].rearrange("p (k w b l) -> p k w b l", k=KC, w=BW, b=B)
        ctx_rows = region_c[:, :].rearrange("p (n h) -> p n h", h=H)
        ln1 = region_e[:, 0:W * H].rearrange("p (w h) -> p w h", h=H)
        spread = region_e[:, W * H:W * H + 4 * P].rearrange("p (d f l) -> p d f l", d=2, f=2)
        ctx_sq = region_f[:, 0:KC * T].rearrange("p (k n) -> p k n", k=KC)
        dist = region_d[:, 0:2 * RC * CW].rearrange("p (m i c) -> p m i c", m=2, c=CW)
        table = region_e[:, :].rearrange("p (s c) -> p s c", c=CW)
        cost = region_f[:, :].rearrange("p (s c) -> p s c", c=CW)
        halves = BW * S // 2
        no_up = region_d[:, 0:halves].bitcast(F16).rearrange("p (w s) -> p w s", w=BW)
        is_left = region_a[:, 3 * KC * T - halves:3 * KC * T].bitcast(F16).rearrange("p (w s) -> p w s", w=BW)
        leave = region_f[:, 0:halves].bitcast(F16).rearrange("p (w s) -> p w s", w=BW)
        leave_b = region_e[:, 0:halves].bitcast(F16).rearrange("p (w s) -> p w s", w=BW)
        entered = region_e[:, halves:halves + BW * HALF // 2].bitcast(F16).rearrange("p (w i) -> p w i", w=BW)
        left = region_e[:, 0:BW * HALF // 2].bitcast(F16).rearrange("p (w i) -> p w i", w=BW)
        pathT = region_d[:, 0:W * SEQ // 2].bitcast(F16).rearrange("p (n w b j) -> p n w b j", n=NI, w=W, b=B)
        ctx16 = region_f[:, halves:halves + W * H].bitcast(F16).rearrange("p (z n h) -> p z n h", z=2, h=H)

        gu16 = region_a[:, 0:2 * KC * IS].bitcast(F16).rearrange("p (m z k i) -> p m z k i", m=2, z=2, k=KC)
        down16 = region_a[:, 2 * KC * IS:3 * KC * IS].bitcast(F16).rearrange("p (z i h) -> p z i h", z=2, h=H)
        yn = region_e[:, 0:W * H].rearrange("p (w h) -> p w h", h=H)
        y16 = region_f[:, 0:W * H].bitcast(F16).rearrange("p (w z h) -> p w z h", w=W, z=2)
        yT = region_c[:, :].bitcast(F16).rearrange("p (g z k n) -> p g z k n", g=NG, z=2, k=KC)
        ew = 3 * KC * IR
        ex_gu = [r[:, 0:ew].bitcast(F16).rearrange("p (z n) -> p z n", z=2) for r in (region_e, region_f)]
        ex_raw = [r[:, ew:ew + KC * IR] for r in (region_e, region_f)]
        gated = [r[:, ew + KC * IR:ew + KC * IR + 512] for r in (region_e, region_f)]
        act32 = [r[:, ew + KC * IR + 512:ew + KC * IR + 1024] for r in (region_e, region_f)]
        act16 = region_d[:, 0:2048].bitcast(F16).rearrange("p (r z n) -> p r z n", r=4, z=2)
        ex_out = region_d[:, 2048:2048 + 2 * 768].rearrange("p (r m h) -> p r m h", r=2, h=H)
        ex_in = region_d[:, 3584:3584 + 768].bitcast(F16).rearrange("p (m z h) -> p m z h", m=3, z=2)
        gathered_rows = region_e[:, 0:2 * W * H].rearrange("p (w k h) -> p w k h", w=W, k=2)
        slots = nc.dram_tensor("slots", (E * CAP, 2 * H), F16).ap()
        ex_rows = nc.dram_tensor("ex_rows", (E * CAP, H), F32).ap()

        exT = sb("exT", [P, 2, 2 * KC, CAP], F16)
        rw = sb("rw", [P, KC, E])
        rw16 = sb("rw16", [P, 2, KC, E], F16)
        earlier = sb("earlier", [P, P])
        key_of = sb("key_of", [P, E, W])
        slot_of = sb("slot_of", [P, E, W])
        goes_on = sb("goes_on", [P, E, W])
        msq = sb("msq", [P, 3, W])
        rms_eps = sb("rms_eps", [P, 1])
        probs = sb("probs", [P, E, W])
        keys = sb("keys", [P, E, W])
        hot = sb("hot", [P, 2, E, W])
        chosen = sb("chosen", [P, E, W])
        upto = sb("upto", [P, E, W])
        fits = sb("fits", [P, E, W])
        lane_total = sb("lane_total", [P, 2, E])
        per_tok = sb("per_tok", [P, 12, W])
        to_slot = sb("to_slot", [P, 2, W], I32)
        from_slot = sb("from_slot", [P, 2, W], I32)
        out_gate = sb("out_gate", [P, 1])
        ident = sb("ident", [P, P])
        ident16 = sb("ident16", [P, P], F16)
        same_batch = sb("same_batch", [P, P])
        ones = sb("ones", [P, NJ])
        iota = sb("iota", [P, S], F16)
        iota_skew = sb("iota_skew", [P, S], F16)
        iota_less = sb("iota_less", [P, S], F16)
        ctx_norm = sb("ctx_norm", [P, HALF])
        raw = sb("raw", [P, 2, PIECE])
        picked = raw[:, 0, :].rearrange("p (r d n) -> p r d n", r=2, d=2)
        exT32 = exT[:, :, :, :].rearrange("p a k n -> p (a k n)").bitcast(F32)
        end_pick = exT32[:, 0:NP * BW].rearrange("p (s w) -> p s w", w=BW)
        ends = exT32[:, NP * BW:NP * BW + 8 * CW].rearrange("p (n w) -> p n w", w=CW)
        zeros = exT32[:, 1280 - H:1280]
        ln_norm = sb("ln_norm", [P, 2, W])
        lane_norm = sb("lane_norm", [P, BW])
        sq_dump = sb("sq_dump", [P, 2, H])
        bn = sb("bn", [P, W, 6])
        mv = sb("mv", [P, W, 2])
        rstd = sb("rstd", [P, 2, W])
        back = sb("back", [P, 2, S + 2], F16)
        pick = sb("pick", [P, 2, S], F16)
        iota_row = sb("iota_row", [P, HALF], F16)
        minus_ident16 = sb("minus_ident16", [P, P], F16)
        last_back = sb("last_back", [P, BW, NP], F16)
        at_meet = sb("at_meet", [P, BW, NP], F16)
        left_after = sb("left_after", [P, BW])
        at_last = sb("at_last", [P, NP])
        entry = sb("entry", [P, 1])
        leave_at = sb("leave_at", [P, BW + 1])
        left_of = sb("left_of", [P, 2])
        lane_of = sb("lane_of", [P, NJ])
        at_pos = sb("at_pos", [P, NP])
        lane_pos = sb("lane_pos", [P, 9])
        pos, shift, border, no_next, base_col, last_row, chain0, chain1, nat_col = (
            lane_pos[:, n:n + 1] for n in range(9))
        chain_col = sb("chain_col", [P, BW])
        meet = sb("meet", [P, 16])
        offers = sb("offers", [P, 4, NP])
        outside = sb("outside", [P, 3, BW])
        gates = sb("gates", [P, 2])
        tanhs = sb("tanhs", [P, 2])
        ln_eps = sb("ln_eps", [P, 1])

        x_loaded = sem("x_loaded")
        ctx_loaded = sem("ctx_loaded")
        small_loaded = sem("small_loaded")
        consts = sem("consts")
        bn_done = sem("bn_done")
        dve_step = sem("dve_step")
        ln1_done = sem("ln1_done")
        std_done = sem("std_done")
        lnT_ready = sem("lnT_ready")
        ctxT_ready = sem("ctxT_ready")
        ctxT_moved = sem("ctxT_moved")
        sq_done = sem("sq_done")
        norm_ready = sem("norm_ready")
        dist_done = sem("dist_done")
        top_set = sem("top_set")
        min_done = sem("min_done")
        scan_done = sem("scan_done")
        shift_done = sem("shift_done")
        pathT_ready = sem("pathT_ready")
        pathT_moved = sem("pathT_moved")
        ctx_hi_done = sem("ctx_hi_done")
        ctx_lo_done = sem("ctx_lo_done")
        aligned_ready = sem("aligned_ready")
        x2_done = sem("x2_done")
        tanh_done = sem("tanh_done")
        stored = sem("stored")
        lnT_moved_act = sem("lnT_moved_act")
        lnT_moved_dve = sem("lnT_moved_dve")
        lanes_done = sem("lanes_done")
        spread_done = sem("spread_done")
        ln_norm_done = sem("ln_norm_done")
        ln_norm_turned = sem("ln_norm_turned")
        lane_norm_ready = sem("lane_norm_ready")
        lane_norm_done = sem("lane_norm_done")
        ctx_norm_done = sem("ctx_norm_done")
        border_set = sem("border_set")
        pads_set = sem("pads_set")
        prod_ready = sem("prod_ready")
        picked_done = sem("picked_done")
        summed = sem("summed")
        clamped = sem("clamped")
        skewed = [[sem(f"skewed{m}_{j}") for j in range(0, NP, TOGETHER[m])] for m in range(NC)]
        raw_loaded = [sem(f"raw_loaded{i}") for i in range(2)]
        is_left_done = sem("is_left_done")
        no_up_done = sem("no_up_done")
        ends_picked = sem("ends_picked")
        offers_done = sem("offers_done")
        offers_ready = sem("offers_ready")
        forced_done = sem("forced_done")
        leave_parts = sem("leave_parts")
        leave_done = sem("leave_done")
        on_path_done = sem("on_path_done")
        raw_hi_done = sem("raw_hi_done")
        raw_scaled = sem("raw_scaled")
        raw_lo_done = sem("raw_lo_done")
        router_loaded = sem("router_loaded")
        zeros_set = sem("zeros_set")
        slots_zeroed = sem("slots_zeroed")
        bn2_done = sem("bn2_done")
        std2_done = sem("std2_done")
        yn_done = sem("yn_done")
        msq_done = sem("msq_done")
        rms_done = sem("rms_done")
        y_hi_done = sem("y_hi_done")
        y_lo_done = sem("y_lo_done")
        y_lo_pool = sem("y_lo_pool")
        yT_ready = sem("yT_ready")
        yT_moved_act = sem("yT_moved_act")
        yT_moved_dve = sem("yT_moved_dve")
        rw_hi_done = sem("rw_hi_done")
        rw_lo_done = sem("rw_lo_done")
        logits_ready = sem("logits_ready")
        shifted = sem("shifted")
        exp_done = sem("exp_done")
        totals_done = sem("totals_done")
        base_ready = sem("base_ready")
        to_slot_done = sem("to_slot_done")
        scattered = sem("scattered")
        ex_raw_loaded = [sem(f"ex_raw_loaded{i}") for i in range(2)]
        ex_hi_done = sem("ex_hi_done")
        ex_lo_done = sem("ex_lo_done")
        ex_in_loaded = sem("ex_in_loaded")
        exT_ready = sem("exT_ready")
        exT_moved_act = sem("exT_moved_act")
        exT_moved_dve = sem("exT_moved_dve")
        gu_ready = sem("gu_ready")
        silu_done = sem("silu_done")
        gated_done = sem("gated_done")
        act_hi_done = sem("act_hi_done")
        act_lo_done = sem("act_lo_done")
        down_done = sem("down_done")
        ex_out_moved = sem("ex_out_moved")
        ex_stored = sem("ex_stored")
        shared_added = sem("shared_added")
        from_slot_done = sem("from_slot_done")
        gathered = [sem(f"gathered{g}") for g in range(NG)]
        routed_added = sem("routed_added")

        block = stack.enter_context(nc.Block())

        class Count:

            def __init__(self, semaphore):
                self.semaphore, self.n = semaphore, 0

            def link(self, eng, instruction):
                self.n += 1
                instruction.then_inc(self.semaphore, 1)
                eng.wait_ge(self.semaphore, self.n)

            def mark(self, instruction):
                self.n += 1
                instruction.then_inc(self.semaphore, 1)
                return self.n

        def store_expert(sp, e):
            full = sum(n == P for _, n in TILES_E)
            r = e * CAP
            sp.wait_ge(ex_out_moved, 2 * (e + 1))
            sp.dma_start(ex_rows[r:r + full * P, :].rearrange("(m p) h -> p m h", p=P),
                         ex_out[:, e % 2, 0:full, :]).then_inc(ex_stored, 16)
            m, n = TILES_E[full]
            for c in range(2):
                sp.dma_start(ex_rows[r + m:r + m + n, c * P:(c + 1) * P],
                             ex_out[c * n:(c + 1) * n, e % 2, full, 0:P]).then_inc(ex_stored, 16)

        def raw_piece(n):
            m, r = divmod(n, 4)
            if m == 2:
                return sd[4 * r * P:4 * (r + 1) * P, :].rearrange("(i p) h -> p i h", p=P)
            k, half = divmod(r, 2)
            return (sg, su)[m][k * P:(k + 1) * P, half * PIECE:(half + 1) * PIECE]

        def split_piece(n, z):
            m, r = divmod(n, 4)
            if m == 2:
                return down16[:, z, 4 * r:4 * (r + 1), :].rearrange("p i h -> p (i h)")
            k, half = divmod(r, 2)
            return gu16[:, m, z, k, half * PIECE:(half + 1) * PIECE]

        def group_of_bank(n):
            g, c = divmod(n, 2)
            return NW - 1 - g, c

        PAIRS = [g * WG // 2 + c for g in ORDER for c in range(WG // 2)]
        GROUPS_FOR = [NW - 1] * (W // 4) + [NW] * (W // 4)

        def half(t, h):
            return t.rearrange("p (g w) -> p g w", g=NG)[:, slice(1, 3) if h == 0 else slice(0, NG, NG - 1), :]

        @block.sync
        def _(sp):
            sp.dma_start(X[:, :, :], x.rearrange("b (l w) h -> (b l) w h", w=W)).then_inc(x_loaded, 16)
            sp.dma_start(ctx_rows, folded.rearrange("b d (c p) h -> p (b d c) h", p=P)).then_inc(ctx_loaded, 16)
            for n, g in enumerate((g_xattn, g_ffn)):
                sp.dma_start(gates[:, n:n + 1], g.partition_broadcast(P)).then_inc(small_loaded, 16)
            for k in range(KC):
                sp.dma_start(rw[:, k, :], router_w[:, k * P:(k + 1) * P].rearrange("e p -> p e"),
                             allow_slow_non_contiguous=True).then_inc(router_loaded, 16)
            for m in range(NC):
                sp.wait_ge(dist_done, PARTS_TO[m])
                if m == 0:
                    sp.wait_ge(pads_set, 3)
                    sp.wait_ge(border_set, 1)
                for j in range(NP):
                    r = 2 + ROW_0[m] + SKEW * j
                    sp.dma_start(table[j:P:NP, r:r + ROWS[m], :], dist[j:P:NP, m % 2, 0:ROWS[m], :]).then_inc(
                        skewed[m][j // TOGETHER[m]], 16)
            sp.wait_ge(dist_done, len(PARTS))
            def load_piece(n):
                if n >= 2:
                    sp.wait_ge(raw_lo_done, n - 1)
                sp.dma_start(raw[:, n % 2, :] if n < 8 else raw[:, n % 2, :].rearrange("p (i h) -> p i h", h=H),
                             raw_piece(n)).then_inc(raw_loaded[n % 2], 16)

            for n in SPLIT_EARLY:
                load_piece(n)
            sp.wait_ge(zeros_set, 1)
            for n in range(E * CAP // P):
                sp.dma_start(slots[n * P:(n + 1) * P, :], zeros.bitcast(F16)).then_inc(slots_zeroed, 16)
            for n in range(len(SPLIT_EARLY), 12):
                load_piece(n)

            def load_expert(u):
                e, m = divmod(u, 3)
                src = (rg[e], ru[e], rd[e])[m].rearrange("(k p) i -> p k i", p=P)
                sp.dma_start(ex_raw[u % 2].rearrange("p (k i) -> p k i", k=src.shape[1]), src).then_inc(ex_raw_loaded[u % 2], 16)

            sp.wait_ge(pathT_ready, 2 * NW)
            load_expert(0)
            sp.wait_ge(x2_done, W // 2)
            load_expert(1)
            tiles_full = sum(n == P for _, n in TILES_E)
            sp.wait_ge(ex_lo_done, KC)
            load_expert(2)
            sp.wait_ge(scattered, 16 * 2 * W)
            for e in range(E):
                if e:
                    sp.wait_ge(exT_ready, 2 * e)
                r = e * CAP
                sp.dma_start(ex_in[:, 0:tiles_full, :, :], slots[r:r + tiles_full * P, :].rearrange(
                    "(m p) (z h) -> p m z h", p=P, z=2)).then_inc(ex_in_loaded, 16)
                for m, n in TILES_E[tiles_full:]:
                    sp.dma_start(ex_in[0:n, m // P, :, :], slots[r + m:r + m + n, :].rearrange(
                        "p (z h) -> p z h", z=2)).then_inc(ex_in_loaded, 16)
                for u in range(max(3 * e + 2, 3), min(3 * e + 5, 3 * E)):
                    sp.wait_ge(ex_lo_done, (u - 1) * KC)
                    load_expert(u)
                if e:
                    store_expert(sp, e - 1)
            store_expert(sp, E - 1)
            outs = out.rearrange("b (l w) h -> (b l) w h", w=W)
            for k, g in enumerate(ORDER):
                sp.wait_ge(shared_added, 2 * (k + 1))
                sp.wait_ge(routed_added, 2 * WG * (k + 1))
                sp.dma_start(outs[:, g * WG:(g + 1) * WG, :], X[:, g * WG:(g + 1) * WG, :]).then_inc(stored, 16)
            sp.wait_ge(stored, 16 * NG)

        @block.gpsimd
        def _(pool):
            pool.memset(zeros, 0.0).then_inc(zeros_set, 1)
            pool.memset(ident[:, :], 0.0).then_inc(consts, 1)
            pool.memset(ident16[:, :], 0.0).then_inc(consts, 1)
            pool.memset(ones[:, :], 1.0).then_inc(consts, 1)
            pool.memset(ln_eps[:, :], LN_EPS).then_inc(consts, 1)
            pool.memset(same_batch[:, :], 0.0).then_inc(consts, 1)
            pool.iota(iota[:, :], [[1, S]], base=0, channel_multiplier=0,
                      allow_small_or_imprecise_dtypes=True).then_inc(consts, 1)
            pool.wait_ge(consts, 6)
            pool.tensor_scalar(iota_less[:, :], iota[:, :], 0.5, None, ALU.subtract).then_inc(consts, 1)
            for m in (ident, ident16):
                pool.affine_select(out=m[:, :], in_=m[:, :], compare_op=ALU.not_equal, fill=1.0,
                                   base=0, pattern=[[-1, P]], channel_multiplier=1).then_inc(consts, 1)
            for b in range(B):
                pool.wait_ge(consts, 9 + b)
                pool.memset(same_batch[NJ * b:NJ * (b + 1), NJ * b:NJ * (b + 1)], 1.0).then_inc(consts, 1)
            pool.wait_ge(consts, 13)
            for n in range(KC * B):
                b, k = divmod(n, KC)
                s = slice(b * SEQ, (b + 1) * SEQ)
                pool.wait_ge(ctxT_moved, n + 1)
                pool.tensor_tensor(ctx_sq[:, k, s], ctxT[:, k, s], ctxT[:, k, s], ALU.mult).then_inc(sq_done, 1)
            pool.wait_ge(lnT_ready, KC * W // 4)
            pool.wait_ge(ln_norm_done, W)
            pool.wait_ge(lane_norm_ready, 1)
            pool.memset(region_e[:, 0:(SKEW * (NP - 1) + 2) * CW], 0.0).then_inc(pads_set, 1)
            pool.memset(region_e[:, (HALF + 2) * CW:(S + 2) * CW], 0.0).then_inc(pads_set, 1)
            pool.wait_ge(pads_set, 2)
            pool.memset(table[:, 0, 0:1], BIG).then_inc(pads_set, 1)
            pool.wait_ge(norm_ready, 1)
            pool.memset(cost[:, 0, 1:CW], BIG).then_inc(top_set, 1)
            pool.wait_ge(lane_norm_done, 1)
            pool.wait_ge(ctx_norm_done, 2)
            n_sum = 0
            for n, (m, q) in enumerate(PARTS):
                V, R = PER_BANK[m], ROWS[m]
                both = picked[:, n % 2, :, :]
                total = both[:, 0, :].rearrange("p (w i) -> p w i", w=V)
                pool.wait_ge(picked_done, 2 * (n + 1))
                for part in (both[:, 1, :].rearrange("p (w i) -> p w i", w=V),
                             lane_norm[:, V * q:V * (q + 1)].unsqueeze(2).broadcast_to((P, V, R)),
                             ctx_norm[:, ROW_0[m]:ROW_0[m] + R].unsqueeze(1).broadcast_to((P, V, R))):
                    if n_sum % 3:
                        pool.wait_ge(summed, n_sum)
                    pool.tensor_tensor(total, total, part, ALU.add).then_inc(summed, 1)
                    n_sum += 1
            def low_halves(pieces):
                for n in pieces:
                    pool.wait_ge(raw_scaled, n + 1)
                    pool.tensor_tensor(split_piece(n, 1), raw[:, n % 2, :], split_piece(n, 0), ALU.subtract).then_inc(raw_lo_done, 1)

            low_halves(SPLIT_EARLY)
            pool.memset(earlier[:, :], 1.0).then_inc(consts, 1)
            pool.memset(rms_eps[:, :], RMS_EPS).then_inc(consts, 1)
            pool.memset(goes_on[:, :, :], 1.0).then_inc(consts, 1)
            pool.iota(key_of[:, :, :], [[-1, E], [0, W]], base=E, channel_multiplier=0,
                      allow_small_or_imprecise_dtypes=True).then_inc(consts, 1)
            pool.iota(slot_of[:, :, :], [[CAP, E], [0, W]], base=0, channel_multiplier=0,
                      allow_small_or_imprecise_dtypes=True).then_inc(consts, 1)
            pool.wait_ge(consts, 18)
            pool.memset(goes_on[:, :, 0:1], 0.0).then_inc(consts, 1)
            pool.affine_select(out=earlier[:, :], in_=earlier[:, :], compare_op=ALU.is_gt, fill=0.0,
                               base=0, pattern=[[1, P]], channel_multiplier=-1).then_inc(consts, 1)
            pool.wait_ge(is_left_done, N_MASKS)
            pool.wait_ge(no_up_done, 1)
            pool.wait_ge(ends_picked, 1)
            for w in range(BW):
                pool.tensor_tensor(leave[:, w, :], is_left[:, w, :], iota[:, :], ALU.mult).then_inc(leave_parts, 1)
                pool.tensor_tensor(leave_b[:, w, :], no_up[:, w, :], iota_less[:, :], ALU.mult).then_inc(leave_parts, 1)
            for b in range(B):
                pool.wait_ge(ctx_hi_done, b + 1)
                s = slice(b * NI, (b + 1) * NI)
                pool.tensor_tensor(ctx16[:, 1, s, :], ctx_rows[:, s, :], ctx16[:, 0, s, :],
                                   ALU.subtract).then_inc(ctx_lo_done, 1)
            low_halves((*SPLIT_BEFORE, *SPLIT_AT_END))
            for n in range(2):
                s = slice(ORDER[n] * WG, (ORDER[n] + 1) * WG)
                pool.wait_ge(y_hi_done, n + 1)
                pool.wait_ge(yn_done, (n + 1) * WG)
                pool.tensor_tensor(y16[:, s, 1, :], yn[:, s, :], y16[:, s, 0, :], ALU.subtract).then_inc(y_lo_pool, 1)
            low_halves(split_beside.values())
            pool.wait_ge(slots_zeroed, 16 * (E * CAP // P))
            pool.wait_ge(y_lo_done, 2)
            pool.wait_ge(y_lo_pool, 2)
            pool.wait_ge(y_hi_done, NG)
            pool.wait_ge(to_slot_done, 1)
            for w in range(W):
                for k in range(2):
                    pool.indirect_dma_start(slots, bass.IndirectOffsetOnAxis(ap=to_slot[:, k, w:w + 1], axis=0),
                                            y16[:, w, :, :].rearrange("p z h -> p (z h)"), None,
                                            bounds_check=E * CAP - 1, oob_is_err=False).then_inc(scattered, 16)
            pool.wait_ge(from_slot_done, 1)
            pool.wait_ge(ex_stored, EX_STORES * E)
            pool.wait_ge(down_done, FIRST_CHUNK[E + 2])
            pool.wait_ge(ex_lo_done, E * PIECES)
            for w in (g * WG + c for g in ORDER for c in range(WG)):
                for k in range(2):
                    pool.indirect_dma_start(gathered_rows[:, w, k, :], None, ex_rows,
                                            bass.IndirectOffsetOnAxis(ap=from_slot[:, k, w:w + 1], axis=0),
                                            bounds_check=E * CAP - 1, oob_is_err=False).then_inc(gathered[w // WG], 16)

        @block.scalar
        def _(act):
            def move_yT(n):
                act.wait_ge(yT_ready, 2 * n + 1)
                act.activation(yT[:, ORDER[n], 0, :, :], bank[6][:, :].bitcast(F16).rearrange("p (k n) -> p k n", k=KC),
                               ACT.Copy).then_inc(yT_moved_act, 1)

            def move_pathT(g):
                for n in (2 * g, 2 * g + 1):
                    q, c = group_of_bank(n)
                    f, v = divmod(WQ * q, W)
                    src = bank[n % 4][:, :].rearrange("p (w b l) -> p w b l", w=WQ, b=B)
                    act.wait_ge(pathT_ready, n + 1)
                    act.activation(pathT[:, c, v:v + WQ, :, f:NJ:2], src[:, :, :, 0:NP], ACT.Copy).then_inc(pathT_moved, 1)
                    act.activation(pathT[:, 2 + c, W - WQ - v:W - v, :, 1 - f:NJ:2], src[:, ::-1, :, NJ - 1:NP - 1:-1],
                                   ACT.Copy).then_inc(pathT_moved, 1)

            def move_ctxT(n):
                b, k = divmod(n, KC)
                act.wait_ge(ctxT_ready, n + 1)
                act.activation(ctxT[:, k, b * SEQ:(b + 1) * SEQ], bank[n % 4][:, :], ACT.Copy).then_inc(ctxT_moved, 1)

            act.wait_ge(consts, 4)
            act.wait_ge(bn_done, 1)
            act.activation(rstd[:, 0, :], mv[:, :, 1], ACT.Sqrt, bias=ln_eps[:, 0:1]).then_inc(std_done, 1)
            for n in range(KC * B):
                move_ctxT(n)
            for n in range(KC * W // 4):
                q, k = divmod(n, KC)
                act.wait_ge(lnT_ready, n + 1)
                for f in range(2):
                    w = W * f + 4 * q
                    act.activation(lnT[:, k, w:w + 4, :, 0:NP],
                                   bank[4 + n % 4][:, :].rearrange("p (w b j f) -> p f w b j", w=4, b=B, f=2)[:, f],
                                   ACT.Copy, scale=-2.0).then_inc(lnT_moved_act, 1)
            act.wait_ge(ln1_done, W)
            for w in range(W):
                if w >= 2:
                    act.wait_ge(ln_norm_done, w - 1)
                act.activation(sq_dump[:, w % 2, :], ln1[:, w, :], ACT.Square,
                               accum_out=ln_norm[:, 0, w:w + 1]).then_inc(ln_norm_done, 1)
            act.wait_ge(lanes_done, 1)
            for n in range(len(PARTS) + 1):
                if n < len(PARTS):
                    V = PER_BANK[PARTS[n][0]]
                    act.wait_ge(prod_ready, n + 1)
                    if n >= 2:
                        act.wait_ge(clamped, n - 1)
                        act.wait_ge(dist_done, n - 1)
                    for d, mine in enumerate((chain0, chain1)):
                        act.activation(picked[:, n % 2, d, :].rearrange("p (w i) -> p w i", w=V),
                                       bank[1 + n % 3][:, :].rearrange("p (w d i) -> p d w i", w=V, d=2)[:, d],
                                       ACT.Copy, scale=mine).then_inc(picked_done, 1)
                if n:
                    r = n - 1
                    m, q = PARTS[r]
                    V = PER_BANK[m]
                    act.wait_ge(summed, 3 * n)
                    act.activation(picked[:, r % 2, 0, :], picked[:, r % 2, 0, :], ACT.Relu).then_inc(clamped, 1)
                    act.wait_ge(clamped, n)
                    if q == 0 and m >= 2:
                        for moved in skewed[m - 2]:
                            act.wait_ge(moved, 16 * TOGETHER[m - 2])
                    act.activation(dist[:, m % 2, 0:ROWS[m], 1 + V * q:1 + V * (q + 1)].rearrange("p i w -> p w i"),
                                   picked[:, r % 2, 0, :].rearrange("p (w i) -> p w i", w=V), ACT.Sqrt).then_inc(dist_done, 1)
            def high_halves(pieces):
                for n in pieces:
                    act.wait_ge(raw_loaded[n % 2], 16 * (n // 2 + 1))
                    act.activation(split_piece(n, 0), raw[:, n % 2, :], ACT.Copy, scale=W_SCALE).then_inc(raw_hi_done, 1)
                    act.wait_ge(raw_hi_done, n + 1)
                    act.activation(raw[:, n % 2, :], raw[:, n % 2, :], ACT.Copy, scale=W_SCALE).then_inc(raw_scaled, 1)

            high_halves(SPLIT_EARLY)
            act.wait_ge(router_loaded, 16 * KC)
            act.activation(rw16[:, 0, :, :], rw[:, :, :], ACT.Copy, scale=W_SCALE).then_inc(rw_hi_done, 1)
            act.wait_ge(small_loaded, 32)
            act.activation(tanhs[:, :], gates[:, :], ACT.Tanh).then_inc(tanh_done, 1)
            act.wait_ge(is_left_done, N_MASKS)
            act.wait_ge(no_up_done, 1)
            act.wait_ge(ends_picked, 1)
            for b in range(B):
                s = slice(b * NI, (b + 1) * NI)
                act.activation(ctx16[:, 0, s, :], ctx_rows[:, s, :], ACT.Copy).then_inc(ctx_hi_done, 1)
            act.wait_ge(leave_done, 1)
            high_halves(SPLIT_BEFORE)
            for g in range(NW - 1):
                move_pathT(g)
            high_halves(SPLIT_AT_END)
            move_pathT(NW - 1)

            for h in range(2):
                if h:
                    for n in range(2):
                        move_yT(n)
                act.wait_ge(bn2_done, h + 1)
                act.activation(half(rstd[:, 0, :], h), half(mv[:, :, 1], h), ACT.Sqrt, bias=ln_eps[:, 0:1]).then_inc(std2_done, 1)
                for n in (2 * h, 2 * h + 1):
                    s = slice(ORDER[n] * WG, (ORDER[n] + 1) * WG)
                    act.wait_ge(yn_done, (n + 1) * WG)
                    act.activation(y16[:, s, 0, :], yn[:, s, :], ACT.Copy).then_inc(y_hi_done, 1)
            act.wait_ge(msq_done, 1)
            act.activation(msq[:, 1, :], msq[:, 0, :], ACT.Sqrt, scale=1.0 / Y_SCALE ** 2, bias=rms_eps[:, 0:1]).then_inc(rms_done, 1)

            for q in range(NCH + 1):
                if q < NCH:
                    n, kind, i, c = CHUNKS[q]
                    cols = GT if kind == "shared" else CAP
                    act.wait_ge(gu_ready, q + 1)
                    if q >= 2:
                        act.wait_ge(gated_done, q - 1)
                    act.activation(gated[q % 2][:, 0:cols], bank[q % 2][:, 0:cols], ACT.Silu,
                                   scale=1.0 / (Y_SCALE * W_SCALE)).then_inc(silu_done, 1)
                if q >= 1:
                    r = q - 1
                    cols = GT if CHUNKS[r][1] == "shared" else CAP
                    act.wait_ge(gated_done, q)
                    if r >= 4:
                        act.wait_ge(down_done, r - 3)
                    act.activation(act16[:, r % 4, 0, 0:cols], act32[r % 2][:, 0:cols], ACT.Copy).then_inc(act_hi_done, 1)
                if q in split_beside:
                    high_halves((split_beside[q],))
                if q == LATE_TURN:
                    for n in range(2, NG):
                        move_yT(n)
                if q == ROUTER_FROM:
                    act.wait_ge(shifted, 1)
                    act.activation(probs[:, :, :], probs[:, :, :], ACT.Exp).then_inc(exp_done, 1)
                for e, j in split_at.get(q, ()):
                    u, k = divmod(j, KC)
                    m = 3 * e + u
                    act.wait_ge(ex_raw_loaded[m % 2], 16 * (m // 2 + 1))
                    if e >= 2:
                        act.wait_ge(down_done, FIRST_CHUNK[e + 1])
                    if e == 1:
                        act.wait_ge(scattered, 16 * 2 * W)
                    act.activation(ex_gu[e % 2][:, 0, j * PIECE:(j + 1) * PIECE],
                                   ex_raw[m % 2][:, k * PIECE:(k + 1) * PIECE], ACT.Copy,
                                   scale=W_SCALE).then_inc(ex_hi_done, 1)
                if q in turn_at:
                    e = turn_at[q]
                    act.wait_ge(exT_ready, 2 * e + 1)
                    act.activation(exT[:, e % 2, 0:KC, :], bank[6][:, :].bitcast(F16)[:, 0:KC * CAP].rearrange(
                        "p (k n) -> p k n", k=KC), ACT.Copy).then_inc(exT_moved_act, 1)
                job = next((n for n in range(len(JOBS)) if FIRST_CHUNK[n + 1] + LAG - 1 == q), None)
                if job is not None and JOBS[job][0] == "expert":
                    e = JOBS[job][1]
                    act.wait_ge(down_done, FIRST_CHUNK[job + 1])
                    if e >= 2:
                        act.wait_ge(ex_stored, EX_STORES * (e - 1))
                    act.activation(ex_out[:, e % 2, 0:2, :], bank[4][:, :].rearrange("p (m h) -> p m h", m=2),
                                   ACT.Copy).then_inc(ex_out_moved, 1)
                    act.activation(ex_out[:, e % 2, 2, 0:P], bank[5][:, 0:P], ACT.Copy).then_inc(ex_out_moved, 1)

        @block.vector
        def _(dve):
            step = Count(dve_step)

            def link(instruction):
                step.link(dve, instruction)

            dve.wait_ge(consts, 13)
            link(nc.vector.tensor_reduce(lane_of[:, :], ident[:, :].rearrange("p (b l) -> p l b", b=B), AX_X, ALU.add))
            link(nc.vector.tensor_tensor(at_pos[:, :], lane_of[:, 0:NP], lane_of[:, NP:NJ], ALU.add))
            link(nc.vector.tensor_tensor(offers[:, 0, :], at_pos[:, :], iota[:, 0:NP], ALU.mult))
            link(nc.vector.tensor_reduce(pos, offers[:, 0, :], AX_X, ALU.add))
            for dst, src, a, b2 in ((shift, pos, float(SKEW), 0.0), (border, at_pos[:, 0:1], BIG, 0.0),
                                    (no_next, lane_of[:, NP - 1:NP], BIG, 0.0), (base_col, pos, float(BW), 0.0),
                                    (last_row, pos, float(SKEW), float(HALF - 1)),
                                    (nat_col, pos, float(BW), 0.0)):
                step.mark(nc.vector.tensor_scalar(dst, src, a, b2, ALU.mult, ALU.add))
            step.mark(nc.vector.tensor_reduce(chain0, lane_of[:, 0:NP], AX_X, ALU.add))
            step.mark(nc.vector.tensor_reduce(chain1, lane_of[:, NP:NJ], AX_X, ALU.add))
            dve.wait_ge(dve_step, step.n)
            nc.vector.tensor_scalar(chain_col[:, :], iota[:, 0:BW], base_col, None, ALU.add).then_inc(lanes_done, 1)
            step.mark(nc.vector.tensor_scalar(iota_skew[:, :], iota[:, :], float(SKEW), None, ALU.add))
            step.mark(nc.vector.tensor_scalar(iota_row[:, :], iota[:, 0:HALF], shift, None, ALU.add))
            step.mark(nc.vector.tensor_scalar(minus_ident16[:, :], ident16[:, :], -1.0, None, ALU.mult))
            step.mark(nc.vector.tensor_scalar(at_last[:, :], at_pos[:, :], last_row, None, ALU.mult))
            nc.vector.tensor_scalar(dist[:, :, :, 0].rearrange("p m i -> p (m i)"), iota[:, 0:2 * RC], 0.0, border,
                                    ALU.is_ge, ALU.mult).then_inc(border_set, 1)
            dve.wait_ge(x_loaded, 16)
            for w in range(W):
                last = step.mark(nc.vector.bn_stats(bn[:, w, :], X[:, w, :]))
            dve.wait_ge(dve_step, last)
            for w in range(W - 1):
                last = step.mark(nc.vector.bn_aggr(mv[:, w, :], bn[:, w, :]))
            dve.wait_ge(dve_step, last)
            nc.vector.bn_aggr(mv[:, W - 1, :], bn[:, W - 1, :]).then_inc(bn_done, 1)
            dve.wait_ge(std_done, 1)
            link(nc.vector.reciprocal(rstd[:, 1, :], rstd[:, 0, :]))
            for w in range(W):
                nc.vector.tensor_scalar(ln1[:, w, :], X[:, w, :], mv[:, w, 0:1], rstd[:, 1, w:w + 1],
                                        ALU.subtract, ALU.mult).then_inc(ln1_done, 1)
            link(nc.vector.memset(spread, 0.0))
            for f in range(2):
                cols = ident[:, :].rearrange("p (b j) -> p b j", b=B)
                step.mark(nc.vector.tensor_copy(spread[:, 0, f, :].rearrange("p (b l) -> p b l", b=B)[:, :, 0:NP],
                                                cols[:, :, f:NJ:2]))
                nc.vector.tensor_copy(spread[:, 1, f, :].rearrange("p (b l) -> p b l", b=B)[:, :, NP:NJ],
                                      cols[:, :, NJ - 1 - f::-2]).then_inc(spread_done, 1)
            for n in range(KC * W // 4):
                q, k = divmod(n, KC)
                dve.wait_ge(lnT_moved_act, 2 * (n + 1))
                dve.wait_ge(lnT_ready, n + 1)
                for f in range(2):
                    w = W * f + W - 4 - 4 * q
                    src = bank[4 + n % 4][:, :].rearrange("p (w b j) -> p w b j", w=4, b=B)
                    nc.vector.tensor_scalar(lnT[:, k, w:w + 4, :, NP:NJ], src[:, ::-1, :, NJ - 1 - f::-2],
                                            -2.0, None, ALU.mult).then_inc(lnT_moved_dve, 1)
            dve.wait_ge(ln_norm_done, W)
            nc.vector.tensor_copy(ln_norm[:, 1, :], ln_norm[:, 0, ::-1]).then_inc(ln_norm_turned, 1)
            dve.wait_ge(norm_ready, 1)
            nc.vector.tensor_scalar(ctx_norm[:, :], bank[0][:, 0:HALF], chain0, None, ALU.mult).then_inc(ctx_norm_done, 1)
            dve.wait_ge(ctx_norm_done, 1)
            nc.vector.scalar_tensor_tensor(out=ctx_norm[:, :], in0=bank[0][:, HALF:SEQ], scalar=chain1,
                                           in1=ctx_norm[:, :], op0=ALU.mult, op1=ALU.add).then_inc(ctx_norm_done, 1)
            dve.wait_ge(lane_norm_ready, 1)
            nc.vector.tensor_copy(lane_norm[:, :], bank[4][:, 0:BW]).then_inc(lane_norm_done, 1)
            link(nc.vector.tensor_scalar(cost[:, 0, 0:1], border, -1.0, BIG, ALU.mult, ALU.add))
            def mark_is_left(s):
                nc.vector.tensor_tensor(is_left[:, :, s:s + MASK_ROWS],
                                        cost[:, s + 1:s + MASK_ROWS + 1, 0:BW].rearrange("p s w -> p w s"),
                                        table[:, s:s + MASK_ROWS, 1:CW].rearrange("p s w -> p w s"),
                                        ALU.is_lt).then_inc(is_left_done, 1)

            dve.wait_ge(top_set, 1)
            to_next = [l - (l % NP > 0) for l in range(NJ)]
            for s in range(S):
                for m in range(NC):
                    j, odd = divmod(s - ROW_0[m], SKEW * TOGETHER[m])
                    if not odd and 0 <= j < len(skewed[m]):
                        dve.wait_ge(skewed[m][j], 16 * TOGETHER[m])
                if s:
                    dve.wait_ge(scan_done, s)
                nc.vector.tensor_tensor(table[:, s, 1:CW], cost[:, s, 1:CW], cost[:, s, 0:BW],
                                        ALU.min).then_inc(min_done, 1)
                if s == MASK_FROM:
                    dve.wait_ge(prod_ready, len(PARTS))
                if s >= MASK_FROM:
                    mark_is_left(MASK_ROWS * (s - MASK_FROM))
                dve.wait_ge(min_done, s + 1)
                if s:
                    dve.wait_ge(shift_done, s)
                nc.vector.tensor_tensor_scan(out=cost[:, s + 1, :], data0=table[:, s, :], data1=table[:, s + 2, :],
                                             initial=BIG, op0=ALU.min, op1=ALU.add).then_inc(scan_done, 1)
                nc.vector.stream_shuffle(table[:, s + 1, 0:1], cost[:, s, BW:CW], to_next).then_inc(shift_done, 1)
            dve.wait_ge(scan_done, S)
            dve.wait_ge(shift_done, S)
            mark_is_left(S - MASK_ROWS)
            nc.vector.tensor_tensor(end_pick[:, :, :], cost[:, HALF:HALF + SKEW * (NP - 1) + 1:SKEW, 1:CW],
                                    at_pos[:, :].unsqueeze(2).broadcast_to((P, NP, BW)), ALU.mult).then_inc(ends_picked, 1)
            nc.vector.tensor_tensor(no_up, cost[:, 0:S, 1:CW].rearrange("p s w -> p w s"),
                                    cost[:, 0:S, 0:BW].rearrange("p s w -> p w s"), ALU.is_ge).then_inc(no_up_done, 1)
            dve.wait_ge(ends_picked, 1)
            last_meet = step.mark(nc.vector.tensor_reduce(ends[:, 0, 0:BW], end_pick[:, :, :].rearrange("p s w -> p w s"),
                                                          AX_X, ALU.add))
            beside = [NJ - 1 - l if l < NP else l for l in range(NJ)]
            beside_next = [NJ - 2 - l if l < NP - 1 else l for l in range(NJ)]
            v = nc.vector

            def find_meeting(n):
                got = bank[0][:, 0:3 * NP].rearrange("p (n j) -> p n j", n=3)
                if n == 0:
                    return v.stream_shuffle(ends[:, 1, 0:BW], ends[:, 0, 0:BW], beside)
                if n == 1:
                    return v.stream_shuffle(ends[:, 2, BW:CW], ends[:, 0, BW - 1:BW], beside_next)
                if n == 2:
                    return v.tensor_copy(ends[:, 2, 0:BW], ends[:, 1, BW - 1::-1])
                if n == 3:
                    return v.tensor_scalar(ends[:, 2, BW:CW], ends[:, 2, BW:CW], no_next, None, ALU.add)
                if n == 4:
                    return v.tensor_tensor(ends[:, 3, 0:BW], ends[:, 2, 0:BW], ends[:, 2, 1:CW], ALU.min)
                if n == 5:
                    return v.tensor_tensor(ends[:, 3, 0:BW], ends[:, 3, 0:BW], ends[:, 0, 0:BW], ALU.add)
                if n == 6:
                    return v.tensor_tensor(ends[:, 4, 0:BW], ends[:, 2, 1:CW], ends[:, 2, 0:BW], ALU.is_le)
                if n == 7:
                    return v.tensor_reduce(meet[:, 0:1], ends[:, 3, 0:BW], AX_X, ALU.min)
                if n == 8:
                    return v.tensor_scalar(ends[:, 5, 0:BW], ends[:, 3, 0:BW], meet[:, 0:1], None, ALU.is_equal)
                if n == 9:
                    return v.tensor_tensor(ends[:, 5, 0:BW], ends[:, 5, 0:BW], iota[:, BW:0:-1], ALU.mult)
                if n == 10:
                    return v.tensor_reduce(meet[:, 1:2], ends[:, 5, 0:BW], AX_X, ALU.max)
                if n == 11:
                    return v.tensor_scalar(ends[:, 6, 0:BW], ends[:, 5, 0:BW], meet[:, 1:2], None, ALU.is_equal)
                if n == 12:
                    return v.tensor_tensor(ends[:, 6, 0:BW], ends[:, 6, 0:BW], ends[:, 4, 0:BW], ALU.mult)
                if n == 13:
                    return v.tensor_reduce(meet[:, 3:4], ends[:, 6, 0:BW], AX_X, ALU.add)
                if n == 14:
                    return v.tensor_scalar(meet[:, 2:3], meet[:, 1:2], -1.0, float(BW), ALU.mult, ALU.add)
                if n == 15:
                    return v.tensor_tensor(meet[:, 1:2], meet[:, 2:3], nat_col, ALU.add)
                if n == 16:
                    return v.tensor_tensor(meet[:, 2:3], meet[:, 1:2], meet[:, 3:4], ALU.add)
                if n in (17, 18, 19):
                    return v.tensor_scalar(offers[:, n - 17, :], lane_of[:, 0:NP], meet[:, n - 17:n - 16], None, ALU.mult)
                if n == 20:
                    dve.wait_ge(offers_ready, 1)
                    return v.tensor_reduce(meet[:, 4:5], got[:, 0, :], AX_X, ALU.min)
                if n == 21:
                    return v.tensor_scalar(offers[:, 3, :], got[:, 0, :], meet[:, 4:5], None, ALU.is_equal)
                if n == 22:
                    return v.tensor_tensor(offers[:, 3, :], offers[:, 3, :], iota[:, NP:0:-1], ALU.mult)
                if n == 23:
                    return v.tensor_reduce(meet[:, 5:6], offers[:, 3, :], AX_X, ALU.max)
                if n == 24:
                    return v.tensor_scalar(offers[:, 3, :], offers[:, 3, :], meet[:, 5:6], None, ALU.is_equal)
                if n in (25, 27):
                    m = (n - 23) // 2
                    return v.tensor_tensor(offers[:, m, :], got[:, m, :], offers[:, 3, :], ALU.mult)
                if n in (26, 28):
                    m = (n - 24) // 2
                    return v.tensor_reduce(meet[:, 5 + m:6 + m], offers[:, m, :], AX_X, ALU.add)
                if n == 29:
                    return v.tensor_scalar(meet[:, 8:9], meet[:, 7:8], -1.0, float(SEQ - 1), ALU.mult, ALU.add)
                if n == 30:
                    return v.tensor_tensor(meet[:, 8:9], meet[:, 8:9], chain1, ALU.mult)
                return v.scalar_tensor_tensor(out=meet[:, 9:10], in0=meet[:, 6:7], scalar=chain0, in1=meet[:, 8:9],
                                              op0=ALU.mult, op1=ALU.add)

            def keep_last(w):
                return step.mark(v.tensor_copy(last_back[:, w, :], back[:, (w + 1) % 2, HALF:HALF + SKEW * (NP - 1) + 1:SKEW]))

            step.mark(v.memset(back[:, :, 0:1], 0.0))
            link(v.tensor_copy(back[:, 0, 1:S + 1], iota[:, :]))
            dve.wait_ge(no_up_done, 1)
            dve.wait_ge(is_left_done, N_MASKS)
            for w in range(BW):
                a = w % 2
                step.mark(v.tensor_tensor(pick[:, 0, :], no_up[:, w, :], back[:, a, 0:S], ALU.mult))
                picks = step.mark(v.tensor_tensor(pick[:, 1, :], is_left[:, w, :], back[:, a, 1:S + 1], ALU.mult))
                if w:
                    keep_last(w - 1)
                dve.wait_ge(dve_step, picks)
                composed = step.mark(v.tensor_tensor_scan(out=back[:, 1 - a, 1:S + 1], data0=pick[:, 0, :], data1=pick[:, 1, :],
                                                          initial=0.0, op0=ALU.max, op1=ALU.max))
                dve.wait_ge(dve_step, last_meet)
                if w == 19:
                    find_meeting(w).then_inc(offers_done, 1)
                else:
                    last_meet = step.mark(find_meeting(w))
                dve.wait_ge(dve_step, composed)
            keep_last(BW - 1)
            dve.wait_ge(dve_step, last_meet)
            for n, (op, by) in enumerate(((ALU.is_gt, 1.0), (ALU.is_gt, BIG_ROW), (ALU.is_equal, 1.0))):
                step.mark(v.tensor_scalar(outside[:, n, :], chain_col[:, :], meet[:, 9:10], by, op, ALU.mult))
            link(v.tensor_scalar(meet[:, 10:11], chain_col[:, BW - 1:BW], meet[:, 9:10], last_row, ALU.is_ge, ALU.mult))
            step.mark(v.tensor_reduce(meet[:, 11:12], outside[:, 2, :], AX_X, ALU.max))
            step.mark(v.tensor_scalar(meet[:, 14:15], meet[:, 10:11], 0.0, None, ALU.is_equal))
            link(v.tensor_tensor(at_meet[:, :, :], outside[:, 2, :].unsqueeze(2).broadcast_to((P, BW, NP)),
                                 at_pos[:, :].unsqueeze(1).broadcast_to((P, BW, NP)), ALU.mult))
            link(v.tensor_scalar(meet[:, 13:14], meet[:, 11:12], -1.0, 1.0, ALU.mult, ALU.add))
            step.mark(v.tensor_tensor(meet[:, 13:14], meet[:, 13:14], meet[:, 10:11], ALU.mult))
            link(v.tensor_tensor_reduce(out=at_meet[:, :, :].rearrange("p w j -> p (w j)"),
                                        in0=last_back[:, :, :].rearrange("p w j -> p (w j)"),
                                        in1=at_meet[:, :, :].rearrange("p w j -> p (w j)"), scale=1.0,
                                        scalar=0.0, op0=ALU.mult, op1=ALU.max, accum_out=meet[:, 12:13]))
            link(v.tensor_tensor(meet[:, 12:13], meet[:, 12:13], meet[:, 13:14], ALU.add))
            step.mark(v.tensor_copy(entry[:, :], last_row))
            link(v.tensor_scalar(back[:, 0, 1:S + 1], back[:, 0, 1:S + 1], meet[:, 14:15], meet[:, 12:13], ALU.mult, ALU.add))
            to_before = [l + (l % NP < NP - 1) for l in range(NJ)]
            def latest(w, to):
                dve.wait_ge(leave_parts, 2 * to)
                return step.mark(v.tensor_tensor(leave[:, w:to, :], leave[:, w:to, :], leave_b[:, w:to, :], ALU.max))

            for j in range(NP - 1):
                last = step.mark(v.scalar_tensor_tensor(out=pick[:, 0, :], in0=iota_skew[:, :], scalar=entry[:, 0:1],
                                            in1=back[:, 0, 1:S + 1], op0=ALU.is_equal, op1=ALU.mult,
                                            accum_out=left_of[:, 0:1]))
                latest(2 * j, 2 * j + 2)
                dve.wait_ge(dve_step, last)
                link(v.stream_shuffle(entry[:, :], left_of[:, 0:1], to_before))
            link(v.tensor_scalar(entry[:, :], entry[:, :], float(SKEW), None, ALU.subtract))
            link(v.tensor_scalar(leave_at[:, BW:BW + 1], entry[:, :], meet[:, 14:15], meet[:, 10:11], ALU.mult, ALU.add))
            forced = end_pick[:, :, :].rearrange("p s w -> p w s")
            v.tensor_tensor(forced, outside[:, 0, :].unsqueeze(2).broadcast_to((P, BW, NP)),
                            at_last[:, :].unsqueeze(1).broadcast_to((P, BW, NP)), ALU.mult).then_inc(forced_done, 1)
            dve.wait_ge(dve_step, latest(2 * (NP - 1), BW))
            dve.wait_ge(forced_done, 1)
            last_cells = leave[:, :, HALF - 1:S:SKEW]
            v.tensor_tensor(last_cells, last_cells, forced, ALU.max).then_inc(leave_done, 1)
            dve.wait_ge(leave_done, 1)

            def mark_left(w):
                v.tensor_scalar(left[:, w, :], iota_row[:, :], left_after[:, w:w + 1], None, ALU.is_lt).then_inc(on_path_done, 1)

            def after_group(w):
                return step.mark(v.tensor_tensor(left_after[:, w:w + WQ], leave_at[:, w:w + WQ], outside[:, 1, w:w + WQ], ALU.add))

            for n, w in enumerate(reversed(range(BW))):
                upper = step.mark(v.tensor_scalar(pick[:, 1, :], iota[:, :], leave_at[:, w + 1:w + 2], None, ALU.is_le))
                v.tensor_scalar(entered[:, w, :], iota_row[:, :], leave_at[:, w + 1:w + 2], None, ALU.is_le).then_inc(on_path_done, 1)
                if n and n % WQ == 0:
                    group = after_group(w + 1)
                dve.wait_ge(dve_step, upper)
                found = step.mark(v.tensor_tensor_reduce(out=pick[:, 0, :], in0=pick[:, 1, :], in1=leave[:, w, :], scale=1.0,
                                                         scalar=0.0, op0=ALU.mult, op1=ALU.max,
                                                         accum_out=leave_at[:, w:w + 1]))
                if n >= WQ:
                    dve.wait_ge(dve_step, group)
                    mark_left(w + WQ)
                dve.wait_ge(dve_step, found)
            dve.wait_ge(dve_step, after_group(0))
            for w in reversed(range(WQ)):
                mark_left(w)
            dve.wait_ge(rw_hi_done, 1)
            nc.vector.scalar_tensor_tensor(out=rw16[:, 1, :, :], in0=rw[:, :, :], scalar=W_SCALE,
                                           in1=rw16[:, 0, :, :], op0=ALU.mult, op1=ALU.subtract).then_inc(rw_lo_done, 1)

            def normalise(h):
                dve.wait_ge(std2_done, h + 1)
                r = half(rstd[:, 1, :], h)
                link(nc.vector.reciprocal(r, half(rstd[:, 0, :], h)))
                link(nc.vector.tensor_scalar(r, r, Y_SCALE, None, ALU.mult))
                if h == 0:
                    dve.wait_ge(pathT_ready, 2 * NW - 2)
                for n in (2 * h, 2 * h + 1):
                    for w in range(ORDER[n] * WG, (ORDER[n] + 1) * WG):
                        nc.vector.tensor_scalar(yn[:, w, :], X[:, w, :], mv[:, w, 0:1], rstd[:, 1, w:w + 1],
                                                ALU.subtract, ALU.mult).then_inc(yn_done, 1)
                if h:
                    link(nc.vector.tensor_tensor(msq[:, 0, :], mv[:, :, 1], rstd[:, 1, :], ALU.mult))
                    nc.vector.tensor_tensor(msq[:, 0, :], msq[:, 0, :], rstd[:, 1, :], ALU.mult).then_inc(msq_done, 1)

            def low_half(n):
                s = slice(ORDER[n] * WG, (ORDER[n] + 1) * WG)
                dve.wait_ge(y_hi_done, n + 1)
                dve.wait_ge(yn_done, (n + 1) * WG)
                nc.vector.tensor_tensor(y16[:, s, 1, :], yn[:, s, :], y16[:, s, 0, :], ALU.subtract).then_inc(y_lo_done, 1)

            def move_yT(n):
                dve.wait_ge(yT_ready, 2 * n + 2)
                nc.vector.tensor_copy(yT[:, ORDER[n], 1, :, :], bank[7][:, :].bitcast(F16).rearrange("p (k n) -> p k n", k=KC))\
                    .then_inc(yT_moved_dve, 1)

            dve.wait_ge(tanh_done, 1)
            for m, n in enumerate(PAIRS):
                dve.wait_ge(aligned_ready, m + 1)
                nc.vector.scalar_tensor_tensor(out=X[:, 2 * n:2 * n + 2, :], in0=bank[4 + m % 4][:, :],
                                               scalar=tanhs[:, 0:1], in1=X[:, 2 * n:2 * n + 2, :],
                                               op0=ALU.mult, op1=ALU.add).then_inc(x2_done, 1)
                dve.wait_ge(x2_done, m + 1)
                for w in (2 * n, 2 * n + 1):
                    last = step.mark(nc.vector.bn_stats(bn[:, w, :], X[:, w, :]))
                dve.wait_ge(dve_step, last)
                last = step.mark(nc.vector.bn_aggr(mv[:, 2 * n, :], bn[:, 2 * n, :]))
                last = nc.vector.bn_aggr(mv[:, 2 * n + 1, :], bn[:, 2 * n + 1, :])
                if m % 4 < 3:
                    step.mark(last)
                else:
                    last.then_inc(bn2_done, 1)
                if m == 3:
                    normalise(0)
            for n in range(2):
                move_yT(n)
            normalise(1)
            for n in range(2, NG):
                low_half(n)

            by_token = "p e w -> p w e"
            all_e = (P, E, W)

            def over_e(row):
                return row.unsqueeze(1).broadcast_to(all_e)

            def route(stage):
                if stage == 0:
                    dve.wait_ge(rms_done, 1)
                    link(nc.vector.reciprocal(msq[:, 2, :], msq[:, 1, :]))
                    link(nc.vector.tensor_scalar(msq[:, 2, :], msq[:, 2, :], 1.0 / (Y_SCALE * W_SCALE), None, ALU.mult))
                    dve.wait_ge(logits_ready, 1)
                    link(nc.vector.tensor_tensor(probs[:, :, :], bank[7][:, 0:W * E].rearrange("p (w e) -> p e w", e=E),
                                                 over_e(msq[:, 2, :]), ALU.mult))
                    link(nc.vector.tensor_reduce(per_tok[:, 0, :], probs[:, :, :].rearrange(by_token), AX_X, ALU.max))
                    nc.vector.tensor_tensor(probs[:, :, :], probs[:, :, :], over_e(per_tok[:, 0, :]), ALU.subtract).then_inc(shifted, 1)
                elif stage == 1:
                    dve.wait_ge(exp_done, 1)
                    link(nc.vector.tensor_reduce(per_tok[:, 1, :], probs[:, :, :].rearrange(by_token), AX_X, ALU.add))
                    link(nc.vector.reciprocal(per_tok[:, 2, :], per_tok[:, 1, :]))
                    link(nc.vector.tensor_tensor(probs[:, :, :], probs[:, :, :], over_e(per_tok[:, 2, :]), ALU.mult))
                elif stage in (2, 3):
                    k = stage - 2
                    link(nc.vector.tensor_reduce(per_tok[:, 3 + k, :], probs[:, :, :].rearrange(by_token), AX_X, ALU.max))
                    link(nc.vector.tensor_tensor(keys[:, :, :], probs[:, :, :], over_e(per_tok[:, 3 + k, :]), ALU.is_equal))
                    link(nc.vector.tensor_tensor(keys[:, :, :], keys[:, :, :], key_of[:, :, :], ALU.mult))
                    link(nc.vector.tensor_reduce(per_tok[:, 5, :], keys[:, :, :].rearrange(by_token), AX_X, ALU.max))
                    link(nc.vector.tensor_tensor(hot[:, k, :, :], keys[:, :, :], over_e(per_tok[:, 5, :]), ALU.is_equal))
                    if stage == 2:
                        link(nc.vector.scalar_tensor_tensor(out=probs[:, :, :], in0=hot[:, 0, :, :], scalar=-2.0,
                                                            in1=probs[:, :, :], op0=ALU.mult, op1=ALU.add))
                elif stage == 4:
                    link(nc.vector.tensor_tensor(chosen[:, :, :], hot[:, 0, :, :], hot[:, 1, :, :], ALU.add))
                    link(nc.vector.tensor_tensor_scan(out=upto[:, :, :].rearrange("p e w -> p (e w)"),
                                                      data0=goes_on[:, :, :].rearrange("p e w -> p (e w)"),
                                                      data1=chosen[:, :, :].rearrange("p e w -> p (e w)"),
                                                      initial=0.0, op0=ALU.mult, op1=ALU.add))
                    nc.vector.tensor_copy(lane_total[:, 0, :], upto[:, :, W - 1]).then_inc(totals_done, 1)
                    dve.wait_ge(totals_done, 1)
                    link(nc.vector.tensor_tensor(upto[:, :, :], upto[:, :, :], chosen[:, :, :], ALU.subtract))
                elif stage == 5:
                    dve.wait_ge(base_ready, 1)
                    link(nc.vector.tensor_copy(lane_total[:, 1, :], bank[7][:, W * E:(W + 1) * E]))
                    link(nc.vector.tensor_tensor(upto[:, :, :], upto[:, :, :], lane_total[:, 1, :].unsqueeze(2).broadcast_to(all_e),
                                                 ALU.add))
                    step.mark(nc.vector.tensor_scalar(fits[:, :, :], upto[:, :, :], float(CAP), None, ALU.is_lt))
                    link(nc.vector.tensor_tensor(upto[:, :, :], upto[:, :, :], slot_of[:, :, :], ALU.add))
                elif stage == 6:
                    for k in range(2):
                        for v, row in ((fits, 6 + k), (upto, 8 + k)):
                            link(nc.vector.tensor_tensor(keys[:, :, :], hot[:, k, :, :], v[:, :, :], ALU.mult))
                            link(nc.vector.tensor_reduce(per_tok[:, row, :], keys[:, :, :].rearrange(by_token), AX_X, ALU.add))
                    link(nc.vector.tensor_tensor(per_tok[:, 10:12, :], per_tok[:, 8:10, :], per_tok[:, 6:8, :], ALU.mult))
                    nc.vector.tensor_copy(from_slot[:, :, :], per_tok[:, 10:12, :]).then_inc(from_slot_done, 1)
                    dve.wait_ge(from_slot_done, 1)
                elif stage == 7:
                    link(nc.vector.tensor_scalar(per_tok[:, 8:10, :], per_tok[:, 8:10, :], float(NO_SLOT), None, ALU.subtract))
                    link(nc.vector.tensor_tensor(per_tok[:, 8:10, :], per_tok[:, 8:10, :], per_tok[:, 6:8, :], ALU.mult))
                    link(nc.vector.tensor_scalar(per_tok[:, 8:10, :], per_tok[:, 8:10, :], float(NO_SLOT), None, ALU.add))
                    nc.vector.tensor_copy(to_slot[:, :, :], per_tok[:, 8:10, :]).then_inc(to_slot_done, 1)
                elif stage == 8:
                    link(nc.vector.tensor_tensor(per_tok[:, 0, :], per_tok[:, 3, :], per_tok[:, 4, :], ALU.add))
                    link(nc.vector.reciprocal(per_tok[:, 1, :], per_tok[:, 0, :]))
                    link(nc.vector.tensor_scalar(out_gate[:, :], tanhs[:, 1:2], OUT_SCALE, None, ALU.mult))
                    for k in range(2):
                        link(nc.vector.tensor_tensor(per_tok[:, 3 + k, :], per_tok[:, 3 + k, :], per_tok[:, 1, :], ALU.mult))
                    link(nc.vector.scalar_tensor_tensor(out=per_tok[:, 3:5, :], in0=per_tok[:, 3:5, :], scalar=out_gate[:, 0:1],
                                                        in1=per_tok[:, 6:8, :], op0=ALU.mult, op1=ALU.mult))

            def add_routed(n):
                w = ORDER[n // WG] * WG + n % WG
                for k in range(2):
                    dve.wait_ge(gathered[ORDER[n // WG]], 16 * 2 * WG)
                    if k:
                        dve.wait_ge(routed_added, 2 * n + 1)
                    nc.vector.scalar_tensor_tensor(out=X[:, w, :], in0=gathered_rows[:, w, k, :],
                                                   scalar=per_tok[:, 3 + k, w:w + 1], in1=X[:, w, :],
                                                   op0=ALU.mult, op1=ALU.add).then_inc(routed_added, 1)

            def add_shared(g):
                for h in range(2):
                    w = g * WG + 2 * h
                    nc.vector.scalar_tensor_tensor(out=X[:, w:w + 2, :], in0=bank[4 + h][:, :].rearrange(
                        "p (w h) -> p w h", w=2), scalar=out_gate[:, 0:1], in1=X[:, w:w + 2, :],
                        op0=ALU.mult, op1=ALU.add).then_inc(shared_added, 1)

            for q in range(NCH + 1):
                if q < NCH:
                    n, kind, i, c = CHUNKS[q]
                    cols = GT if kind == "shared" else CAP
                    dve.wait_ge(silu_done, q + 1)
                    if q >= 2:
                        dve.wait_ge(act_lo_done, q - 1)
                    nc.vector.scalar_tensor_tensor(out=act32[q % 2][:, 0:cols], in0=bank[2 + q % 2][:, 0:cols],
                                                   scalar=A_SCALE / (Y_SCALE * W_SCALE), in1=gated[q % 2][:, 0:cols],
                                                   op0=ALU.mult, op1=ALU.mult).then_inc(gated_done, 1)
                if q >= 1:
                    r = q - 1
                    cols = GT if CHUNKS[r][1] == "shared" else CAP
                    dve.wait_ge(act_hi_done, q)
                    dve.wait_ge(gated_done, q)
                    nc.vector.tensor_tensor(act16[:, r % 4, 1, 0:cols], act32[r % 2][:, 0:cols],
                                            act16[:, r % 4, 0, 0:cols], ALU.subtract).then_inc(act_lo_done, 1)
                if q == LATE_TURN:
                    for n in range(2, NG):
                        move_yT(n)
                for stage in router_stages.get(q, ()):
                    route(stage)
                for e, j in split_at.get(q, ()):
                    u, k = divmod(j, KC)
                    m = 3 * e + u
                    dve.wait_ge(ex_hi_done, e * PIECES + j + 1)
                    nc.vector.scalar_tensor_tensor(out=ex_gu[e % 2][:, 1, j * PIECE:(j + 1) * PIECE],
                                                   in0=ex_raw[m % 2][:, k * PIECE:(k + 1) * PIECE], scalar=W_SCALE,
                                                   in1=ex_gu[e % 2][:, 0, j * PIECE:(j + 1) * PIECE],
                                                   op0=ALU.mult, op1=ALU.subtract).then_inc(ex_lo_done, 1)
                if q in turn_at:
                    e = turn_at[q]
                    dve.wait_ge(exT_ready, 2 * e + 2)
                    nc.vector.tensor_copy(exT[:, e % 2, KC:2 * KC, :], bank[7][:, :].bitcast(F16)[:, 0:KC * CAP].rearrange(
                        "p (k n) -> p k n", k=KC)).then_inc(exT_moved_dve, 1)
                job = next((n for n in range(len(JOBS)) if FIRST_CHUNK[n + 1] + LAG - 1 == q), None)
                if job is not None and JOBS[job][0] == "shared":
                    dve.wait_ge(down_done, FIRST_CHUNK[job + 1])
                    add_shared(JOBS[job][1])
                if q >= FIRST_CHUNK[-2] and q < NCH:
                    add_routed(q - FIRST_CHUNK[-2])
            dve.wait_ge(down_done, NCH)
            dve.wait_ge(routed_added, 2 * W)
            add_shared(JOBS[-1][1])

        @block.tensor
        def _(pe):
            def warm_up(products, to):
                for _ in range(products):
                    pe.matmul(to[:, 0:P], ident[:, :], ident[:, :], start=True, stop=True)

            pe.wait_ge(consts, 13)
            pe.wait_ge(ctx_loaded, 16)
            for n in range(KC * B):
                b, k = divmod(n, KC)
                if n >= 4:
                    pe.wait_ge(ctxT_moved, n - 3)
                for c in range(NI):
                    last = pe.transpose(bank[n % 4][:, c * P:(c + 1) * P],
                                        ctx_rows[:, b * NI + c, k * P:(k + 1) * P], ident[:, :])
                last.then_inc(ctxT_ready, 1)
            for n in range(KC * W // 4):
                q, k = divmod(n, KC)
                pe.wait_ge(ln1_done, 4 * q + 4)
                if n >= 4:
                    pe.wait_ge(lnT_moved_act, 2 * (n - 3))
                    pe.wait_ge(lnT_moved_dve, 2 * (n - 3))
                for c in range(4):
                    last = pe.transpose(bank[4 + n % 4][:, c * P:(c + 1) * P],
                                        ln1[:, 4 * q + c, k * P:(k + 1) * P], ident[:, :])
                last.then_inc(lnT_ready, 1)
            pe.wait_ge(sq_done, KC * B)
            pe.wait_ge(ctxT_moved, KC * B)
            for k in range(KC):
                for b in range(B):
                    last = pe.matmul(bank[0][NJ * b:NJ * (b + 1), :], ones[:, :], ctx_sq[:, k, b * SEQ:(b + 1) * SEQ],
                                     start=(k == 0), stop=(k == KC - 1))
            last.then_inc(norm_ready, 1)
            pe.wait_ge(lnT_moved_act, 2 * KC * W // 4)
            pe.wait_ge(lnT_moved_dve, 2 * KC * W // 4)

            warm_up(WARM_UP_D, bank[1])

            def lane_norms():
                pe.wait_ge(spread_done, 2)
                pe.wait_ge(ln_norm_turned, 1)
                for f in range(2):
                    o = bank[4][:, W * f:W * (f + 1)]
                    pe.matmul(o, spread[:, 0, f, :], ln_norm[:, 0, :], start=True, stop=False)
                    last = pe.matmul(o, spread[:, 1, f, :], ln_norm[:, 1, :], start=False, stop=True)
                last.then_inc(lane_norm_ready, 1)

            for n, (m, q) in enumerate(PARTS):
                V, R = PER_BANK[m], ROWS[m]
                if n == 1:
                    lane_norms()
                if n >= 3:
                    pe.wait_ge(picked_done, 2 * (n - 2))
                for v in range(V):
                    for k in range(KC):
                        rows = ctxT[:, k, :].rearrange("p (b d i) -> p b d i", b=B, d=2)
                        for b in range(B):
                            last = pe.matmul(bank[1 + n % 3][NJ * b:NJ * (b + 1), 2 * R * v:2 * R * (v + 1)],
                                             lnT[:, k, V * q + v, b, :], rows[:, b, :, ROW_0[m]:ROW_0[m] + R],
                                             start=(k == 0), stop=(k == KC - 1))
                last.then_inc(prod_ready, 1)
            pe.wait_ge(offers_done, 1)
            pe.matmul(bank[0][:, 0:3 * NP], same_batch[:, :], offers[:, 0:3, :].rearrange("p n j -> p (n j)"),
                      start=True, stop=True).then_inc(offers_ready, 1)
            def turn_path(g):
                for n in (2 * g, 2 * g + 1):
                    q, c = group_of_bank(n)
                    pe.wait_ge(on_path_done, min(2 * WQ * (g + 1) + WQ, 2 * BW))
                    if n >= 4:
                        pe.wait_ge(pathT_moved, 2 * (n - 3))
                    for v in range(WQ):
                        o = bank[n % 4][:, v * P:(v + 1) * P]
                        rows = slice(c * P, (c + 1) * P)
                        pe.matmul(o, entered[:, WQ * q + v, rows], ident16[:, :], start=True, stop=False)
                        last = pe.matmul(o, left[:, WQ * q + v, rows], minus_ident16[:, :], start=False, stop=True)
                    last.then_inc(pathT_ready, 1)

            def align(m):
                n = PAIRS[m]
                pe.wait_ge(pathT_moved, 4 * GROUPS_FOR[m])
                if m >= 4:
                    pe.wait_ge(x2_done, m - 3)
                for c in range(2):
                    for z in range(2):
                        for i in range(NI):
                            for b in range(B):
                                last = pe.matmul(bank[4 + m % 4][NJ * b:NJ * (b + 1), c * H:(c + 1) * H],
                                                 pathT[:, i, 2 * n + c, b, :], ctx16[:, z, b * NI + i, :],
                                                 start=(z == 0 and i == 0), stop=(z == 1 and i == NI - 1))
                last.then_inc(aligned_ready, 1)

            for g in range(NW):
                turn_path(g)
                if NW - 5 <= g < NW - 2:
                    warm_up(WARM_UP // 3, bank[7])
            pe.wait_ge(ctx_lo_done, B)
            pe.wait_ge(ctx_hi_done, B)
            for m in range(W // 2):
                align(m)

            def turn_y(n):
                pe.wait_ge(y_hi_done, n + 1)
                if n < 2:
                    pe.wait_ge(y_lo_pool, n + 1)
                else:
                    pe.wait_ge(y_lo_done, n - 1)
                pe.wait_ge(x2_done, W // 2)
                for z in range(2):
                    if n:
                        pe.wait_ge((yT_moved_act, yT_moved_dve)[z], n)
                    for k in range(KC):
                        for c in range(WG):
                            last = pe.transpose(bank[6 + z][:, :].bitcast(F16)[:, (k * WG + c) * P:(k * WG + c + 1) * P],
                                                y16[:, ORDER[n] * WG + c, z, k * P:(k + 1) * P], ident16[:, :])
                    last.then_inc(yT_ready, 1)

            pairs = ((0, 0), (0, 1), (1, 0))
            for n in range(2):
                turn_y(n)

            def logits():
                pe.wait_ge(yT_moved_act, NG)
                pe.wait_ge(yT_moved_dve, NG)
                pe.wait_ge(rw_lo_done, 1)
                for w in range(W):
                    g, c = divmod(w, WG)
                    for n, (k, (zy, zw)) in enumerate((k, p) for k in range(KC) for p in pairs):
                        last = pe.matmul(bank[7][:, w * E:(w + 1) * E], yT[:, g, zy, k, c * P:(c + 1) * P], rw16[:, zw, k, :],
                                         start=(n == 0), stop=(n == 3 * KC - 1))
                last.then_inc(logits_ready, 1)

            def gate_and_up(q):
                n, kind, i, c = CHUNKS[q]
                cols = GT if kind == "shared" else CAP
                for m in range(2):
                    for k in range(KC):
                        for zw, zy in pairs:
                            if kind == "shared":
                                weights = gu16[:, m, zw, k, c * P:(c + 1) * P]
                                moving = yT[:, i, zy, k, :]
                            else:
                                o = (m * KC + k) * IR + c * P
                                weights = ex_gu[i % 2][:, zw, o:o + P]
                                moving = exT[:, i % 2, zy * KC + k, :]
                            first = k == 0 and (zw, zy) == pairs[0]
                            final = k == KC - 1 and (zw, zy) == pairs[-1]
                            last = pe.matmul(bank[2 * m + q % 2][:, 0:cols], weights, moving, start=first, stop=final)
                last.then_inc(gu_ready, 1)

            def down(q):
                n, kind, i, c = CHUNKS[q]
                tiles = [(m * P, P) for m in range(WG)] if kind == "shared" else TILES_E
                for t, (m, rows) in enumerate(tiles):
                    for za, zw in pairs:
                        weights = down16[:, zw, c, :] if kind == "shared" else \
                            ex_gu[i % 2][:, zw, 2 * KC * IR + c * H:2 * KC * IR + (c + 1) * H]
                        first = c == 0 and t % 2 == 0 and (za, zw) == pairs[0]
                        final = q + 1 == FIRST_CHUNK[n + 1] and (za, zw) == pairs[-1]
                        if rows == P:
                            last = pe.matmul(bank[4 + t // 2][:, (t % 2) * H:(t % 2 + 1) * H],
                                             act16[:, q % 4, za, m:m + rows], weights,
                                             start=first, stop=final, skip_group_check=True)
                            continue
                        for h in range(2):
                            last = pe.matmul(bank[4 + t // 2][h * rows:(h + 1) * rows, 0:P],
                                             act16[:, q % 4, za, m:m + rows], weights[:, h * P:(h + 1) * P],
                                             start=first, stop=final, skip_group_check=True)
                last.then_inc(down_done, 1)

            for q in range(NCH + LAG):
                if q < NCH:
                    n, kind, i, c = CHUNKS[q]
                    if kind == "shared" and q == 0:
                        pe.wait_ge(raw_lo_done, 8)
                        pe.wait_ge(yT_moved_act, 2)
                        pe.wait_ge(yT_moved_dve, 2)
                    if kind == "expert" and c == 0:
                        pe.wait_ge(ex_lo_done, i * PIECES + 2 * PIECES // 3)
                        pe.wait_ge(exT_moved_act, i + 1)
                        pe.wait_ge(exT_moved_dve, i + 1)
                    if q >= 2:
                        pe.wait_ge(silu_done, q - 1)
                        pe.wait_ge(gated_done, q - 1)
                    gate_and_up(q)
                if q >= LAG:
                    r = q - LAG
                    n, kind, i, c = CHUNKS[r]
                    if kind == "expert" and c == 0:
                        pe.wait_ge(ex_lo_done, (i + 1) * PIECES)
                    if c == 0 and n:
                        if JOBS[n - 1][0] == "shared":
                            pe.wait_ge(shared_added, 2 * sum(k == "shared" for k, _ in JOBS[:n]))
                        else:
                            pe.wait_ge(ex_out_moved, 2 * (JOBS[n - 1][1] + 1))
                    if n == 0 and c % 4 == 0:
                        pe.wait_ge(raw_lo_done, 9 + c // 4)
                    pe.wait_ge(act_lo_done, r + 1)
                    down(r)
                if q == LATE_TURN:
                    for n in range(2, NG):
                        turn_y(n)
                elif q == LATE_TURN + 1:
                    logits()
                elif q == BASE_AT:
                    pe.wait_ge(totals_done, 1)
                    pe.matmul(bank[7][:, W * E:(W + 1) * E], earlier[:, :], lane_total[:, 0, :],
                              start=True, stop=True).then_inc(base_ready, 1)
                if q in turn_at:
                    e = turn_at[q]
                    pe.wait_ge(ex_in_loaded, 32 * (e + 1))
                    for z in range(2):
                        if e:
                            pe.wait_ge((exT_moved_act, exT_moved_dve)[z], e)
                        for k in range(KC):
                            for t, (m, rows) in enumerate(TILES_E):
                                o = k * CAP + m
                                last = pe.transpose(bank[6 + z][:, :].bitcast(F16)[:, o:o + rows],
                                                    ex_in[0:rows, t, z, k * P:(k + 1) * P], ident16[0:rows, 0:rows])
                        last.then_inc(exT_ready, 1)


_INS = ["x", "folded", "g_xattn", "g_ffn", "L0_ffn_router_w", "L0_ffn_rg", "L0_ffn_ru", "L0_ffn_rd",
        "L0_ffn_sg", "L0_ffn_su", "L0_ffn_sd"]
_OUTS = [((4, 512, 256), "float32")]


def kernel(**inputs):
    import numpy as _np
    import concourse.bacc as _bacc
    from concourse import mybir as _mybir
    from concourse.bass_utils import run_bass_kernel_spmd as _run

    nc = _bacc.Bacc("TRN2", target_bir_lowering=False, num_devices=1)
    ctx = inputs["ctx_1024"]
    half = ctx.shape[1] // 2
    inputs = dict(inputs, folded=_np.stack([ctx[:, :half], ctx[:, :half - 1:-1]], axis=1))
    arrays, args = {}, []
    for name in _INS:
        a = _np.ascontiguousarray(inputs[name])
        arrays[f"in_{name}_dram"] = a
        args.append(nc.dram_tensor(f"in_{name}_dram", a.shape, _mybir.dt.from_np(a.dtype), kind="ExternalInput").ap())
    for i, (shape, dtype) in enumerate(_OUTS):
        dt = _mybir.dt.from_np(_np.dtype(dtype))
        args.append(nc.dram_tensor(f"out_{i}_dram", shape, dt, kind="ExternalOutput").ap())
    flamingo_dtw_moe(nc, *args)
    r = _run(nc, [arrays], core_ids=[0])
    return r.results[0]["out_0_dram"]
```
